# Optimizing a Trainium2 kernel written in Bass

```python
import numpy as np
import jax
import jax.numpy as jnp

def _softmax(x, axis=-1):
    return jax.nn.softmax(x, axis=axis)

def _gelu(x):
    return jax.nn.gelu(x, approximate=True)

def _silu(x):
    return jax.nn.silu(x)

def _sigmoid(x):
    return jax.nn.sigmoid(x)

def _layernorm(x, axis=-1, eps=1e-05):
    m = jnp.mean(x, axis=axis, keepdims=True)
    v = jnp.var(x, axis=axis, keepdims=True)
    return (x - m) / jnp.sqrt(v + eps)

def _scatter_add(tgt, idx, src, axis=0):
    return tgt.at[idx].add(src)

def _segment_sum(src, seg, n):
    return jax.ops.segment_sum(src, seg, n)
kernel_name = 'mk_gps_d1_gnn_r8_88e38e'

def setup_inputs(seed: int=0):
    np.random.seed(seed)
    _w = jnp.asarray

    def _rec_inputs():
        import jax
        import jax.numpy as jnp
        _gk = jax.random.key(seed)
        x = -0.0003713 + 1 * jax.random.normal(jax.random.fold_in(_gk, 1), (6250, 256), jnp.float32)
        src = jax.random.randint(jax.random.fold_in(_gk, 2), (200000,), 0, 6250, jnp.int32)
        dst = jnp.minimum((6250 * jax.random.uniform(jax.random.fold_in(_gk, 3), (200000,)) ** 2.0).astype(jnp.int32), 49999)
        _o = jnp.argsort(dst, stable=True)
        src = src[_o]
        dst = dst[_o]
        return (x, src, dst)
    x, src, dst = _rec_inputs()

    def _L0_gnn_setup():
        import jax, jax.numpy as jnp
        import numpy as np
        N_NODES = 6250
        N_EDGES = 100000
        D = 256
        key = jax.random.key(seed)
        k_x, k_e, k_w1, k_w2 = jax.random.split(key, 4)
        x = jax.random.normal(k_x, (N_NODES, D), dtype=jnp.float32)
        edge_index = jax.random.randint(k_e, (2, N_EDGES), 0, N_NODES, dtype=jnp.int64)
        W1 = jax.random.normal(k_w1, (D, D // 2), dtype=jnp.float32) * (1.0 / np.sqrt(D))
        b1 = jnp.zeros((D // 2,), dtype=jnp.float32)
        W2 = jax.random.normal(k_w2, (D // 2, 1), dtype=jnp.float32) * (1.0 / np.sqrt(D // 2))
        b2 = jnp.zeros((1,), dtype=jnp.float32)
        return {'x': x, 'edge_index': edge_index, 'W1': W1, 'b1': b1, 'W2': W2, 'b2': b2}
    _L0_gnn_all = _L0_gnn_setup()
    _L0_gnn_in = {k: v for k, v in _L0_gnn_all.items() if k in ('W1', 'b1', 'W2', 'b2')}
    del _L0_gnn_all

    def _L0_mix_setup():
        import jax, jax.numpy as jnp
        import numpy as np
        HEADS = 8
        EPS = 1e-05

        def _ln(t, w, b, headc):
            m = jnp.mean(t, axis=-1, keepdims=True)
            d = t - m
            std = jnp.sqrt(jnp.sum(d * d, axis=-1, keepdims=True) / (headc - 1))
            return w * (d / (std + EPS)) + b
        key = jax.random.key(seed)
        B, N, C = (32, 512, 256)
        headc = C // HEADS
        x = jax.random.normal(key, (B, N, C), dtype=jnp.float32)
        return {'x': x, 'kln_weight': jnp.ones((HEADS, 1, headc), dtype=jnp.float32), 'kln_bias': jnp.zeros((HEADS, 1, headc), dtype=jnp.float32), 'vln_weight': jnp.ones((HEADS, 1, headc), dtype=jnp.float32), 'vln_bias': jnp.zeros((HEADS, 1, headc), dtype=jnp.float32)}
    _L0_mix_all = _L0_mix_setup()
    _L0_mix_in = {k: v for k, v in _L0_mix_all.items() if k in ('kln_weight', 'kln_bias', 'vln_weight', 'vln_bias')}
    del _L0_mix_all

    def _L0_ffn_setup():
        import jax, jax.numpy as jnp
        import numpy as np
        E, D, H, TOP_K = (6, 256, 256, 2)
        ROUTER_H = D // 2
        key = jax.random.key(seed)
        ks = jax.random.split(key, 12)
        s = 1.0 / np.sqrt(D)
        sh = 1.0 / np.sqrt(H)
        sr = 1.0 / np.sqrt(ROUTER_H)
        return {'features': jax.random.normal(ks[0], (8, 512, D), dtype=jnp.float32), 'router_w1': jax.random.uniform(ks[1], (D, ROUTER_H), jnp.float32, -s, s), 'router_b1': jnp.zeros((ROUTER_H,), jnp.float32), 'router_w2': jax.random.uniform(ks[2], (ROUTER_H, E), jnp.float32, -sr, sr), 'router_b2': jnp.zeros((E,), jnp.float32), 'expert_w1': jax.random.uniform(ks[3], (E, D, H), jnp.float32, -s, s), 'expert_b1': jnp.zeros((E, H), jnp.float32), 'expert_w2': jax.random.uniform(ks[4], (E, H, H), jnp.float32, -sh, sh), 'expert_b2': jnp.zeros((E, H), jnp.float32), 'expert_w3': jax.random.uniform(ks[5], (E, H, D), jnp.float32, -sh, sh), 'expert_b3': jnp.zeros((E, D), jnp.float32)}
    _L0_ffn_all = _L0_ffn_setup()
    _L0_ffn_in = {k: v for k, v in _L0_ffn_all.items() if k in ('router_w1', 'router_b1', 'router_w2', 'router_b2', 'expert_w1', 'expert_b1', 'expert_w2', 'expert_b2', 'expert_w3', 'expert_b3')}
    del _L0_ffn_all
    return {'x': x, 'src': src, 'dst': dst, 'L0_gnn_W1': _L0_gnn_in['W1'], 'L0_gnn_b1': _L0_gnn_in['b1'], 'L0_gnn_W2': _L0_gnn_in['W2'], 'L0_gnn_b2': _L0_gnn_in['b2'], 'L0_mix_kln_weight': _L0_mix_in['kln_weight'], 'L0_mix_kln_bias': _L0_mix_in['kln_bias'], 'L0_mix_vln_weight': _L0_mix_in['vln_weight'], 'L0_mix_vln_bias': _L0_mix_in['vln_bias'], 'L0_ffn_router_w1': _L0_ffn_in['router_w1'], 'L0_ffn_router_b1': _L0_ffn_in['router_b1'], 'L0_ffn_router_w2': _L0_ffn_in['router_w2'], 'L0_ffn_router_b2': _L0_ffn_in['router_b2'], 'L0_ffn_expert_w1': _L0_ffn_in['expert_w1'], 'L0_ffn_expert_b1': _L0_ffn_in['expert_b1'], 'L0_ffn_expert_w2': _L0_ffn_in['expert_w2'], 'L0_ffn_expert_b2': _L0_ffn_in['expert_b2'], 'L0_ffn_expert_w3': _L0_ffn_in['expert_w3'], 'L0_ffn_expert_b3': _L0_ffn_in['expert_b3']}

def reference(x, src, dst, L0_gnn_W1, L0_gnn_b1, L0_gnn_W2, L0_gnn_b2, L0_mix_kln_weight, L0_mix_kln_bias, L0_mix_vln_weight, L0_mix_vln_bias, L0_ffn_router_w1, L0_ffn_router_b1, L0_ffn_router_w2, L0_ffn_router_b2, L0_ffn_expert_w1, L0_ffn_expert_b1, L0_ffn_expert_w2, L0_ffn_expert_b2, L0_ffn_expert_w3, L0_ffn_expert_b3):
    import jax
    import jax.numpy as jnp

    def _L0_gnn_ref(x, edge_index, W1, b1, W2, b2):
        import jax, jax.numpy as jnp
        import numpy as np
        N_NODES = 6250
        N_EDGES = 100000
        D = 256
        row, col = (edge_index[0], edge_index[1])
        neigh = x[col]
        h = jax.nn.relu(neigh @ W1 + b1)
        w = jax.nn.sigmoid(h @ W2 + b2)
        num = jax.ops.segment_sum(neigh * w, row, num_segments=N_NODES)
        den = jax.ops.segment_sum(w, row, num_segments=N_NODES)
        out = jnp.where(den > 0, num / jnp.maximum(den, 1e-12), 0.0)
        return out

    def _L0_mix_ref(x, kln_weight, kln_bias, vln_weight, vln_bias):
        import jax, jax.numpy as jnp
        import numpy as np
        HEADS = 8
        EPS = 1e-05

        def _ln(t, w, b, headc):
            m = jnp.mean(t, axis=-1, keepdims=True)
            d = t - m
            std = jnp.sqrt(jnp.sum(d * d, axis=-1, keepdims=True) / (headc - 1))
            return w * (d / (std + EPS)) + b
        B, N, C = x.shape
        headc = C // HEADS
        qkv = x.reshape(B, N, HEADS, headc).transpose(0, 2, 1, 3)
        k = _ln(qkv, kln_weight, kln_bias, headc)
        v = _ln(qkv, vln_weight, vln_bias, headc)
        kv = jnp.einsum('bhnd,bhne->bhde', k, v) / N
        out = jnp.einsum('bhnd,bhde->bhne', qkv, kv)
        out = out.transpose(0, 2, 1, 3).reshape(B, N, C)
        return out + x

    def _L0_ffn_ref(features, router_w1, router_b1, router_w2, router_b2, expert_w1, expert_b1, expert_w2, expert_b2, expert_w3, expert_b3):
        import jax, jax.numpy as jnp
        import numpy as np
        E, D, H, TOP_K = (6, 256, 256, 2)
        ROUTER_H = D // 2
        rh = jax.nn.relu(features @ router_w1 + router_b1)
        expert_logits = jax.nn.softmax(rh @ router_w2 + router_b2, axis=-1)
        top_w, top_i = jax.lax.top_k(expert_logits, TOP_K)
        routing_weights = jax.nn.softmax(top_w, axis=-1)
        h1 = jax.nn.relu(jnp.einsum('bsd,edh->bseh', features, expert_w1) + expert_b1)
        h2 = jax.nn.relu(jnp.einsum('bseh,ehf->bsef', h1, expert_w2) + expert_b2)
        expert_out = jnp.einsum('bsef,efo->bseo', h2, expert_w3) + expert_b3
        sel = jnp.take_along_axis(expert_out, top_i[:, :, :, None], axis=2)
        combined = jnp.sum(sel * routing_weights[..., None], axis=2)
        return combined
    edge_index = jnp.stack([src, dst])
    xn = _layernorm(x, axis=-1)
    x = x + _L0_gnn_ref(xn, edge_index, L0_gnn_W1, L0_gnn_b1, L0_gnn_W2, L0_gnn_b2) + _L0_mix_ref(xn[None], L0_mix_kln_weight, L0_mix_kln_bias, L0_mix_vln_weight, L0_mix_vln_bias)[0]
    x = x + _L0_ffn_ref(_layernorm(x, axis=-1)[None], L0_ffn_router_w1, L0_ffn_router_b1, L0_ffn_router_w2, L0_ffn_router_b2, L0_ffn_expert_w1, L0_ffn_expert_b1, L0_ffn_expert_w2, L0_ffn_expert_b2, L0_ffn_expert_w3, L0_ffn_expert_b3)[0]
    return x

_drawn_inputs = setup_inputs


def setup_inputs(seed=0):
    import zlib

    import numpy as np

    out = dict(_drawn_inputs(seed))
    spreads = {'L0_gnn_b1': (0.0, 2.0),
     'L0_mix_kln_weight': (1.0, 0.2),
     'L0_mix_kln_bias': (0.0, 0.459),
     'L0_mix_vln_weight': (1.0, 0.2),
     'L0_mix_vln_bias': (0.0, 0.457),
     'L0_ffn_router_b1': (0.0, 0.626),
     'L0_ffn_router_b2': (0.0, 0.412),
     'L0_ffn_expert_b1': (0.0, 0.8),
     'L0_ffn_expert_b2': (0.0, 0.8),
     'L0_ffn_expert_b3': (0.0, 0.33)}
    factors = {'L0_gnn_W1': 3.075,
     'L0_gnn_W2': 3.003,
     'L0_ffn_expert_w1': 3.374,
     'L0_ffn_expert_w2': 2.885}
    for name, (base, spread) in spreads.items():
        noise = np.random.default_rng([zlib.crc32(name.encode()), seed]).standard_normal(out[name].shape)
        drawn = base * np.exp(spread * noise) if base else spread * noise
        out[name] = jnp.asarray(drawn.astype(out[name].dtype))
    for name, factor in factors.items():
        out[name] = (out[name] * factor).astype(out[name].dtype)
    return out
```

```python
from contextlib import ExitStack

import numpy as np
import concourse.bass as bass
from concourse import mybir

ALU = mybir.AluOpType
ACT = mybir.ActivationFunctionType
AX = mybir.AxisListType
F32 = mybir.dt.float32
I32 = mybir.dt.int32
U32 = mybir.dt.uint32

P = 128
NODES, DIM = 6250, 256
EDGES = 200000
HID = 128
HEADS = 8
HEAD_DIM = DIM // HEADS
EXPERTS = 6
HALVES = DIM // P
LN_EPS = 1e-5
HEAD_EPS = 1e-5

BLOCKS = -(-NODES // P)
LAST_ROWS = NODES - (BLOCKS - 1) * P
ROW = DIM + 1

LEVELS = 18
COLS = 2**LEVELS // P
HALF = COLS // 2
TURNED = 7
LOAD_ROWS = 125
LOAD_COLS = EDGES // LOAD_ROWS
DST_BITS = 13
DST_MASK = 2**DST_BITS - 1
BLOCK_SHIFT = DST_BITS + 7
KEY_BASE = 0x38000000
PAD_KEY = float(np.array([KEY_BASE | (BLOCKS * P) << DST_BITS], np.int32).view(np.float32)[0])

CHUNKS = -(-EDGES // P)
GROUP = 11
GROUPS_PER_BLOCK = 3
STEPS_PER_BLOCK = GROUP * GROUPS_PER_BLOCK
STEPS = STEPS_PER_BLOCK * BLOCKS
assert STEPS >= CHUNKS + BLOCKS - 1
STEP_TILES = -(-STEPS // P)
EDGE_COLS = STEP_TILES * P
SUM_BANKS = 3
BANK = 512
PICKS = 3


def splits(level):
    return level not in (TURNED, LEVELS - 1, LEVELS)


def exchanges_before(level, bit):
    return level * (level - 1) // 2 + level - 1 - bit


def instructions_before(level, bit):
    whole = sum(2 * k + 2 * splits(k) for k in range(1, level))
    return whole + 2 * (level - 1 - bit) + (2 if splits(level) and bit < level - 1 else 0)


def turns_before(level, bit):
    if level <= TURNED:
        return 0
    return 2 * (level - TURNED - 1) + (2 if bit < TURNED else 1)


def is_after_turn(level, bit):
    return level > TURNED and bit in (level - 1, TURNED - 1)


def distance(bit):
    return 2**bit if bit < TURNED else 2 ** (bit - TURNED)


SORT_END = instructions_before(LEVELS + 1, LEVELS)
TURNS_END = 2 * (LEVELS - TURNED)


def gps_layer(nc, a, out, y_table):
    with ExitStack() as ctx:
        def sb(name, shape, dt=F32):
            return ctx.enter_context(nc.sbuf_tensor(name, shape, dt))

        def sem(name):
            return ctx.enter_context(nc.semaphore(name))

        base = sb("base", [P, BLOCKS, DIM])
        acc_mem = sb("acc_mem", [P, (BLOCKS + 1) * ROW])
        feat_mem = sb("feat_mem", [P, HALVES * BLOCKS * P])
        sort_mem = sb("sort_mem", [P, STEPS_PER_BLOCK * P])
        gath_mem = sb("gath_mem", [P, 2 * EDGE_COLS])
        tab_mem = sb("tab_mem", [P, 3 * STEPS])

        keys = [sort_mem[:, 0:COLS], sort_mem[:, COLS:2 * COLS]]
        src_in = gath_mem[:, 0:LOAD_COLS].bitcast(I32)
        dst_in = gath_mem[:, LOAD_COLS:2 * LOAD_COLS].bitcast(I32)
        dst_of_edge = gath_mem[:, 0:EDGE_COLS]
        src_of_edge = gath_mem[:, EDGE_COLS:2 * EDGE_COLS]
        chunk_of_step = keys[0][:, 0:STEPS]
        pick = keys[0][:, STEPS:STEPS + PICKS * P].rearrange("p (s n) -> p s n", s=PICKS)
        past_block = keys[1][0:BLOCKS, 0:STEPS]
        step_dst = tab_mem[:, 0:STEPS].bitcast(U32)
        step_rel = tab_mem[:, STEPS:2 * STEPS]
        step_no = tab_mem[:, 2 * STEPS:3 * STEPS]
        step_acc = tab_mem[0:1, 2 * STEPS:3 * STEPS].bitcast(I32)
        gathered = gath_mem[:, 0:GROUP * ROW].rearrange("p (s n) -> p s n", s=GROUP)
        onehot = sort_mem[:, :].rearrange("p (s n) -> p s n", s=STEPS_PER_BLOCK)
        used = [0]

        def early(n):
            at = used[0]
            used[0] += n
            assert used[0] <= (BLOCKS + 1) * ROW
            return acc_mem[:, at:at + n]

        def slots(t, n=2):
            return t.rearrange("p (s n) -> p s n", s=n)

        xnT = feat_mem[:, :].rearrange("p (h n) -> p h n", h=HALVES)
        x_stats = early(6 * BLOCKS).rearrange("p (b n) -> p b n", n=6)
        x_mean_var = early(2 * BLOCKS).rearrange("p (b n) -> p b n", n=2)
        x_rstd, x_bias, gate, y_scale, y_bias = (early(BLOCKS) for _ in range(5))
        xs, dev, dev2, zed = (slots(early(2 * DIM)) for _ in range(4))
        xsT = early(2 * DIM).rearrange("p (h n) -> p h n", h=HALVES)
        mixT = early(DIM).rearrange("p (h n) -> p h n", h=HALVES)
        hid = early(2 * P)
        y_out = slots(early(2 * ROW))
        dev_sum, dev_r, dev_std = (early(2 * HEADS) for _ in range(3))
        k_col_w, k_col_b, z_sum, kw_sum = (early(HALVES) for _ in range(4))
        v_row_w, v_row_b, z_row, kv_a, kv_b = (early(DIM).rearrange("p (h n) -> p h n", h=HALVES) for _ in range(5))
        diag_sum = early(DIM).rearrange("p (h n) -> p h n", h=HALVES)
        late = [0]

        def after(n):
            at = late[0]
            late[0] += n
            assert late[0] <= HALVES * BLOCKS * P
            return feat_mem[:, at:at + n]

        w1, w2, w3 = (after(EXPERTS * HALVES * DIM).rearrange("p (e h n) -> p e h n", e=EXPERTS, h=HALVES) for _ in range(3))
        x2, xn2, y_acc = after(DIM), after(DIM), after(DIM)
        next_T, this_T = (after(DIM).rearrange("p (h n) -> p h n", h=HALVES) for _ in range(2))
        router_hid = after(P)
        gates_T = after(P)[0:EXPERTS, :]
        h1_T, h2_T = (after(2 * DIM).rearrange("p (s h n) -> p s h n", s=2, h=HALVES) for _ in range(2))
        ident, lane, centre, ones, same_head = (sb(n, [P, P]) for n in ("ident", "lane", "centre", "ones", "same_head"))
        kv = sb("kv", [P, HALVES, P])
        gnn_w1, router_w1 = sb("gnn_w1", [P, HALVES, HID]), sb("router_w1", [P, HALVES, HID])
        gnn_w2, gnn_b1, gnn_b2, router_b1 = (sb(n, [P, 1]) for n in ("gnn_w2", "gnn_b1", "gnn_b2", "router_b1"))
        router_w2, router_b2 = sb("router_w2", [P, EXPERTS]), sb("router_b2", [1, EXPERTS])
        b1, b2 = sb("b1", [P, EXPERTS, HALVES]), sb("b2", [P, EXPERTS, HALVES])
        b3 = sb("b3", [EXPERTS, DIM])
        row_no, row_odd = sb("row_no", [P, 1], I32), sb("row_odd", [P, 1], I32)
        sign = sb("sign", [P, 2])
        bound = sb("bound", [P, BLOCKS + 1], I32)
        below = sb("below", [P, 2, BLOCKS + 1])
        cut = acc_mem[:, used[0]:used[0] + (BLOCKS + 1) * (COLS // P)].rearrange("p (b c) -> p b c", b=BLOCKS + 1)
        used[0] += (BLOCKS + 1) * (COLS // P)
        assert used[0] <= (BLOCKS + 1) * ROW
        counts = sb("counts", [BLOCKS, 8])
        chunk_w, neg_block, acc_w = (sb(n, [BLOCKS, P]) for n in ("chunk_w", "neg_block", "acc_w"))
        upto = sb("upto", [BLOCKS, BLOCKS])
        edge_no = sb("edge_no", [P, STEP_TILES])
        last_block = sb("last_block", [BLOCKS, 1])
        step_idx = sb("step_idx", [P, STEPS_PER_BLOCK], U32)
        minus_half = sb("minus_half", [P, BLOCKS])
        half_power, minus_one, over_count, head_eps = (sb(n, [P, 2 * HEADS]) for n in ("half_power", "minus_one", "over_count", "head_eps"))
        den, stats, mean_var = sb("den", [P, 2]), sb("stats", [P, 6]), sb("mean_var", [P, 2])
        rstd, logit_max, exp_l = sb("rstd", [P, 2]), sb("logit_max", [P, 1]), sb("exp_l", [P, EXPERTS])
        exp_sum, probs, top, top_i = sb("exp_sum", [P, 2]), sb("probs", [P, 8]), sb("top", [P, 8]), sb("top_i", [P, 8], U32)
        top_f, top_w = sb("top_f", [P, 2]), sb("top_w", [P, 4])
        gate_1, gate_2, gates = (sb(n, [P, EXPERTS]) for n in ("gate_1", "gate_2", "gates"))

        turned = ctx.enter_context(nc.psum_tensor("turned", [P, COLS], F32))
        front = ctx.enter_context(nc.psum_tensor("front", [P, COLS], F32))

        def bank(i):
            return front[:, i * BANK:(i + 1) * BANK]

        ps_xT = bank(0).rearrange("p (h n) -> p h n", h=HALVES)
        ps_dev = slots(bank(1))
        ps_hid = bank(2)[:, 0:2 * P]
        ps_z = bank(3)[:, 0:HALVES * (P + 1)].rearrange("p (h n) -> p h n", h=HALVES)
        ps_logit = bank(2)[:, 2 * P:2 * P + BLOCKS]
        ps_z_row = bank(0)[:, 0:DIM].rearrange("p (h n) -> p h n", h=HALVES)
        ps_mix = bank(1)[:, 0:DIM]
        ps_counts = bank(3)[0:BLOCKS, 0:4]
        ps_end = bank(3)[0:BLOCKS, 4:5]
        ps_sum = [turned[:, BANK * i:BANK * i + ROW] for i in range(SUM_BANKS)]
        ps_h1 = [bank(s)[:, 0:DIM].rearrange("p (h n) -> p h n", h=HALVES) for s in range(2)]
        ps_h2 = [bank(2 + s)[:, 0:DIM].rearrange("p (h n) -> p h n", h=HALVES) for s in range(2)]
        ps_y = [turned[:, BANK * s:BANK * s + DIM] for s in range(2)]
        prep_bank, route_bank = (turned[:, BANK * s:BANK * (s + 1)] for s in (2, 3))
        ps_x2T = prep_bank[:, 0:DIM].rearrange("p (h n) -> p h n", h=HALVES)
        ps_router = prep_bank[:, DIM:DIM + P]
        ps_b3 = route_bank[:, 0:DIM]
        ps_gates_T = route_bank[0:EXPERTS, DIM:DIM + P]
        ps_l = route_bank[:, DIM + P:DIM + P + EXPERTS]

        names = """x_loaded x_zeroed edges_loaded small_loaded ln_loaded consts weights_loaded
            key_step pool_step act_step x_stat x_stats_ready x_norm
            xs_ready xT_ps xT_ready xT_filed hid_ps hid_ready logit_ps dev_ps dev_ready zed_ready z_summed z_zeroed
            z_copied diag_ready z_row_ps z_row_ready kv_final gate_ready y_params y_ready
            mix_staged mix_ps mix_done
            fields_ready edges_ready below_ready counts_ps counts_ready ends_ps past_ready steps_ps chunk_ready
            acc_row_ready pick_ready pick_used picked_ps tables_ready acc_zeroed
            idx_staged slot_free onehot_ready sum_ps sum_added
            ffn_step ffn_pass x2_rstd x2_norm x2T_ps x2T_ready router_ps router_ready logits_ps logit_max_ready exp_ready
            top_diff_ready top_exp_ready gates_ready gatesT_ps gatesT_ready b3_ps this_ready
            h1_ps h1_ready h2_ps h2_ready ey_ps ey_added row_stored""".split()
        S = {name: sem(name) for name in names}
        sorted_half = [sem("sorted_half0"), sem("sorted_half1")]
        half_turned = [sem("half_turned0"), sem("half_turned1")]
        upper_copied = [sem("upper_copied0"), sem("upper_copied1")]
        y_stored = [sem("y_stored0"), sem("y_stored1")]
        rows_in = [sem(f"rows_in{i}") for i in range(GROUP)]

        N_CONSTS = 17
        SPREAD_LINKS = 1 + HEAD_DIM.bit_length() - 1 + 4
        N_SMALL = 13
        N_MIX_LOADS = 6
        FULL = BLOCKS - 1
        PAIRS = FULL // 2
        MIX_LEVEL = 11
        TILES_PER_LEVEL = BLOCKS // (LEVELS - MIX_LEVEL)
        assert TILES_PER_LEVEL * (LEVELS - MIX_LEVEL) == BLOCKS
        N_NORM, N_ROUTE = 6, 10
        FFN_LINKS = N_NORM + N_ROUTE + 1

        def half_view(t, half):
            return t[:, half * HALF:(half + 1) * HALF]

        block = ctx.enter_context(nc.Block())

        @block.sync
        def _(sp):
            sp.dma_start(src_in[0:LOAD_ROWS, :], a["src"].rearrange("(p c) -> p c", p=LOAD_ROWS)).then_inc(S["edges_loaded"], 16)
            sp.dma_start(dst_in[0:LOAD_ROWS, :], a["dst"].rearrange("(p c) -> p c", p=LOAD_ROWS)).then_inc(S["edges_loaded"], 16)
            sp.dma_start(base[:, 0:FULL, :], a["x"][0:FULL * P, :].rearrange("(b p) d -> p b d", p=P)).then_inc(S["x_loaded"], 16)
            sp.wait_ge(S["x_zeroed"], 1)
            sp.dma_start(base[0:LAST_ROWS, FULL, :], a["x"][FULL * P:NODES, :]).then_inc(S["x_loaded"], 16)
            sp.dma_start(gnn_w1[:, :, :], a["L0_gnn_W1"].rearrange("(h p) n -> p h n", p=P)).then_inc(S["small_loaded"], 16)
            sp.dma_start(gnn_b1[:, :], a["L0_gnn_b1"].rearrange("(p o) -> p o", o=1)).then_inc(S["small_loaded"], 16)
            sp.dma_start(gnn_w2[:, :], a["L0_gnn_W2"]).then_inc(S["small_loaded"], 16)
            sp.dma_start(gnn_b2[:, :], a["L0_gnn_b2"].partition_broadcast(P)).then_inc(S["small_loaded"], 16)
            sp.dma_start(router_w1[:, :, :], a["L0_ffn_router_w1"].rearrange("(h p) n -> p h n", p=P)).then_inc(S["small_loaded"], 16)
            sp.dma_start(router_b1[:, :], a["L0_ffn_router_b1"].rearrange("(p o) -> p o", o=1)).then_inc(S["small_loaded"], 16)
            sp.dma_start(router_w2[:, :], a["L0_ffn_router_w2"]).then_inc(S["small_loaded"], 16)
            sp.dma_start(router_b2[:, :], a["L0_ffn_router_b2"].rearrange("(o e) -> o e", o=1)).then_inc(S["small_loaded"], 16)
            sp.dma_start(b3[:, :], a["L0_ffn_expert_b3"]).then_inc(S["small_loaded"], 16)
            with nc.allow_non_contiguous_dma(reason="biases and head weights with the feature on the partition, once"):
                for bias, name in ((b1, "L0_ffn_expert_b1"), (b2, "L0_ffn_expert_b2")):
                    for h in range(HALVES):
                        sp.dma_start(bias[:, :, h], a[name][:, h * P:(h + 1) * P].rearrange("e p -> p e")).then_inc(S["small_loaded"], 16)
                for t, name in ((k_col_w, "kln_weight"), (k_col_b, "kln_bias")):
                    for h in range(HALVES):
                        rows = a["L0_mix_" + name].rearrange("g o c -> (g o c)")[h * P:(h + 1) * P]
                        sp.dma_start(t[:, h:h + 1], rows.rearrange("(p o) -> p o", o=1)).then_inc(S["ln_loaded"], 16)
            for t, name in ((v_row_w, "vln_weight"), (v_row_b, "vln_bias")):
                sp.dma_start(t.rearrange("p h n -> p (h n)"),
                             a["L0_mix_" + name].rearrange("g o c -> (g o c)").partition_broadcast(P)).then_inc(S["ln_loaded"], 16)

            with sp.Fori(0, PAIRS) as i:
                for s in range(2):
                    sp.wait_ge(S["y_ready"], 2 * i + s + 1)
                    sp.dma_start(y_table[bass.ds((2 * i + s) * P, P), :], y_out[:, s, :]).then_inc(y_stored[s], 16)
            sp.wait_ge(S["y_ready"], BLOCKS)
            sp.dma_start(y_table[FULL * P:BLOCKS * P, :], y_out[:, 0, :]).then_inc(y_stored[0], 16)

            sp.wait_ge(S["mix_done"], 1 + BLOCKS)
            for w, name in ((w1, "L0_ffn_expert_w1"), (w2, "L0_ffn_expert_w2"), (w3, "L0_ffn_expert_w3")):
                for e in range(EXPERTS):
                    sp.dma_start(w[:, e, :, :], a[name][e].rearrange("(h p) n -> p h n", p=P)).then_inc(S["weights_loaded"], 16)

            with sp.Fori(0, FULL) as b:
                sp.wait_ge(S["ey_added"], 2 + EXPERTS * b + EXPERTS)
                sp.dma_start(out[bass.ds(b * P, P), :], y_acc).then_inc(S["row_stored"], 16)
            sp.wait_ge(S["ey_added"], 2 + EXPERTS * BLOCKS)
            sp.dma_start(out[FULL * P:NODES, :], y_acc[0:LAST_ROWS, :]).then_inc(S["row_stored"], 16)
            sp.wait_ge(S["row_stored"], 1 + 16 * BLOCKS)

        @block.gpsimd
        def _(pool):
            nc.gpsimd.memset(base[:, FULL, :], 0.0).then_inc(S["x_zeroed"], 1)
            nc.gpsimd.iota(row_no[:, :], pattern=[[0, 1]], base=0, channel_multiplier=1).then_inc(S["consts"], 1)
            nc.gpsimd.iota(bound[:, :], pattern=[[1, BLOCKS + 1]], base=0, channel_multiplier=0).then_inc(S["consts"], 1)
            nc.gpsimd.memset(ident[:, :], 0.0).then_inc(S["pool_step"], 1)
            nc.gpsimd.memset(same_head[:, :], 0.0).then_inc(S["pool_step"], 1)
            nc.gpsimd.memset(upto[:, :], 1.0).then_inc(S["pool_step"], 1)
            nc.gpsimd.memset(last_block[:, :], 0.0).then_inc(S["pool_step"], 1)
            nc.gpsimd.memset(ones[:, :], 1.0).then_inc(S["consts"], 1)
            nc.gpsimd.memset(neg_block[:, :], -float(P)).then_inc(S["consts"], 1)
            nc.gpsimd.memset(acc_w[:, :], float(ROW)).then_inc(S["consts"], 1)
            nc.gpsimd.memset(probs[:, :], -1.0).then_inc(S["consts"], 1)
            nc.gpsimd.memset(minus_half[:, :], -0.5).then_inc(S["consts"], 1)
            nc.gpsimd.memset(half_power[:, :], 0.5).then_inc(S["consts"], 1)
            nc.gpsimd.memset(minus_one[:, :], -1.0).then_inc(S["consts"], 1)
            nc.gpsimd.memset(over_count[:, :], 1.0 / (HEAD_DIM - 1)).then_inc(S["consts"], 1)
            nc.gpsimd.memset(head_eps[:, :], HEAD_EPS).then_inc(S["consts"], 1)
            nc.gpsimd.iota(lane[:, :], pattern=[[1, P]], base=0, channel_multiplier=0,
                           allow_small_or_imprecise_dtypes=True).then_inc(S["consts"], 1)
            nc.gpsimd.iota(edge_no[:, :], pattern=[[P, STEP_TILES]], base=0, channel_multiplier=1,
                           allow_small_or_imprecise_dtypes=True).then_inc(S["consts"], 1)
            nc.gpsimd.iota(step_no, pattern=[[1, STEPS]], base=0, channel_multiplier=0,
                           allow_small_or_imprecise_dtypes=True).then_inc(S["consts"], 1)
            pool.wait_ge(S["pool_step"], 4)
            nc.gpsimd.affine_select(out=ident[:, :], in_=ident[:, :], compare_op=ALU.not_equal, fill=1.0, base=0,
                                    pattern=[[-1, P]], channel_multiplier=1).then_inc(S["consts"], 1)
            nc.gpsimd.affine_select(out=upto[:, :], in_=upto[:, :], compare_op=ALU.is_ge, fill=0.0, base=0,
                                    pattern=[[1, BLOCKS]], channel_multiplier=-1).then_inc(S["consts"], 1)
            nc.gpsimd.affine_select(out=last_block[:, :], in_=last_block[:, :], compare_op=ALU.not_equal, fill=1.0,
                                    base=-(BLOCKS - 1), pattern=[[0, 1]], channel_multiplier=1).then_inc(S["pool_step"], 1)
            pool.wait_ge(S["consts"], N_CONSTS - 1)
            pool.wait_ge(S["pool_step"], 5)
            for h in range(P // HEAD_DIM):
                part = slice(h * HEAD_DIM, (h + 1) * HEAD_DIM)
                nc.gpsimd.memset(same_head[part, part], 1.0).then_inc(S["pool_step"], 1)
            n = 5 + P // HEAD_DIM
            pool.wait_ge(S["pool_step"], n)
            nc.gpsimd.tensor_scalar(centre[:, :], same_head[:, :], -1.0 / HEAD_DIM, None, ALU.mult).then_inc(S["pool_step"], 1)
            pool.wait_ge(S["pool_step"], n + 1)
            nc.gpsimd.tensor_tensor(centre[:, :], centre[:, :], ident[:, :], ALU.add).then_inc(S["consts"], 1)
            pool.nop().then_inc(S["zed_ready"], 1)

            pool.wait_ge(S["x_stats_ready"], BLOCKS)
            nc.gpsimd.tensor_scalar(x_bias, x_mean_var[:, :, 1], LN_EPS, None, ALU.add).then_inc(S["pool_step"], 1)
            pool.wait_ge(S["pool_step"], n + 2)
            nc.gpsimd.tensor_tensor(x_rstd, x_bias, minus_half[:, :], ALU.pow).then_inc(S["pool_step"], 1)
            pool.wait_ge(S["pool_step"], n + 3)
            nc.gpsimd.tensor_tensor(x_bias, x_mean_var[:, :, 0], x_rstd, ALU.mult).then_inc(S["pool_step"], 1)
            pool.wait_ge(S["pool_step"], n + 4)
            nc.gpsimd.tensor_scalar(x_bias, x_bias, -1.0, None, ALU.mult).then_inc(S["x_norm"], 1)
            n += 4

            def spread(u, tiles, first):
                links = first + SPREAD_LINKS * u
                by_head = [v[:, 0:tiles, :].rearrange("p s (h c) -> p (s h) c", c=HEAD_DIM) for v in (dev, dev2, zed)]
                heads = tiles * HEADS
                pool.wait_ge(S["dev_ready"], u + 1)
                nc.gpsimd.tensor_tensor(by_head[1], by_head[0], by_head[0], ALU.mult).then_inc(S["pool_step"], 1)
                links += 1
                pool.wait_ge(S["pool_step"], links)
                width = HEAD_DIM // 2
                while width:
                    pair = (by_head[1][:, :, 0:width], by_head[1][:, :, width:2 * width])
                    to = pair[0] if width > 1 else dev_sum[:, 0:heads].unsqueeze(2)
                    nc.gpsimd.tensor_tensor(to, pair[0], pair[1], ALU.add).then_inc(S["pool_step"], 1)
                    links, width = links + 1, width // 2
                    pool.wait_ge(S["pool_step"], links)
                steps = ((dev_r, dev_sum, over_count, ALU.mult), (dev_sum, dev_r, half_power, ALU.pow),
                         (dev_r, dev_sum, head_eps, ALU.add), (dev_std, dev_r, minus_one, ALU.pow))
                for to, of, by, op in steps:
                    nc.gpsimd.tensor_tensor(to[:, 0:heads], of[:, 0:heads], by[:, 0:heads], op).then_inc(S["pool_step"], 1)
                    links += 1
                    pool.wait_ge(S["pool_step"], links)
                pool.wait_ge(S["z_summed"], u + 1)
                nc.gpsimd.tensor_tensor(by_head[2], by_head[0], dev_std[:, 0:heads].unsqueeze(2).broadcast_to([P, heads, HEAD_DIM]),
                                        ALU.mult).then_inc(S["zed_ready"], 1)

            with nc.gpsimd.Fori(0, PAIRS) as u:
                spread(u, 2, n)
            spread(PAIRS, 1, n)
            n += SPREAD_LINKS * (PAIRS + 1)

            pool.wait_ge(S["gate_ready"], 1)
            nc.gpsimd.tensor_tensor(y_scale, x_rstd, gate, ALU.mult).then_inc(S["y_params"], 1)
            nc.gpsimd.tensor_tensor(y_bias, x_bias, gate, ALU.mult).then_inc(S["y_params"], 1)

            pool.wait_ge(S["ln_loaded"], 16 * N_MIX_LOADS)
            pool.wait_ge(S["z_copied"], 2)
            for h in range(HALVES):
                last = nc.gpsimd.tensor_scalar(diag_sum[:, h, :], ident[:, :], z_sum[:, h:h + 1], None, ALU.mult)
                last.then_inc(S["diag_ready"], 1)
            nc.gpsimd.tensor_tensor(kw_sum, k_col_w, z_sum, ALU.mult).then_inc(S["pool_step"], 1)
            nc.gpsimd.tensor_tensor(kv_a, kv_a, v_row_w, ALU.mult).then_inc(S["pool_step"], 1)
            nc.gpsimd.tensor_scalar(kv_b, v_row_b, float(NODES), None, ALU.mult).then_inc(S["pool_step"], 1)
            pool.wait_ge(S["z_row_ready"], 1)
            nc.gpsimd.tensor_tensor(z_row, z_row, v_row_w, ALU.mult).then_inc(S["pool_step"], 1)
            pool.wait_ge(S["pool_step"], n + 4)
            nc.gpsimd.tensor_tensor(kv_b, kv_b, z_row, ALU.add).then_inc(S["pool_step"], 1)
            pool.wait_ge(S["pool_step"], n + 5)
            for h in range(HALVES):
                nc.gpsimd.tensor_scalar(kv_a[:, h, :], kv_a[:, h, :], k_col_w[:, h:h + 1], None, ALU.mult).then_inc(S["pool_step"], 1)
                nc.gpsimd.tensor_scalar(kv_b[:, h, :], kv_b[:, h, :], k_col_b[:, h:h + 1], None, ALU.mult).then_inc(S["pool_step"], 1)
                nc.gpsimd.tensor_scalar(z_row[:, h, :], v_row_b[:, h, :], kw_sum[:, h:h + 1], None, ALU.mult).then_inc(S["pool_step"], 1)
            pool.wait_ge(S["pool_step"], n + 5 + 3 * HALVES)
            nc.gpsimd.tensor_tensor(kv_a, kv_a, kv_b, ALU.add).then_inc(S["pool_step"], 1)
            pool.wait_ge(S["pool_step"], n + 6 + 3 * HALVES)
            nc.gpsimd.tensor_tensor(kv_a, kv_a, z_row, ALU.add).then_inc(S["pool_step"], 1)
            pool.wait_ge(S["pool_step"], n + 7 + 3 * HALVES)
            nc.gpsimd.tensor_tensor(kv_a, kv_a, same_head[:, :].unsqueeze(1).broadcast_to([P, HALVES, P]),
                                    ALU.mult).then_inc(S["pool_step"], 1)
            pool.wait_ge(S["pool_step"], n + 8 + 3 * HALVES)
            nc.gpsimd.tensor_scalar(kv_a, kv_a, 1.0 / NODES, None, ALU.mult).then_inc(S["pool_step"], 1)
            pool.wait_ge(S["pool_step"], n + 9 + 3 * HALVES)
            nc.gpsimd.tensor_tensor(kv[:, :, :], kv_a, ident[:, :].unsqueeze(1).broadcast_to([P, HALVES, P]),
                                    ALU.add).then_inc(S["kv_final"], 1)

            pool.wait_ge(y_stored[0], 1 + 16 * (PAIRS + 1))
            pool.wait_ge(y_stored[1], 1 + 16 * PAIRS)
            pool.wait_ge(S["mix_done"], 1 + BLOCKS)
            pool.wait_ge(S["below_ready"], 4)
            nc.gpsimd.memset(acc_mem[:, :], 0.0).then_inc(S["acc_zeroed"], 1)

            with nc.gpsimd.Fori(0, BLOCKS) as i:
                for j in range(STEPS_PER_BLOCK):
                    slot = j % GROUP
                    if slot == 0:
                        pool.wait_ge(S["idx_staged"], GROUPS_PER_BLOCK * i + j // GROUP + 1)
                    pool.wait_ge(S["sum_ps"], STEPS_PER_BLOCK * i + j + 1 + STEPS_PER_BLOCK - GROUP)
                    pool.nop().then_inc(S["slot_free"], 1)
                    nc.gpsimd.indirect_dma_start(
                        out=gathered[:, slot, :], out_offset=None, in_=y_table,
                        in_offset=bass.IndirectOffsetOnAxis(ap=step_idx[:, j:j + 1], axis=0)).then_inc(rows_in[slot], 16)

            with nc.gpsimd.Fori(0, BLOCKS) as b:
                pool.wait_ge(S["ffn_step"], FFN_LINKS * b + N_NORM)
                nc.gpsimd.tensor_tensor(rstd[:, 0:1], rstd[:, 1:2], minus_half[:, 0:1], ALU.pow).then_inc(S["x2_rstd"], 1)

        @block.scalar
        def _(act):
            act.nop().then_inc(S["mix_done"], 1)
            for s in range(2):
                act.nop().then_inc(y_stored[s], 1)
            act.nop().then_inc(S["h1_ready"], 2 * HALVES)
            act.nop().then_inc(S["h2_ready"], 2 * HALVES)
            act.wait_ge(S["small_loaded"], 16 * N_SMALL)
            act.wait_ge(S["x_loaded"], 32)
            act.wait_ge(S["x_norm"], 1)

            def norm(u, tiles):
                act.wait_ge(S["xT_ps"], u)
                for s in range(tiles):
                    act.wait_ge(S["x_norm"], 1)
                    nc.scalar.activation(xs[:, s, :], base[:, 2 * u + s, :], ACT.Identity, bias=x_bias[:, bass.ds(2 * u + s, 1)],
                                         scale=x_rstd[:, bass.ds(2 * u + s, 1)]).then_inc(S["xs_ready"], 1)

            def keep_turned(u, tiles):
                act.wait_ge(S["xT_ps"], u + 1)
                act.wait_ge(S["dev_ps"], u)
                act.wait_ge(S["xT_filed"], u)
                nc.scalar.activation(xsT[:, :, 0:tiles * P], ps_xT[:, :, 0:tiles * P], ACT.Copy).then_inc(S["xT_ready"], 1)

            def hidden(u, tiles):
                act.wait_ge(S["hid_ps"], u + 1)
                act.wait_ge(S["logit_ps"], u + 1)
                nc.scalar.activation(hid[:, 0:tiles * P], ps_hid[:, 0:tiles * P], ACT.Relu, bias=gnn_b1[:, 0:1]).then_inc(S["hid_ready"], 1)
                act.wait_ge(S["dev_ps"], u + 1)
                act.wait_ge(S["zed_ready"], u + 1)
                nc.scalar.activation(dev[:, 0:tiles, :], ps_dev[:, 0:tiles, :], ACT.Copy).then_inc(S["dev_ready"], 1)

            def file_turned(u, tiles):
                act.wait_ge(S["xT_ready"], u + 1)
                act.wait_ge(S["x_norm"], 1)
                nc.scalar.activation(xnT[:, :, bass.ds(2 * P * u, tiles * P)], xsT[:, :, 0:tiles * P], ACT.Copy).then_inc(S["xT_filed"], 1)

            norm(0, 2)
            keep_turned(0, 2)
            norm(1, 2)
            file_turned(0, 2)
            with nc.scalar.Fori(0, PAIRS - 2) as u:
                hidden(u, 2)
                keep_turned(u + 1, 2)
                norm(u + 2, 2)
                file_turned(u + 1, 2)
            for u in range(PAIRS - 2, PAIRS):
                tiles = 2 if u + 1 < PAIRS else 1
                hidden(u, 2)
                keep_turned(u + 1, tiles)
                if u + 2 <= PAIRS:
                    norm(u + 2, 1)
                file_turned(u + 1, tiles)
            hidden(PAIRS, 1)

            act.wait_ge(S["z_summed"], 1 + PAIRS + 1)
            nc.scalar.activation(kv_a, ps_z[:, :, 0:P], ACT.Copy).then_inc(S["z_copied"], 1)
            nc.scalar.activation(z_sum, ps_z[:, :, P], ACT.Copy).then_inc(S["z_copied"], 1)
            act.wait_ge(S["logit_ps"], 1 + PAIRS + 1)
            nc.scalar.activation(gate, ps_logit, ACT.Sigmoid, bias=gnn_b2[:, 0:1]).then_inc(S["gate_ready"], 1)
            act.wait_ge(S["z_row_ps"], HALVES)
            nc.scalar.activation(z_row, ps_z_row, ACT.Copy).then_inc(S["z_row_ready"], 1)

            def gated(t, s, pair):
                act.wait_ge(y_stored[s], 1 + 16 * pair)
                act.wait_ge(S["y_params"], 2)
                nc.scalar.activation(y_out[:, s, 0:DIM], base[:, t, :], ACT.Identity, bias=y_bias[:, bass.ds(t, 1)],
                                     scale=y_scale[:, bass.ds(t, 1)])
                nc.scalar.activation(y_out[:, s, DIM:ROW], gate[:, bass.ds(t, 1)], ACT.Copy).then_inc(S["y_ready"], 1)

            act.wait_ge(S["gate_ready"], 1)
            with nc.scalar.Fori(0, PAIRS) as i:
                for s in range(2):
                    gated(2 * i + s, s, i)
            gated(FULL, 0, PAIRS)

            def copy_upper(level, bit):
                into = keys[exchanges_before(level, bit) % 2]
                d = distance(bit)
                for half in range(2):
                    act.wait_ge(half_turned[half], turns_before(level, bit))
                    if d == HALF:
                        if half == 1:
                            nc.scalar.activation(half_view(into, 1), half_view(turned, 1), ACT.Copy).then_inc(upper_copied[1], 1)
                        else:
                            act.nop().then_inc(upper_copied[0], 1)
                        continue
                    pairs_in, pairs_out = (half_view(t, half).rearrange("p (g t d) -> p g t d", t=2, d=d) for t in (turned, into))
                    nc.scalar.activation(pairs_out[:, :, 1, :], pairs_in[:, :, 1, :], ACT.Copy).then_inc(upper_copied[half], 1)

            for level in range(TURNED + 1, LEVELS + 1):
                copy_upper(level, level - 1)
                copy_upper(level, TURNED - 1)
                first = (level - MIX_LEVEL) * TILES_PER_LEVEL
                if 0 <= first < BLOCKS:
                    act.wait_ge(S["kv_final"], 1)
                    with nc.scalar.Fori(first, first + TILES_PER_LEVEL) as t:
                        act.wait_ge(S["mix_ps"], t + 1)
                        act.wait_ge(S["kv_final"], 1)
                        nc.scalar.activation(mixT, xnT[:, :, bass.ds(t * P, P)], ACT.Copy).then_inc(S["mix_staged"], 1)
                        act.wait_ge(S["mix_ps"], 1 + t + 1)
                        act.wait_ge(S["kv_final"], 1)
                        nc.scalar.activation(base[:, t, :], ps_mix, ACT.Copy).then_inc(S["mix_done"], 1)

            for n, t in enumerate((dst_of_edge, src_of_edge)):
                act.wait_ge(S["fields_ready"], n + 1)
                nc.scalar.activation(t, t.bitcast(I32), ACT.Copy).then_inc(S["edges_ready"], 1)
            act.wait_ge(S["steps_ps"], 2)
            act.wait_ge(S["chunk_ready"], 1)
            nc.scalar.activation(step_acc, front[0:1, 0:STEPS], ACT.Copy).then_inc(S["acc_row_ready"], 1)
            act.wait_ge(S["picked_ps"], 1)
            nc.scalar.activation(step_rel, front[:, 0:STEPS], ACT.Copy).then_inc(S["tables_ready"], 1)

            act.wait_ge(S["tables_ready"], 2)
            with nc.scalar.Fori(0, BLOCKS) as i:
                for g in range(GROUPS_PER_BLOCK):
                    at = slice(g * GROUP, (g + 1) * GROUP)
                    act.wait_ge(S["sum_ps"], STEPS_PER_BLOCK * i + GROUP * (g + 1))
                    act.wait_ge(S["tables_ready"], 2)
                    nc.scalar.activation(step_idx[:, at], step_dst[:, bass.ds(STEPS_PER_BLOCK * i + GROUP * g, GROUP)],
                                         ACT.Copy).then_inc(S["idx_staged"], 1)

            def turned_rows(b):
                act.wait_ge(S["x2T_ps"], b + 1)
                nc.scalar.activation(next_T, ps_x2T, ACT.Copy).then_inc(S["x2T_ready"], 1)

            def router_hidden(b):
                act.wait_ge(S["router_ps"], b + 1)
                nc.scalar.activation(router_hid, ps_router, ACT.Relu, bias=router_b1[:, 0:1]).then_inc(S["router_ready"], 1)

            def exponentials(b):
                act.wait_ge(S["logit_max_ready"], b + 1)
                nc.scalar.activation(exp_l[:, :], ps_l, ACT.Exp, bias=logit_max[:, 0:1], accum_out=exp_sum[:, 0:1]).then_inc(S["exp_ready"], 1)
                act.wait_ge(S["top_diff_ready"], b + 1)
                nc.scalar.activation(top_w[:, 1:2], top_w[:, 0:1], ACT.Exp).then_inc(S["top_exp_ready"], 1)

            def relu(b, e, ps_done, ps, sb_t, bias, ready):
                act.wait_ge(ps_done, EXPERTS * b + e + 1)
                for h in range(HALVES):
                    nc.scalar.activation(sb_t[:, e % 2, h, :], ps[e % 2][:, h, :], ACT.Relu, bias=bias[:, e, h:h + 1]).then_inc(ready, 1)

            def experts(b, following):
                act.wait_ge(S["x2T_ready"], b + 1)
                nc.scalar.activation(this_T, next_T, ACT.Copy).then_inc(S["this_ready"], 1)
                relu(b, 0, S["h1_ps"], ps_h1, h1_T, b1, S["h1_ready"])
                act.wait_ge(S["gatesT_ps"], b + 1)
                nc.scalar.activation(gates_T, ps_gates_T, ACT.Copy).then_inc(S["gatesT_ready"], 1)
                relu(b, 1, S["h1_ps"], ps_h1, h1_T, b1, S["h1_ready"])
                for e in range(EXPERTS):
                    if e >= 1 and e + 1 < EXPERTS:
                        relu(b, e + 1, S["h1_ps"], ps_h1, h1_T, b1, S["h1_ready"])
                    relu(b, e, S["h2_ps"], ps_h2, h2_T, b2, S["h2_ready"])
                    if following and e == 2:
                        turned_rows(b + 1)
                    if following and e == 3:
                        router_hidden(b + 1)
                if following:
                    exponentials(b + 1)

            turned_rows(0)
            router_hidden(0)
            exponentials(0)
            with nc.scalar.Fori(0, FULL) as b:
                experts(b, True)
            experts(FULL, False)

        @block.tensor
        def _(pe):
            pe.nop().then_inc(S["logit_ps"], 1)
            pe.nop().then_inc(S["z_summed"], 1)
            pe.nop().then_inc(S["mix_ps"], 1)
            pe.nop().then_inc(S["sum_ps"], STEPS_PER_BLOCK)
            pe.wait_ge(S["consts"], N_CONSTS)
            pe.wait_ge(S["small_loaded"], 16 * N_SMALL)
            pe.wait_ge(S["z_zeroed"], 1)

            def turn_rows(u, tiles):
                pe.wait_ge(S["xs_ready"], 2 * u + tiles)
                pe.wait_ge(S["xT_ready"], u)
                for s in range(tiles):
                    for h in range(HALVES):
                        last = nc.tensor.transpose(ps_xT[:, h, s * P:(s + 1) * P], xs[:, s, h * P:(h + 1) * P], ident[:, :])
                last.then_inc(S["xT_ps"], 1)

            def hidden(u, tiles):
                pe.wait_ge(S["xT_ready"], u + 1)
                pe.wait_ge(S["hid_ready"], u)
                for h in range(HALVES):
                    last = nc.tensor.matmul(ps_hid[:, 0:tiles * P], gnn_w1[:, h, :], xsT[:, h, 0:tiles * P], start=(h == 0), stop=(h == 1))
                last.then_inc(S["hid_ps"], 1)
                pe.wait_ge(S["dev_ready"], u)
                for s in range(tiles):
                    for h in range(HALVES):
                        last = nc.tensor.matmul(ps_dev[:, s, h * P:(h + 1) * P], xsT[:, h, s * P:(s + 1) * P], centre[:, :],
                                                start=True, stop=True)
                last.then_inc(S["dev_ps"], 1)

            def logit(u, tiles):
                pe.wait_ge(S["hid_ready"], u + 1)
                for s in range(tiles):
                    last = nc.tensor.matmul(ps_logit[:, bass.ds(2 * u + s, 1)], hid[:, s * P:(s + 1) * P], gnn_w2[:, :], start=True,
                                            stop=True)
                last.then_inc(S["logit_ps"], 1)

            def sum_z(u, tiles):
                pe.wait_ge(S["zed_ready"], 1 + u + 1)
                for s in range(tiles):
                    for h in range(HALVES):
                        part = zed[:, s, h * P:(h + 1) * P]
                        nc.tensor.matmul(ps_z[:, h, 0:P], part, part, start=False, stop=False, skip_group_check=True)
                        last = nc.tensor.matmul(ps_z[:, h, P:P + 1], part, ones[:, 0:1], start=False, stop=False, skip_group_check=True)
                last.then_inc(S["z_summed"], 1)

            turn_rows(0, 2)
            turn_rows(1, 2)
            hidden(0, 2)
            logit(0, 2)
            with nc.tensor.Fori(1, PAIRS - 1) as u:
                turn_rows(u + 1, 2)
                hidden(u, 2)
                sum_z(u - 1, 2)
                logit(u, 2)
            turn_rows(PAIRS, 1)
            hidden(PAIRS - 1, 2)
            sum_z(PAIRS - 2, 2)
            logit(PAIRS - 1, 2)
            hidden(PAIRS, 1)
            sum_z(PAIRS - 1, 2)
            logit(PAIRS, 1)
            sum_z(PAIRS, 1)
            pe.wait_ge(S["diag_ready"], HALVES)
            for h in range(HALVES):
                nc.tensor.matmul(ps_z_row[:, h, :], ones[:, :], diag_sum[:, h, :], start=True, stop=True).then_inc(S["z_row_ps"], 1)

            def turn(level, bit):
                held = keys[exchanges_before(level, bit) % 2]
                for half in range(2):
                    pe.wait_ge(sorted_half[half], instructions_before(level, bit))
                    for at in range(half * HALF, (half + 1) * HALF, P):
                        last = nc.tensor.transpose(turned[:, at:at + P], held[:, at:at + P], ident[:, :])
                    last.then_inc(half_turned[half], 1)

            for level in range(TURNED + 1, LEVELS + 1):
                turn(level, level - 1)
                turn(level, TURNED - 1)
                first = (level - MIX_LEVEL) * TILES_PER_LEVEL
                if 0 <= first < BLOCKS:
                    pe.wait_ge(S["kv_final"], 1)
                    pe.wait_ge(S["dev_ready"], PAIRS + 1)
                    with nc.tensor.Fori(first, first + TILES_PER_LEVEL) as t:
                        pe.wait_ge(S["mix_staged"], t + 1)
                        pe.wait_ge(S["mix_done"], t + 1)
                        nc.tensor.matmul(ps_mix, ident[:, :], base[:, t, :], start=True, stop=False)
                        for h in range(HALVES):
                            last = nc.tensor.matmul(ps_mix[:, h * P:(h + 1) * P], mixT[:, h, :], kv[:, h, :],
                                                    start=False, stop=(h == 1))
                        last.then_inc(S["mix_ps"], 1)

            pe.wait_ge(S["below_ready"], 4)
            for n, (which, at) in enumerate(((0, 0), (0, 1), (1, 1))):
                last = nc.tensor.matmul(ps_counts[:, n:n + 1], below[:, which, at:at + BLOCKS], ones[:, 0:1], start=True, stop=True)
            last.then_inc(S["counts_ps"], 1)
            pe.wait_ge(S["counts_ready"], 2)
            nc.tensor.matmul(ps_end, upto[:, :], counts[:, 4:5], start=True, stop=True).then_inc(S["ends_ps"], 1)
            pe.wait_ge(S["past_ready"], 2)
            pe.wait_ge(S["mix_done"], 1 + BLOCKS)
            for ps, w in ((turned, chunk_w), (front, acc_w)):
                for at in range(0, STEPS, BANK):
                    to = min(at + BANK, STEPS)
                    last = nc.tensor.matmul(ps[:, at:to], w[:, :], past_block[:, at:to], start=True, stop=True)
                last.then_inc(S["steps_ps"], 1)
            pe.wait_ge(S["edges_ready"], 2)
            pe.wait_ge(S["chunk_ready"], 1)
            pe.wait_ge(S["acc_row_ready"], 1)
            picks = 0
            for tile in range(STEP_TILES):
                at, to = tile * P, min(tile * P + P, STEPS)
                sources = [c for c in (tile - 1, tile) if c >= 0]
                for c in sources:
                    chosen = pick[:, picks % PICKS, 0:to - at]
                    picks += 1
                    pe.wait_ge(S["pick_ready"], picks)
                    nc.tensor.matmul(turned[:, at:to], dst_of_edge[:, c * P:c * P + P], chosen, start=(c == sources[0]), stop=(c == tile))
                    nc.tensor.matmul(front[:, at:to], src_of_edge[:, c * P:c * P + P], chosen, start=(c == sources[0]),
                                     stop=False).then_inc(S["pick_used"], 1)
                last = nc.tensor.matmul(front[:, at:to], neg_block[:, :], past_block[:, at:to], start=False, stop=True)
            last.then_inc(S["picked_ps"], 1)

            pe.wait_ge(S["tables_ready"], 2)
            with nc.tensor.Fori(0, BLOCKS) as i:
                for j in range(STEPS_PER_BLOCK):
                    slot, group = j % GROUP, j // GROUP
                    if slot == 0:
                        pe.wait_ge(S["onehot_ready"], GROUPS_PER_BLOCK * i + group + 1)
                    pe.wait_ge(S["sum_added"], STEPS_PER_BLOCK * i + j + 1)
                    pe.wait_ge(rows_in[slot], 16 * (GROUPS_PER_BLOCK * i + group + 1))
                    nc.tensor.matmul(ps_sum[j % SUM_BANKS], onehot[:, j, :], gathered[:, slot, :], start=True,
                                     stop=True).then_inc(S["sum_ps"], 1)

            pe.wait_ge(S["weights_loaded"], 16 * 3 * EXPERTS)

            def turn_block(b):
                pe.wait_ge(S["x2_norm"], b + 1)
                pe.wait_ge(S["router_ready"], b)
                for h in range(HALVES):
                    last = nc.tensor.transpose(ps_x2T[:, h, :], xn2[:, h * P:(h + 1) * P], ident[:, :])
                last.then_inc(S["x2T_ps"], 1)

            def router(b):
                pe.wait_ge(S["x2T_ready"], b + 1)
                for h in range(HALVES):
                    last = nc.tensor.matmul(ps_router, router_w1[:, h, :], next_T[:, h, :], start=(h == 0), stop=(h == 1))
                last.then_inc(S["router_ps"], 1)

            def logits(b):
                pe.wait_ge(S["router_ready"], b + 1)
                pe.wait_ge(S["ffn_step"], FFN_LINKS * b)
                nc.tensor.matmul(ps_l, router_hid, router_w2[:, :], start=True, stop=False)
                nc.tensor.matmul(ps_l, ones[0:1, :], router_b2[:, :], start=False, stop=True).then_inc(S["logits_ps"], 1)

            def first_layer(b, e):
                n = EXPERTS * b + e
                pe.wait_ge(S["h1_ready"], HALVES * n + HALVES)
                for o in range(HALVES):
                    for h in range(HALVES):
                        last = nc.tensor.matmul(ps_h1[e % 2][:, o, :], w1[:, e, h, o * P:(o + 1) * P], this_T[:, h, :],
                                                start=(h == 0), stop=(h == 1))
                last.then_inc(S["h1_ps"], 1)

            def second_layer(b, e):
                n = EXPERTS * b + e
                pe.wait_ge(S["h2_ready"], HALVES * n + HALVES)
                pe.wait_ge(S["h1_ready"], 2 * HALVES + HALVES * n + HALVES)
                for o in range(HALVES):
                    for h in range(HALVES):
                        last = nc.tensor.matmul(ps_h2[e % 2][:, o, :], w2[:, e, h, o * P:(o + 1) * P], h1_T[:, e % 2, h, :],
                                                start=(h == 0), stop=(h == 1))
                last.then_inc(S["h2_ps"], 1)

            def third_layer(b, e):
                n = EXPERTS * b + e
                pe.wait_ge(S["ey_added"], n + 1)
                pe.wait_ge(S["h2_ready"], 2 * HALVES + HALVES * n + HALVES)
                for h in range(HALVES):
                    last = nc.tensor.matmul(ps_y[e % 2], h2_T[:, e % 2, h, :], w3[:, e, h, :], start=(h == 0), stop=(h == 1))
                last.then_inc(S["ey_ps"], 1)

            def experts(b, following):
                pe.wait_ge(S["this_ready"], b + 1)
                first_layer(b, 0)
                pe.wait_ge(S["gates_ready"], b + 1)
                nc.tensor.transpose(ps_gates_T, gates[:, :], ident[:, :]).then_inc(S["gatesT_ps"], 1)
                first_layer(b, 1)
                pe.wait_ge(S["gatesT_ready"], b + 1)
                nc.tensor.matmul(ps_b3, gates_T, b3[:, :], start=True, stop=True).then_inc(S["b3_ps"], 1)
                for e in range(EXPERTS):
                    if e >= 1:
                        if e + 1 < EXPERTS:
                            first_layer(b, e + 1)
                        third_layer(b, e - 1)
                    second_layer(b, e)
                    if following and e == 2:
                        turn_block(b + 1)
                    if following and e == 3:
                        router(b + 1)
                    if following and e == 4:
                        logits(b + 1)
                third_layer(b, EXPERTS - 1)

            turn_block(0)
            router(0)
            logits(0)
            with nc.tensor.Fori(0, FULL) as b:
                experts(b, True)
            experts(FULL, False)

        @block.vector
        def _(dve):
            dve.nop().then_inc(S["sum_added"], SUM_BANKS)
            dve.nop().then_inc(S["ey_added"], 2)
            dve.nop().then_inc(S["row_stored"], 1)
            nc.vector.memset(bank(3), 0.0).then_inc(S["z_zeroed"], 1)
            nc.vector.memset(keys[1], PAD_KEY).then_inc(S["key_step"], 1)
            dve.wait_ge(S["consts"], 2)
            nc.vector.tensor_scalar(row_odd[:, :], row_no[:, :], 1, None, ALU.bitwise_and).then_inc(S["key_step"], 1)
            nc.vector.tensor_scalar(bound[:, :], bound[:, :], BLOCK_SHIFT, KEY_BASE, ALU.logical_shift_left,
                                    ALU.bitwise_or).then_inc(S["key_step"], 1)
            dve.wait_ge(S["key_step"], 3)
            nc.vector.tensor_scalar(sign[:, 0:1], row_odd[:, :], -2.0, 1.0, ALU.mult, ALU.add).then_inc(S["key_step"], 1)
            nc.vector.tensor_scalar(sign[:, 1:2], row_odd[:, :], 2.0, -1.0, ALU.mult, ALU.add).then_inc(S["key_step"], 1)
            dve.wait_ge(S["edges_loaded"], 32)
            nc.vector.tensor_scalar(src_in[0:LOAD_ROWS, :], src_in[0:LOAD_ROWS, :], DST_BITS, KEY_BASE, ALU.logical_shift_left,
                                    ALU.bitwise_or).then_inc(S["key_step"], 1)
            dve.wait_ge(S["key_step"], 6)
            nc.vector.tensor_tensor(keys[1][0:LOAD_ROWS, 0:LOAD_COLS].bitcast(I32), src_in[0:LOAD_ROWS, :], dst_in[0:LOAD_ROWS, :],
                                    ALU.bitwise_or).then_inc(S["key_step"], 1)
            dve.wait_ge(S["key_step"], 7)
            flat, signed = (t.rearrange("p (g t) -> p g t", t=2) for t in (keys[1], keys[0]))
            for t in range(2):
                nc.vector.tensor_scalar(signed[:, :, t], flat[:, :, t], sign[:, t:t + 1], None, ALU.mult).then_inc(S["key_step"], 1)

            dve.wait_ge(S["x_loaded"], 32)
            dve.wait_ge(S["x_zeroed"], 1)
            with nc.vector.Fori(0, BLOCKS // 7) as t:
                for k in range(7):
                    nc.vector.bn_stats(x_stats[:, 7 * t + k, :], base[:, 7 * t + k, :]).then_inc(S["x_stat"], 1)
            dve.wait_ge(S["x_stat"], BLOCKS)
            for t in range(BLOCKS):
                nc.vector.bn_aggr(x_mean_var[:, t, :], x_stats[:, t, :]).then_inc(S["x_stats_ready"], 1)

            def exchange(level, bit, half):
                done = exchanges_before(level, bit)
                held, into = keys[done % 2], keys[(done + 1) % 2]
                d = distance(bit)
                both = d == HALF
                for other in range(2):
                    if both or other == half or (level == LEVELS and d == HALF // 2):
                        dve.wait_ge(sorted_half[other], instructions_before(level, bit) if other >= half or both else
                                    instructions_before(level, bit))
                if is_after_turn(level, bit):
                    for other in (range(2) if both else (half,)):
                        dve.wait_ge(half_turned[other], turns_before(level, bit))
                        dve.wait_ge(upper_copied[other], turns_before(level, bit))
                lower_from = turned if is_after_turn(level, bit) else held
                views = [t[:, 0:COLS] if both else half_view(t, half) for t in (lower_from, held, into)]
                if bit == level - 1 and splits(level):
                    lower, upper, o = (v.rearrange("p (g r t d) -> p g r t d", r=2, t=2, d=d) for v in views)
                    for r in range(2):
                        sides = (lower[:, :, r, 0, :], upper[:, :, r, 1, :])
                        for t, op in ((0, ALU.min), (1, ALU.max)):
                            nc.vector.scalar_tensor_tensor(o[:, :, r, t, :], sides[1 - r], -1.0, sides[r], ALU.mult,
                                                           op).then_inc(sorted_half[half], 1)
                    return
                lower, upper, o = (v.rearrange("p (g t d) -> p g t d", t=2, d=d) for v in views)
                sides = (lower[:, :, 0, :], upper[:, :, 1, :])
                r = half if level == LEVELS - 1 else 0
                for t, op in ((0, ALU.min), (1, ALU.max)):
                    if bit == level - 1:
                        last = nc.vector.scalar_tensor_tensor(o[:, :, t, :], sides[1 - r], -1.0, sides[r], ALU.mult, op)
                    else:
                        last = nc.vector.tensor_tensor(o[:, :, t, :], sides[0], sides[1], op)
                    last.then_inc(sorted_half[t if both else half], 2 if both else 1)

            dve.wait_ge(S["key_step"], 9)
            for level in range(1, LEVELS + 1):
                for bit in range(level - 1, -1, -1):
                    for half in range(1 if distance(bit) == HALF and bit >= TURNED else 2):
                        exchange(level, bit, half)
            ordered = keys[exchanges_before(LEVELS + 1, LEVELS) % 2]

            for half in range(2):
                dve.wait_ge(sorted_half[half], SORT_END)
            bits = ordered[:, 0:EDGE_COLS].bitcast(I32)
            nc.vector.tensor_scalar(dst_of_edge.bitcast(I32), bits, DST_MASK, None, ALU.bitwise_and).then_inc(S["fields_ready"], 1)
            nc.vector.tensor_scalar(src_of_edge.bitcast(I32), bits, DST_BITS, DST_MASK, ALU.logical_shift_right,
                                    ALU.bitwise_and).then_inc(S["fields_ready"], 1)
            ends = ordered.rearrange("p (c n) -> p c n", n=P)
            limits = bound[:, :].bitcast(F32).unsqueeze(2).broadcast_to([P, BLOCKS + 1, COLS // P])
            for n, lane_of in enumerate((P - 1, 0)):
                keys_at = ends[:, :, lane_of].unsqueeze(1).broadcast_to([P, BLOCKS + 1, COLS // P])
                if n:
                    dve.wait_ge(S["below_ready"], 2)
                nc.vector.tensor_tensor(cut, keys_at, limits, ALU.is_lt).then_inc(S["below_ready"], 1)
                dve.wait_ge(S["below_ready"], 2 * n + 1)
                nc.vector.tensor_reduce(below[:, n, :], cut, AX.X, ALU.add).then_inc(S["below_ready"], 1)
            dve.wait_ge(S["counts_ps"], 1)
            nc.vector.tensor_copy(counts[:, 0:3], ps_counts[:, 0:3]).then_inc(S["counts_ready"], 1)
            dve.wait_ge(S["counts_ready"], 1)
            nc.vector.tensor_tensor(counts[:, 4:5], counts[:, 2:3], counts[:, 0:1], ALU.subtract).then_inc(S["counts_ready"], 1)
            nc.vector.tensor_tensor(counts[:, 5:6], counts[:, 1:2], counts[:, 2:3], ALU.subtract).then_inc(S["counts_ready"], 1)
            dve.wait_ge(S["counts_ready"], 3)
            nc.vector.scalar_tensor_tensor(counts[:, 6:7], last_block[:, :], 2.0 * EDGE_COLS, counts[:, 5:6], ALU.mult,
                                           ALU.add).then_inc(S["counts_ready"], 1)
            dve.wait_ge(S["counts_ready"], 4)
            nc.vector.tensor_scalar(chunk_w[:, :], ones[0:BLOCKS, :], counts[:, 6:7], None, ALU.mult).then_inc(S["past_ready"], 1)
            dve.wait_ge(S["ends_ps"], 1)
            nc.vector.tensor_copy(counts[:, 7:8], ps_end).then_inc(S["counts_ready"], 1)
            dve.wait_ge(S["counts_ready"], 5)
            nc.vector.tensor_scalar(past_block, step_no[0:BLOCKS, :], counts[:, 7:8], None, ALU.is_ge).then_inc(S["past_ready"], 1)
            dve.wait_ge(S["steps_ps"], 1)
            nc.vector.tensor_tensor(chunk_of_step, turned[:, 0:STEPS], step_no, ALU.add).then_inc(S["chunk_ready"], 1)
            dve.wait_ge(S["chunk_ready"], 1)
            picks = 0
            for tile in range(STEP_TILES):
                at, to = tile * P, min(tile * P + P, STEPS)
                for c in [c for c in (tile - 1, tile) if c >= 0]:
                    if picks >= PICKS:
                        dve.wait_ge(S["pick_used"], picks - PICKS + 1)
                    nc.vector.tensor_scalar(pick[:, picks % PICKS, 0:to - at], chunk_of_step[:, at:to], edge_no[:, c:c + 1], None,
                                            ALU.is_equal).then_inc(S["pick_ready"], 1)
                    picks += 1
            dve.wait_ge(S["picked_ps"], 1)
            nc.vector.tensor_copy(step_dst, turned[:, 0:STEPS]).then_inc(S["tables_ready"], 1)

            dve.wait_ge(S["tables_ready"], 2)
            dve.wait_ge(S["acc_row_ready"], 1)
            dve.wait_ge(S["acc_zeroed"], 1)
            with nc.vector.Fori(0, BLOCKS) as i:
                for g in range(GROUPS_PER_BLOCK):
                    first = STEPS_PER_BLOCK * i + GROUP * g
                    dve.wait_ge(S["sum_ps"], first + GROUP)
                    nc.vector.tensor_tensor(onehot[:, g * GROUP:(g + 1) * GROUP, :],
                                            lane[:, :].unsqueeze(1).broadcast_to([P, GROUP, P]),
                                            step_rel[:, bass.ds(first, GROUP)].unsqueeze(2).broadcast_to([P, GROUP, P]),
                                            ALU.is_equal).then_inc(S["onehot_ready"], 1)
                    for j in range(GROUP):
                        place = dve.value_load(step_acc[0:1, bass.ds(first + j, 1)], min_val=0, max_val=BLOCKS * ROW)
                        sums = acc_mem[:, bass.ds(place, ROW)]
                        dve.wait_ge(S["sum_added"], first + j + SUM_BANKS)
                        dve.wait_ge(S["sum_ps"], first + j + 1 + STEPS_PER_BLOCK)
                        nc.vector.tensor_tensor(sums, sums, ps_sum[(g * GROUP + j) % SUM_BANKS], ALU.add).then_inc(S["sum_added"], 1)

            dve.wait_ge(S["sum_added"], SUM_BANKS + STEPS)

            def normalise(b):
                n = FFN_LINKS * b
                dve.wait_ge(S["ffn_step"], n)
                nc.vector.tensor_scalar(den[:, 0:1], acc_mem[:, bass.ds(ROW * b + DIM, 1)], 1e-12, None, ALU.max).then_inc(S["ffn_step"], 1)
                dve.wait_ge(S["ffn_step"], n + 1)
                nc.vector.reciprocal(den[:, 1:2], den[:, 0:1]).then_inc(S["ffn_step"], 1)
                dve.wait_ge(S["ffn_step"], n + 2)
                nc.vector.scalar_tensor_tensor(x2, acc_mem[:, bass.ds(ROW * b, DIM)], den[:, 1:2], base[:, b, :], ALU.mult,
                                               ALU.add).then_inc(S["ffn_step"], 1)
                dve.wait_ge(S["ffn_step"], n + 3)
                nc.vector.bn_stats(stats[:, :], x2).then_inc(S["ffn_step"], 1)
                dve.wait_ge(S["ffn_step"], n + 4)
                dve.nop().then_inc(S["ffn_pass"], 1)
                nc.vector.bn_aggr(mean_var[:, :], stats[:, :]).then_inc(S["ffn_step"], 1)
                dve.wait_ge(S["ffn_step"], n + 5)
                nc.vector.tensor_scalar(rstd[:, 1:2], mean_var[:, 1:2], LN_EPS, None, ALU.add).then_inc(S["ffn_step"], 1)
                dve.wait_ge(S["x2_rstd"], b + 1)
                dve.wait_ge(S["x2T_ps"], b)
                nc.vector.tensor_scalar(xn2, x2, mean_var[:, 0:1], rstd[:, 0:1], ALU.subtract, ALU.mult).then_inc(S["x2_norm"], 1)

            def route(b):
                n = FFN_LINKS * b + N_NORM
                dve.wait_ge(S["logits_ps"], b + 1)
                nc.vector.tensor_reduce(logit_max[:, :], ps_l, AX.X, ALU.max, negate=True).then_inc(S["logit_max_ready"], 1)
                dve.wait_ge(S["exp_ready"], b + 1)
                nc.vector.reciprocal(exp_sum[:, 1:2], exp_sum[:, 0:1]).then_inc(S["ffn_step"], 1)
                dve.wait_ge(S["ffn_step"], n + 1)
                nc.vector.tensor_scalar(probs[:, 0:EXPERTS], exp_l[:, :], exp_sum[:, 1:2], None, ALU.mult).then_inc(S["ffn_step"], 1)
                dve.wait_ge(S["ffn_step"], n + 2)
                dve.nop().then_inc(S["ffn_pass"], 1)
                nc.vector.max(top[:, :], probs[:, :]).then_inc(S["ffn_step"], 1)
                dve.wait_ge(S["ffn_step"], n + 3)
                nc.vector.tensor_tensor(top_w[:, 0:1], top[:, 1:2], top[:, 0:1], ALU.subtract).then_inc(S["top_diff_ready"], 1)
                nc.vector.max_index(top_i[:, :], top[:, :], probs[:, :]).then_inc(S["ffn_step"], 1)
                dve.wait_ge(S["ffn_step"], n + 4)
                nc.vector.tensor_copy(top_f[:, :], top_i[:, 0:2]).then_inc(S["ffn_step"], 1)
                dve.wait_ge(S["top_exp_ready"], b + 1)
                nc.vector.tensor_scalar(top_w[:, 2:3], top_w[:, 1:2], 1.0, None, ALU.add).then_inc(S["ffn_step"], 1)
                dve.wait_ge(S["ffn_step"], n + 6)
                nc.vector.reciprocal(top_w[:, 3:4], top_w[:, 2:3]).then_inc(S["ffn_step"], 1)
                dve.wait_ge(S["ffn_step"], n + 7)
                nc.vector.tensor_tensor(top_w[:, 0:1], top_w[:, 1:2], top_w[:, 3:4], ALU.mult).then_inc(S["ffn_step"], 1)
                dve.wait_ge(S["ffn_step"], n + 8)
                nc.vector.tensor_scalar(gate_1[:, :], lane[:, 0:EXPERTS], top_f[:, 0:1], top_w[:, 3:4], ALU.is_equal,
                                        ALU.mult).then_inc(S["ffn_step"], 1)
                nc.vector.tensor_scalar(gate_2[:, :], lane[:, 0:EXPERTS], top_f[:, 1:2], top_w[:, 0:1], ALU.is_equal,
                                        ALU.mult).then_inc(S["ffn_step"], 1)
                dve.wait_ge(S["ffn_step"], n + N_ROUTE)
                nc.vector.tensor_tensor(gates[:, :], gate_1[:, :], gate_2[:, :], ALU.add).then_inc(S["gates_ready"], 1)

            def combine(b, following):
                dve.wait_ge(S["row_stored"], 1 + 16 * b)
                dve.wait_ge(S["b3_ps"], b + 1)
                nc.vector.tensor_tensor(y_acc, x2, ps_b3, ALU.add).then_inc(S["ffn_step"], 1)
                if following:
                    normalise(b + 1)
                dve.wait_ge(S["ffn_step"], FFN_LINKS * b + FFN_LINKS)
                for e in range(EXPERTS):
                    n = EXPERTS * b + e
                    dve.wait_ge(S["ey_added"], n + 2)
                    dve.wait_ge(S["ey_ps"], n + 1)
                    nc.vector.scalar_tensor_tensor(y_acc, ps_y[e % 2], gates[:, e:e + 1], y_acc, ALU.mult,
                                                   ALU.add).then_inc(S["ey_added"], 1)
                if following:
                    route(b + 1)

            normalise(0)
            route(0)
            with nc.vector.Fori(0, FULL) as b:
                combine(b, True)
            combine(FULL, False)


INPUTS = ["x", "src", "dst", "L0_gnn_W1", "L0_gnn_b1", "L0_gnn_W2", "L0_gnn_b2", "L0_mix_kln_weight", "L0_mix_kln_bias",
          "L0_mix_vln_weight", "L0_mix_vln_bias", "L0_ffn_router_w1", "L0_ffn_router_b1", "L0_ffn_router_w2", "L0_ffn_router_b2",
          "L0_ffn_expert_w1", "L0_ffn_expert_b1", "L0_ffn_expert_w2", "L0_ffn_expert_b2", "L0_ffn_expert_w3", "L0_ffn_expert_b3"]


def kernel(**inputs):
    import concourse.bacc as bacc
    from concourse.bass_utils import run_bass_kernel_spmd

    nc = bacc.Bacc("TRN2", target_bir_lowering=False, num_devices=1)
    arrays, aps = {}, {}
    for name in INPUTS:
        arrays[f"in_{name}"] = np.ascontiguousarray(inputs[name])
        shape, dt = arrays[f"in_{name}"].shape, mybir.dt.from_np(arrays[f"in_{name}"].dtype)
        aps[name] = nc.dram_tensor(f"in_{name}", shape, dt, kind="ExternalInput").ap()
    out = nc.dram_tensor("out_rows", (NODES, DIM), F32, kind="ExternalOutput").ap()
    y_table = nc.dram_tensor("gated_rows", (BLOCKS * P, ROW), F32, kind="Internal").ap()
    gps_layer(nc, aps, out, y_table)
    result = run_bass_kernel_spmd(nc, [arrays], core_ids=[0])
    return result.results[0]["out_rows"]
```

```python
from contextlib import ExitStack

import numpy as np
import concourse.bass as bass
from concourse import mybir

ALU = mybir.AluOpType
ACT = mybir.ActivationFunctionType
AX = mybir.AxisListType
F32 = mybir.dt.float32
I32 = mybir.dt.int32
U32 = mybir.dt.uint32

P = 128
NODES, DIM = 6250, 256
EDGES = 200000
HID = 128
HEADS = 8
HEAD_DIM = DIM // HEADS
EXPERTS = 6
HALVES = DIM // P
LN_EPS = 1e-5
HEAD_EPS = 1e-5

BLOCKS = -(-NODES // P)
LAST_ROWS = NODES - (BLOCKS - 1) * P
ROW = DIM + 1

LEVELS = 18
COLS = 2**LEVELS // P
HALF = COLS // 2
TURNED = 7
LOAD_ROWS = 125
LOAD_COLS = EDGES // LOAD_ROWS
DST_BITS = 13
DST_MASK = 2**DST_BITS - 1
BLOCK_SHIFT = DST_BITS + 7
KEY_BASE = 0x38000000
PAD_KEY = float(np.array([KEY_BASE | (BLOCKS * P) << DST_BITS], np.int32).view(np.float32)[0])

CHUNKS = -(-EDGES // P)
GROUP = 11
GROUPS_PER_BLOCK = 3
STEPS_PER_BLOCK = GROUP * GROUPS_PER_BLOCK
STEPS = STEPS_PER_BLOCK * BLOCKS
assert STEPS >= CHUNKS + BLOCKS - 1
STEP_TILES = -(-STEPS // P)
EDGE_COLS = STEP_TILES * P
TABLE = STEPS + STEPS_PER_BLOCK
SUM_BANKS = 3
BANK = 512
PICKS = 3
RUNS = ((0, 3), (3, 6), (6, 9), (9, GROUP))
FIRST_AT = [5 * e for e in range(6)]
SECOND_AT = [5 * e + 2 for e in range(6)]
THIRD_AT = [5 * e + 4 for e in range(6)]
ADD_AT = [5 * e + 5 for e in range(6)]
GATES_AT, BIAS_AT, BEGIN_AT = 0, 2, 3
NORM_AT, ROOT_AT = 8, 12
TURN_AT, ROUTER_AT, LOGITS_AT = 17, 19, 21
PEAK_AT, PROBS_AT, TOP_AT, INDEX_AT, SHARE_AT, MOVE_AT, SPREAD_AT = 23, 25, 26, 27, 28, 29, 31
assert FIRST_AT[-1] < MOVE_AT and ADD_AT[-1] < SPREAD_AT < STEPS_PER_BLOCK


def splits(level):
    return level not in (TURNED, LEVELS - 1, LEVELS)


def exchanges_before(level, bit):
    return level * (level - 1) // 2 + level - 1 - bit


def instructions_before(level, bit):
    whole = sum(2 * k + 2 * splits(k) for k in range(1, level))
    return whole + 2 * (level - 1 - bit) + (2 if splits(level) and bit < level - 1 else 0)


def turns_before(level, bit):
    if level <= TURNED:
        return 0
    return 2 * (level - TURNED - 1) + (2 if bit < TURNED else 1)


def is_after_turn(level, bit):
    return level > TURNED and bit in (level - 1, TURNED - 1)


def distance(bit):
    return 2**bit if bit < TURNED else 2 ** (bit - TURNED)


SORT_END = instructions_before(LEVELS + 1, LEVELS)
TURNS_END = 2 * (LEVELS - TURNED)


def gps_layer(nc, a, out, y_table):
    with ExitStack() as ctx:
        def sb(name, shape, dt=F32):
            return ctx.enter_context(nc.sbuf_tensor(name, shape, dt))

        def sem(name):
            return ctx.enter_context(nc.semaphore(name))

        base = sb("base", [P, BLOCKS, DIM])
        acc_mem = sb("acc_mem", [P, (BLOCKS + 1) * ROW])
        feat_mem = sb("feat_mem", [P, HALVES * BLOCKS * P])
        sort_mem = sb("sort_mem", [P, STEPS_PER_BLOCK * P])
        gath_mem = sb("gath_mem", [P, 2 * EDGE_COLS])
        tab_mem = sb("tab_mem", [P, 2 * TABLE + STEPS])

        keys = [sort_mem[:, 0:COLS], sort_mem[:, COLS:2 * COLS]]
        src_in = gath_mem[:, 0:LOAD_COLS].bitcast(I32)
        dst_in = gath_mem[:, LOAD_COLS:2 * LOAD_COLS].bitcast(I32)
        dst_of_edge = gath_mem[:, 0:EDGE_COLS]
        src_of_edge = gath_mem[:, EDGE_COLS:2 * EDGE_COLS]
        chunk_of_step = keys[0][:, 0:STEPS]
        pick = keys[0][:, STEPS:STEPS + PICKS * P].rearrange("p (s n) -> p s n", s=PICKS)
        past_block = keys[1][0:BLOCKS, 0:STEPS]
        step_dst = tab_mem[:, 0:STEPS].bitcast(U32)
        step_rel = tab_mem[:, TABLE:TABLE + STEPS]
        step_no = tab_mem[:, 2 * TABLE:2 * TABLE + STEPS]
        step_acc = tab_mem[0:1, 2 * TABLE:2 * TABLE + STEPS].bitcast(I32)
        dst_ahead, rel_ahead = tab_mem[:, 0:TABLE].bitcast(U32), tab_mem[:, TABLE:2 * TABLE]
        gathered = gath_mem[:, 0:GROUP * ROW].rearrange("p (s n) -> p s n", s=GROUP)
        onehot = sort_mem[:, :].rearrange("p (s n) -> p s n", s=STEPS_PER_BLOCK)
        used = [0]

        def early(n):
            at = used[0]
            used[0] += n
            assert used[0] <= (BLOCKS + 1) * ROW
            return acc_mem[:, at:at + n]

        def slots(t, n=2):
            return t.rearrange("p (s n) -> p s n", s=n)

        xnT = feat_mem[:, :].rearrange("p (h n) -> p h n", h=HALVES)
        x_stats = early(6 * BLOCKS).rearrange("p (b n) -> p b n", n=6)
        x_mean_var = early(2 * BLOCKS).rearrange("p (b n) -> p b n", n=2)
        x_rstd, x_bias, gate, y_scale, y_bias = (early(BLOCKS) for _ in range(5))
        xs, dev, dev2, zed = (slots(early(2 * DIM)) for _ in range(4))
        xsT = early(2 * DIM).rearrange("p (h n) -> p h n", h=HALVES)
        mixT = early(DIM).rearrange("p (h n) -> p h n", h=HALVES)
        hid = early(2 * P)
        y_out = slots(early(2 * ROW))
        dev_sum, dev_r, dev_std = (early(2 * HEADS) for _ in range(3))
        k_col_w, k_col_b, z_sum, kw_sum = (early(HALVES) for _ in range(4))
        v_row_w, v_row_b, z_row, kv_a, kv_b = (early(DIM).rearrange("p (h n) -> p h n", h=HALVES) for _ in range(5))
        diag_sum = early(DIM).rearrange("p (h n) -> p h n", h=HALVES)
        late = [0]

        def after(n):
            at = late[0]
            late[0] += n
            assert late[0] <= HALVES * BLOCKS * P
            return feat_mem[:, at:at + n]

        w1, w2, w3 = (after(EXPERTS * HALVES * DIM).rearrange("p (e h n) -> p e h n", e=EXPERTS, h=HALVES) for _ in range(3))
        x2, xn2, y_acc = after(DIM), after(DIM), after(DIM)
        next_T, this_T = (after(DIM).rearrange("p (h n) -> p h n", h=HALVES) for _ in range(2))
        router_hid = after(P)
        gates_T = after(P)[0:EXPERTS, :]
        h1_T, h2_T = (after(2 * DIM).rearrange("p (s h n) -> p s h n", s=2, h=HALVES) for _ in range(2))
        ident, lane, centre, ones, same_head = (sb(n, [P, P]) for n in ("ident", "lane", "centre", "ones", "same_head"))
        kv = sb("kv", [P, HALVES, P])
        gnn_w1, router_w1 = sb("gnn_w1", [P, HALVES, HID]), sb("router_w1", [P, HALVES, HID])
        gnn_w2, gnn_b1, gnn_b2, router_b1 = (sb(n, [P, 1]) for n in ("gnn_w2", "gnn_b1", "gnn_b2", "router_b1"))
        router_w2, router_b2 = sb("router_w2", [P, EXPERTS]), sb("router_b2", [1, EXPERTS])
        b1, b2 = sb("b1", [P, EXPERTS, HALVES]), sb("b2", [P, EXPERTS, HALVES])
        b3 = sb("b3", [EXPERTS, DIM])
        row_no, row_odd = sb("row_no", [P, 1], I32), sb("row_odd", [P, 1], I32)
        sign = sb("sign", [P, 2])
        bound = sb("bound", [P, BLOCKS + 1], I32)
        below = sb("below", [P, 2, BLOCKS + 1])
        cut = acc_mem[:, used[0]:used[0] + (BLOCKS + 1) * (COLS // P)].rearrange("p (b c) -> p b c", b=BLOCKS + 1)
        used[0] += (BLOCKS + 1) * (COLS // P)
        assert used[0] <= (BLOCKS + 1) * ROW
        counts = sb("counts", [BLOCKS, 8])
        chunk_w, neg_block, acc_w = (sb(n, [BLOCKS, P]) for n in ("chunk_w", "neg_block", "acc_w"))
        upto = sb("upto", [BLOCKS, BLOCKS])
        edge_no = sb("edge_no", [P, STEP_TILES])
        last_block, step_limit, late_block = (sb(n, [BLOCKS, 1]) for n in ("last_block", "step_limit", "late_block"))
        late_flag = sb("late_flag", [1, 1], I32)
        ln_eps = sb("ln_eps", [P, 1])
        step_idx = sb("step_idx", [P, STEPS_PER_BLOCK], U32)
        minus_half = sb("minus_half", [P, BLOCKS])
        half_power, minus_one, over_count, head_eps = (sb(n, [P, 2 * HEADS]) for n in ("half_power", "minus_one", "over_count", "head_eps"))
        den, stats, mean_var = sb("den", [P, 2]), sb("stats", [P, 6]), sb("mean_var", [P, 2])
        rstd, logit_max, exp_l = sb("rstd", [P, 2]), sb("logit_max", [P, 1]), sb("exp_l", [P, EXPERTS])
        exp_sum, probs, top, top_i = sb("exp_sum", [P, 2]), sb("probs", [P, 8]), sb("top", [P, 8]), sb("top_i", [P, 8], U32)
        top_f, top_w = sb("top_f", [P, 2]), sb("top_w", [P, 4])
        gate_1, gate_2, gates = (sb(n, [P, EXPERTS]) for n in ("gate_1", "gate_2", "gates"))

        turned = ctx.enter_context(nc.psum_tensor("turned", [P, COLS], F32))
        front = ctx.enter_context(nc.psum_tensor("front", [P, COLS], F32))

        def bank(i):
            return front[:, i * BANK:(i + 1) * BANK]

        ps_xT = bank(0).rearrange("p (h n) -> p h n", h=HALVES)
        ps_dev = slots(bank(1))
        ps_hid = bank(2)[:, 0:2 * P]
        ps_z = bank(3)[:, 0:HALVES * (P + 1)].rearrange("p (h n) -> p h n", h=HALVES)
        ps_logit = bank(2)[:, 2 * P:2 * P + BLOCKS]
        ps_z_row = bank(0)[:, 0:DIM].rearrange("p (h n) -> p h n", h=HALVES)
        ps_mix = bank(1)[:, 0:DIM]
        ps_counts = bank(3)[0:BLOCKS, 0:4]
        ps_end = bank(3)[0:BLOCKS, 4:5]
        ps_sum = [turned[:, BANK * i:BANK * i + ROW] for i in range(SUM_BANKS)]
        ps_late = turned[0:1, STEPS:STEPS + 1]
        ps_h1, ps_h2 = (bank(n)[:, 0:DIM].rearrange("p (h n) -> p h n", h=HALVES) for n in range(2))
        ps_y = bank(3)[:, 0:DIM]
        ps_x2T = bank(2)[:, 0:DIM].rearrange("p (h n) -> p h n", h=HALVES)
        ps_b3 = bank(2)[:, 0:DIM]
        ps_router = bank(2)[:, DIM:DIM + P]
        ps_l = bank(2)[:, DIM:DIM + EXPERTS]
        ps_gates_T = bank(2)[0:EXPERTS, DIM + P:DIM + 2 * P]

        names = """x_loaded x_zeroed edges_loaded small_loaded ln_loaded consts weights_loaded
            key_step pool_step act_step x_stat x_stats_ready x_norm
            xs_ready xT_ps xT_ready xT_filed hid_ps hid_ready logit_ps dev_ps dev_ready zed_ready z_summed z_zeroed
            z_copied diag_ready z_row_ps z_row_ready kv_final gate_ready y_params y_ready
            mix_staged mix_ps mix_done
            fields_ready edges_ready below_ready counts_ps counts_ready ends_ps past_ready steps_ps chunk_ready
            acc_row_ready pick_ready pick_used picked_ps tables_ready acc_zeroed
            idx_staged slot_free onehot_ready sum_ps sum_added
            late_ready ffn_step ffn_pass x2_var x2_std x2_norm x2T_ps x2T_ready router_ps router_ready logits_ps logit_max_ready
            exp_ready top_diff_ready top_exp_ready gates_ready gatesT_ps gatesT_ready b3_ps this_ready y_begun
            h1_ps h1_ready h2_ps h2_ready ey_ps ey_added row_stored""".split()
        S = {name: sem(name) for name in names}
        sorted_half = [sem("sorted_half0"), sem("sorted_half1")]
        half_turned = [sem("half_turned0"), sem("half_turned1")]
        upper_copied = [sem("upper_copied0"), sem("upper_copied1")]
        y_stored = [sem("y_stored0"), sem("y_stored1")]
        rows_in = [sem(f"rows_in{i}") for i in range(GROUP)]

        N_CONSTS = 20
        SPREAD_LINKS = 1 + HEAD_DIM.bit_length() - 1 + 4
        N_SMALL = 13
        N_MIX_LOADS = 6
        FULL = BLOCKS - 1
        PAIRS = FULL // 2
        MIX_LEVEL = 11
        TILES_PER_LEVEL = BLOCKS // (LEVELS - MIX_LEVEL)
        assert TILES_PER_LEVEL * (LEVELS - MIX_LEVEL) == BLOCKS
        N_NORM, N_ROUTE = 5, 10
        FFN_LINKS = N_NORM + N_ROUTE

        def half_view(t, half):
            return t[:, half * HALF:(half + 1) * HALF]

        block = ctx.enter_context(nc.Block())

        @block.sync
        def _(sp):
            sp.dma_start(src_in[0:LOAD_ROWS, :], a["src"].rearrange("(p c) -> p c", p=LOAD_ROWS)).then_inc(S["edges_loaded"], 16)
            sp.dma_start(dst_in[0:LOAD_ROWS, :], a["dst"].rearrange("(p c) -> p c", p=LOAD_ROWS)).then_inc(S["edges_loaded"], 16)
            sp.dma_start(base[:, 0:FULL, :], a["x"][0:FULL * P, :].rearrange("(b p) d -> p b d", p=P)).then_inc(S["x_loaded"], 16)
            sp.wait_ge(S["x_zeroed"], 1)
            sp.dma_start(base[0:LAST_ROWS, FULL, :], a["x"][FULL * P:NODES, :]).then_inc(S["x_loaded"], 16)
            sp.dma_start(gnn_w1[:, :, :], a["L0_gnn_W1"].rearrange("(h p) n -> p h n", p=P)).then_inc(S["small_loaded"], 16)
            sp.dma_start(gnn_b1[:, :], a["L0_gnn_b1"].rearrange("(p o) -> p o", o=1)).then_inc(S["small_loaded"], 16)
            sp.dma_start(gnn_w2[:, :], a["L0_gnn_W2"]).then_inc(S["small_loaded"], 16)
            sp.dma_start(gnn_b2[:, :], a["L0_gnn_b2"].partition_broadcast(P)).then_inc(S["small_loaded"], 16)
            sp.dma_start(router_w1[:, :, :], a["L0_ffn_router_w1"].rearrange("(h p) n -> p h n", p=P)).then_inc(S["small_loaded"], 16)
            sp.dma_start(router_b1[:, :], a["L0_ffn_router_b1"].rearrange("(p o) -> p o", o=1)).then_inc(S["small_loaded"], 16)
            sp.dma_start(router_w2[:, :], a["L0_ffn_router_w2"]).then_inc(S["small_loaded"], 16)
            sp.dma_start(router_b2[:, :], a["L0_ffn_router_b2"].rearrange("(o e) -> o e", o=1)).then_inc(S["small_loaded"], 16)
            sp.dma_start(b3[:, :], a["L0_ffn_expert_b3"]).then_inc(S["small_loaded"], 16)
            with nc.allow_non_contiguous_dma(reason="biases and head weights with the feature on the partition, once"):
                for bias, name in ((b1, "L0_ffn_expert_b1"), (b2, "L0_ffn_expert_b2")):
                    for h in range(HALVES):
                        sp.dma_start(bias[:, :, h], a[name][:, h * P:(h + 1) * P].rearrange("e p -> p e")).then_inc(S["small_loaded"], 16)
                for t, name in ((k_col_w, "kln_weight"), (k_col_b, "kln_bias")):
                    for h in range(HALVES):
                        rows = a["L0_mix_" + name].rearrange("g o c -> (g o c)")[h * P:(h + 1) * P]
                        sp.dma_start(t[:, h:h + 1], rows.rearrange("(p o) -> p o", o=1)).then_inc(S["ln_loaded"], 16)
            for t, name in ((v_row_w, "vln_weight"), (v_row_b, "vln_bias")):
                sp.dma_start(t.rearrange("p h n -> p (h n)"),
                             a["L0_mix_" + name].rearrange("g o c -> (g o c)").partition_broadcast(P)).then_inc(S["ln_loaded"], 16)

            with sp.Fori(0, PAIRS) as i:
                for s in range(2):
                    sp.wait_ge(S["y_ready"], 2 * i + s + 1)
                    sp.dma_start(y_table[bass.ds((2 * i + s) * P, P), :], y_out[:, s, :]).then_inc(y_stored[s], 16)
            sp.wait_ge(S["y_ready"], BLOCKS)
            sp.dma_start(y_table[FULL * P:BLOCKS * P, :], y_out[:, 0, :]).then_inc(y_stored[0], 16)

            sp.wait_ge(S["mix_done"], 1 + BLOCKS)
            for w, name in ((w1, "L0_ffn_expert_w1"), (w2, "L0_ffn_expert_w2"), (w3, "L0_ffn_expert_w3")):
                for e in range(EXPERTS):
                    sp.dma_start(w[:, e, :, :], a[name][e].rearrange("(h p) n -> p h n", p=P)).then_inc(S["weights_loaded"], 16)

            def store_all(first):
                with sp.Fori(0, FULL) as b:
                    sp.wait_ge(S["ey_added"], 1 + EXPERTS * (first + b + 1))
                    sp.dma_start(out[bass.ds(b * P, P), :], y_acc).then_inc(S["row_stored"], 16)
                sp.wait_ge(S["ey_added"], 1 + EXPERTS * (first + BLOCKS))
                sp.dma_start(out[FULL * P:NODES, :], y_acc[0:LAST_ROWS, :]).then_inc(S["row_stored"], 16)
                sp.wait_ge(S["row_stored"], 1 + 16 * (first + BLOCKS))

            store_all(0)
            with sp.If(sp.value_load(late_flag[:, :], min_val=0, max_val=1)):
                store_all(BLOCKS)

        @block.gpsimd
        def _(pool):
            nc.gpsimd.memset(base[:, FULL, :], 0.0).then_inc(S["x_zeroed"], 1)
            nc.gpsimd.iota(row_no[:, :], pattern=[[0, 1]], base=0, channel_multiplier=1).then_inc(S["consts"], 1)
            nc.gpsimd.iota(bound[:, :], pattern=[[1, BLOCKS + 1]], base=0, channel_multiplier=0).then_inc(S["consts"], 1)
            nc.gpsimd.memset(ident[:, :], 0.0).then_inc(S["pool_step"], 1)
            nc.gpsimd.memset(same_head[:, :], 0.0).then_inc(S["pool_step"], 1)
            nc.gpsimd.memset(upto[:, :], 1.0).then_inc(S["pool_step"], 1)
            nc.gpsimd.memset(last_block[:, :], 0.0).then_inc(S["pool_step"], 1)
            nc.gpsimd.iota(step_limit[:, :], pattern=[[0, 1]], base=STEPS_PER_BLOCK + NORM_AT + 1, channel_multiplier=STEPS_PER_BLOCK,
                           allow_small_or_imprecise_dtypes=True).then_inc(S["pool_step"], 1)
            nc.gpsimd.memset(dst_ahead[:, STEPS:TABLE].bitcast(F32), 0.0).then_inc(S["consts"], 1)
            nc.gpsimd.memset(rel_ahead[:, STEPS:TABLE], 0.0).then_inc(S["consts"], 1)
            nc.gpsimd.memset(ln_eps[:, :], LN_EPS).then_inc(S["consts"], 1)
            nc.gpsimd.memset(ones[:, :], 1.0).then_inc(S["consts"], 1)
            nc.gpsimd.memset(neg_block[:, :], -float(P)).then_inc(S["consts"], 1)
            nc.gpsimd.memset(acc_w[:, :], float(ROW)).then_inc(S["consts"], 1)
            nc.gpsimd.memset(probs[:, :], -1.0).then_inc(S["consts"], 1)
            nc.gpsimd.memset(minus_half[:, :], -0.5).then_inc(S["consts"], 1)
            nc.gpsimd.memset(half_power[:, :], 0.5).then_inc(S["consts"], 1)
            nc.gpsimd.memset(minus_one[:, :], -1.0).then_inc(S["consts"], 1)
            nc.gpsimd.memset(over_count[:, :], 1.0 / (HEAD_DIM - 1)).then_inc(S["consts"], 1)
            nc.gpsimd.memset(head_eps[:, :], HEAD_EPS).then_inc(S["consts"], 1)
            nc.gpsimd.iota(lane[:, :], pattern=[[1, P]], base=0, channel_multiplier=0,
                           allow_small_or_imprecise_dtypes=True).then_inc(S["consts"], 1)
            nc.gpsimd.iota(edge_no[:, :], pattern=[[P, STEP_TILES]], base=0, channel_multiplier=1,
                           allow_small_or_imprecise_dtypes=True).then_inc(S["consts"], 1)
            nc.gpsimd.iota(step_no, pattern=[[1, STEPS]], base=0, channel_multiplier=0,
                           allow_small_or_imprecise_dtypes=True).then_inc(S["consts"], 1)
            pool.wait_ge(S["pool_step"], 5)
            nc.gpsimd.affine_select(out=ident[:, :], in_=ident[:, :], compare_op=ALU.not_equal, fill=1.0, base=0,
                                    pattern=[[-1, P]], channel_multiplier=1).then_inc(S["consts"], 1)
            nc.gpsimd.affine_select(out=upto[:, :], in_=upto[:, :], compare_op=ALU.is_ge, fill=0.0, base=0,
                                    pattern=[[1, BLOCKS]], channel_multiplier=-1).then_inc(S["consts"], 1)
            nc.gpsimd.affine_select(out=last_block[:, :], in_=last_block[:, :], compare_op=ALU.not_equal, fill=1.0,
                                    base=-(BLOCKS - 1), pattern=[[0, 1]], channel_multiplier=1).then_inc(S["pool_step"], 1)
            nc.gpsimd.affine_select(out=step_limit[:, :], in_=step_limit[:, :], compare_op=ALU.not_equal, fill=float(2 * STEPS),
                                    base=-(BLOCKS - 1), pattern=[[0, 1]], channel_multiplier=1).then_inc(S["pool_step"], 1)
            pool.wait_ge(S["consts"], N_CONSTS - 1)
            pool.wait_ge(S["pool_step"], 7)
            for h in range(P // HEAD_DIM):
                part = slice(h * HEAD_DIM, (h + 1) * HEAD_DIM)
                nc.gpsimd.memset(same_head[part, part], 1.0).then_inc(S["pool_step"], 1)
            n = 7 + P // HEAD_DIM
            pool.wait_ge(S["pool_step"], n)
            nc.gpsimd.tensor_scalar(centre[:, :], same_head[:, :], -1.0 / HEAD_DIM, None, ALU.mult).then_inc(S["pool_step"], 1)
            pool.wait_ge(S["pool_step"], n + 1)
            nc.gpsimd.tensor_tensor(centre[:, :], centre[:, :], ident[:, :], ALU.add).then_inc(S["consts"], 1)
            pool.nop().then_inc(S["zed_ready"], 1)

            pool.wait_ge(S["x_stats_ready"], BLOCKS)
            nc.gpsimd.tensor_scalar(x_bias, x_mean_var[:, :, 1], LN_EPS, None, ALU.add).then_inc(S["pool_step"], 1)
            pool.wait_ge(S["pool_step"], n + 2)
            nc.gpsimd.tensor_tensor(x_rstd, x_bias, minus_half[:, :], ALU.pow).then_inc(S["pool_step"], 1)
            pool.wait_ge(S["pool_step"], n + 3)
            nc.gpsimd.tensor_tensor(x_bias, x_mean_var[:, :, 0], x_rstd, ALU.mult).then_inc(S["pool_step"], 1)
            pool.wait_ge(S["pool_step"], n + 4)
            nc.gpsimd.tensor_scalar(x_bias, x_bias, -1.0, None, ALU.mult).then_inc(S["x_norm"], 1)
            n += 4

            def spread(u, tiles, first):
                links = first + SPREAD_LINKS * u
                by_head = [v[:, 0:tiles, :].rearrange("p s (h c) -> p (s h) c", c=HEAD_DIM) for v in (dev, dev2, zed)]
                heads = tiles * HEADS
                pool.wait_ge(S["dev_ready"], u + 1)
                nc.gpsimd.tensor_tensor(by_head[1], by_head[0], by_head[0], ALU.mult).then_inc(S["pool_step"], 1)
                links += 1
                pool.wait_ge(S["pool_step"], links)
                width = HEAD_DIM // 2
                while width:
                    pair = (by_head[1][:, :, 0:width], by_head[1][:, :, width:2 * width])
                    to = pair[0] if width > 1 else dev_sum[:, 0:heads].unsqueeze(2)
                    nc.gpsimd.tensor_tensor(to, pair[0], pair[1], ALU.add).then_inc(S["pool_step"], 1)
                    links, width = links + 1, width // 2
                    pool.wait_ge(S["pool_step"], links)
                steps = ((dev_r, dev_sum, over_count, ALU.mult), (dev_sum, dev_r, half_power, ALU.pow),
                         (dev_r, dev_sum, head_eps, ALU.add), (dev_std, dev_r, minus_one, ALU.pow))
                for to, of, by, op in steps:
                    nc.gpsimd.tensor_tensor(to[:, 0:heads], of[:, 0:heads], by[:, 0:heads], op).then_inc(S["pool_step"], 1)
                    links += 1
                    pool.wait_ge(S["pool_step"], links)
                pool.wait_ge(S["z_summed"], u + 1)
                nc.gpsimd.tensor_tensor(by_head[2], by_head[0], dev_std[:, 0:heads].unsqueeze(2).broadcast_to([P, heads, HEAD_DIM]),
                                        ALU.mult).then_inc(S["zed_ready"], 1)

            with nc.gpsimd.Fori(0, PAIRS) as u:
                spread(u, 2, n)
            spread(PAIRS, 1, n)
            n += SPREAD_LINKS * (PAIRS + 1)

            pool.wait_ge(S["gate_ready"], 1)
            nc.gpsimd.tensor_tensor(y_scale, x_rstd, gate, ALU.mult).then_inc(S["y_params"], 1)
            nc.gpsimd.tensor_tensor(y_bias, x_bias, gate, ALU.mult).then_inc(S["y_params"], 1)

            pool.wait_ge(S["ln_loaded"], 16 * N_MIX_LOADS)
            pool.wait_ge(S["z_copied"], 2)
            for h in range(HALVES):
                last = nc.gpsimd.tensor_scalar(diag_sum[:, h, :], ident[:, :], z_sum[:, h:h + 1], None, ALU.mult)
                last.then_inc(S["diag_ready"], 1)
            nc.gpsimd.tensor_tensor(kw_sum, k_col_w, z_sum, ALU.mult).then_inc(S["pool_step"], 1)
            nc.gpsimd.tensor_tensor(kv_a, kv_a, v_row_w, ALU.mult).then_inc(S["pool_step"], 1)
            nc.gpsimd.tensor_scalar(kv_b, v_row_b, float(NODES), None, ALU.mult).then_inc(S["pool_step"], 1)
            pool.wait_ge(S["z_row_ready"], 1)
            nc.gpsimd.tensor_tensor(z_row, z_row, v_row_w, ALU.mult).then_inc(S["pool_step"], 1)
            pool.wait_ge(S["pool_step"], n + 4)
            nc.gpsimd.tensor_tensor(kv_b, kv_b, z_row, ALU.add).then_inc(S["pool_step"], 1)
            pool.wait_ge(S["pool_step"], n + 5)
            for h in range(HALVES):
                nc.gpsimd.tensor_scalar(kv_a[:, h, :], kv_a[:, h, :], k_col_w[:, h:h + 1], None, ALU.mult).then_inc(S["pool_step"], 1)
                nc.gpsimd.tensor_scalar(kv_b[:, h, :], kv_b[:, h, :], k_col_b[:, h:h + 1], None, ALU.mult).then_inc(S["pool_step"], 1)
                nc.gpsimd.tensor_scalar(z_row[:, h, :], v_row_b[:, h, :], kw_sum[:, h:h + 1], None, ALU.mult).then_inc(S["pool_step"], 1)
            pool.wait_ge(S["pool_step"], n + 5 + 3 * HALVES)
            nc.gpsimd.tensor_tensor(kv_a, kv_a, kv_b, ALU.add).then_inc(S["pool_step"], 1)
            pool.wait_ge(S["pool_step"], n + 6 + 3 * HALVES)
            nc.gpsimd.tensor_tensor(kv_a, kv_a, z_row, ALU.add).then_inc(S["pool_step"], 1)
            pool.wait_ge(S["pool_step"], n + 7 + 3 * HALVES)
            nc.gpsimd.tensor_tensor(kv_a, kv_a, same_head[:, :].unsqueeze(1).broadcast_to([P, HALVES, P]),
                                    ALU.mult).then_inc(S["pool_step"], 1)
            pool.wait_ge(S["pool_step"], n + 8 + 3 * HALVES)
            nc.gpsimd.tensor_scalar(kv_a, kv_a, 1.0 / NODES, None, ALU.mult).then_inc(S["pool_step"], 1)
            pool.wait_ge(S["pool_step"], n + 9 + 3 * HALVES)
            nc.gpsimd.tensor_tensor(kv[:, :, :], kv_a, ident[:, :].unsqueeze(1).broadcast_to([P, HALVES, P]),
                                    ALU.add).then_inc(S["kv_final"], 1)

            pool.wait_ge(y_stored[0], 1 + 16 * (PAIRS + 1))
            pool.wait_ge(y_stored[1], 1 + 16 * PAIRS)
            pool.wait_ge(S["mix_done"], 1 + BLOCKS)
            pool.wait_ge(S["below_ready"], 4)
            nc.gpsimd.memset(acc_mem[:, :], 0.0).then_inc(S["acc_zeroed"], 1)

            with nc.gpsimd.Fori(0, BLOCKS) as i:
                for g in range(GROUPS_PER_BLOCK):
                    pool.wait_ge(S["idx_staged"], GROUPS_PER_BLOCK * i + g + 1)
                    for start, end in RUNS:
                        pool.wait_ge(S["sum_ps"], STEPS_PER_BLOCK * i + g * GROUP + end + STEPS_PER_BLOCK - GROUP)
                        pool.nop().then_inc(S["slot_free"], 1)
                        for slot in range(start, end):
                            j = g * GROUP + slot
                            nc.gpsimd.indirect_dma_start(
                                out=gathered[:, slot, :], out_offset=None, in_=y_table,
                                in_offset=bass.IndirectOffsetOnAxis(ap=step_idx[:, j:j + 1], axis=0)).then_inc(rows_in[slot], 16)

        @block.scalar
        def _(act):
            act.nop().then_inc(S["mix_done"], 1)
            for s in range(2):
                act.nop().then_inc(y_stored[s], 1)
            act.nop().then_inc(S["h1_ready"], HALVES)
            act.nop().then_inc(S["h2_ready"], HALVES)
            act.wait_ge(S["small_loaded"], 16 * N_SMALL)
            act.wait_ge(S["x_loaded"], 32)
            act.wait_ge(S["x_norm"], 1)

            def norm(u, tiles):
                act.wait_ge(S["xT_ps"], u)
                for s in range(tiles):
                    act.wait_ge(S["x_norm"], 1)
                    nc.scalar.activation(xs[:, s, :], base[:, 2 * u + s, :], ACT.Identity, bias=x_bias[:, bass.ds(2 * u + s, 1)],
                                         scale=x_rstd[:, bass.ds(2 * u + s, 1)]).then_inc(S["xs_ready"], 1)

            def keep_turned(u, tiles):
                act.wait_ge(S["xT_ps"], u + 1)
                act.wait_ge(S["dev_ps"], u)
                act.wait_ge(S["xT_filed"], u)
                nc.scalar.activation(xsT[:, :, 0:tiles * P], ps_xT[:, :, 0:tiles * P], ACT.Copy).then_inc(S["xT_ready"], 1)

            def hidden(u, tiles):
                act.wait_ge(S["hid_ps"], u + 1)
                act.wait_ge(S["logit_ps"], u + 1)
                nc.scalar.activation(hid[:, 0:tiles * P], ps_hid[:, 0:tiles * P], ACT.Relu, bias=gnn_b1[:, 0:1]).then_inc(S["hid_ready"], 1)
                act.wait_ge(S["dev_ps"], u + 1)
                act.wait_ge(S["zed_ready"], u + 1)
                nc.scalar.activation(dev[:, 0:tiles, :], ps_dev[:, 0:tiles, :], ACT.Copy).then_inc(S["dev_ready"], 1)

            def file_turned(u, tiles):
                act.wait_ge(S["xT_ready"], u + 1)
                act.wait_ge(S["x_norm"], 1)
                nc.scalar.activation(xnT[:, :, bass.ds(2 * P * u, tiles * P)], xsT[:, :, 0:tiles * P], ACT.Copy).then_inc(S["xT_filed"], 1)

            norm(0, 2)
            keep_turned(0, 2)
            norm(1, 2)
            file_turned(0, 2)
            with nc.scalar.Fori(0, PAIRS - 2) as u:
                hidden(u, 2)
                keep_turned(u + 1, 2)
                norm(u + 2, 2)
                file_turned(u + 1, 2)
            for u in range(PAIRS - 2, PAIRS):
                tiles = 2 if u + 1 < PAIRS else 1
                hidden(u, 2)
                keep_turned(u + 1, tiles)
                if u + 2 <= PAIRS:
                    norm(u + 2, 1)
                file_turned(u + 1, tiles)
            hidden(PAIRS, 1)

            act.wait_ge(S["z_summed"], 1 + PAIRS + 1)
            nc.scalar.activation(kv_a, ps_z[:, :, 0:P], ACT.Copy).then_inc(S["z_copied"], 1)
            nc.scalar.activation(z_sum, ps_z[:, :, P], ACT.Copy).then_inc(S["z_copied"], 1)
            act.wait_ge(S["logit_ps"], 1 + PAIRS + 1)
            nc.scalar.activation(gate, ps_logit, ACT.Sigmoid, bias=gnn_b2[:, 0:1]).then_inc(S["gate_ready"], 1)
            act.wait_ge(S["z_row_ps"], HALVES)
            nc.scalar.activation(z_row, ps_z_row, ACT.Copy).then_inc(S["z_row_ready"], 1)

            def gated(t, s, pair):
                act.wait_ge(y_stored[s], 1 + 16 * pair)
                act.wait_ge(S["y_params"], 2)
                nc.scalar.activation(y_out[:, s, 0:DIM], base[:, t, :], ACT.Identity, bias=y_bias[:, bass.ds(t, 1)],
                                     scale=y_scale[:, bass.ds(t, 1)])
                nc.scalar.activation(y_out[:, s, DIM:ROW], gate[:, bass.ds(t, 1)], ACT.Copy).then_inc(S["y_ready"], 1)

            act.wait_ge(S["gate_ready"], 1)
            with nc.scalar.Fori(0, PAIRS) as i:
                for s in range(2):
                    gated(2 * i + s, s, i)
            gated(FULL, 0, PAIRS)

            def copy_upper(level, bit):
                into = keys[exchanges_before(level, bit) % 2]
                d = distance(bit)
                for half in range(2):
                    act.wait_ge(half_turned[half], turns_before(level, bit))
                    if d == HALF:
                        if half == 1:
                            nc.scalar.activation(half_view(into, 1), half_view(turned, 1), ACT.Copy).then_inc(upper_copied[1], 1)
                        else:
                            act.nop().then_inc(upper_copied[0], 1)
                        continue
                    pairs_in, pairs_out = (half_view(t, half).rearrange("p (g t d) -> p g t d", t=2, d=d) for t in (turned, into))
                    nc.scalar.activation(pairs_out[:, :, 1, :], pairs_in[:, :, 1, :], ACT.Copy).then_inc(upper_copied[half], 1)

            for level in range(TURNED + 1, LEVELS + 1):
                copy_upper(level, level - 1)
                copy_upper(level, TURNED - 1)
                first = (level - MIX_LEVEL) * TILES_PER_LEVEL
                if 0 <= first < BLOCKS:
                    act.wait_ge(S["kv_final"], 1)
                    with nc.scalar.Fori(first, first + TILES_PER_LEVEL) as t:
                        act.wait_ge(S["mix_ps"], t + 1)
                        act.wait_ge(S["kv_final"], 1)
                        nc.scalar.activation(mixT, xnT[:, :, bass.ds(t * P, P)], ACT.Copy).then_inc(S["mix_staged"], 1)
                        act.wait_ge(S["mix_ps"], 1 + t + 1)
                        act.wait_ge(S["kv_final"], 1)
                        nc.scalar.activation(base[:, t, :], ps_mix, ACT.Copy).then_inc(S["mix_done"], 1)

            for n, t in enumerate((dst_of_edge, src_of_edge)):
                act.wait_ge(S["fields_ready"], n + 1)
                nc.scalar.activation(t, t.bitcast(I32), ACT.Copy).then_inc(S["edges_ready"], 1)
            act.wait_ge(S["steps_ps"], 2)
            act.wait_ge(S["chunk_ready"], 1)
            nc.scalar.activation(step_acc, front[0:1, 0:STEPS], ACT.Copy).then_inc(S["acc_row_ready"], 1)
            act.wait_ge(S["picked_ps"], 1)
            nc.scalar.activation(step_rel, front[:, 0:STEPS], ACT.Copy).then_inc(S["tables_ready"], 1)

            def stage(i, g):
                at = slice(g * GROUP, (g + 1) * GROUP)
                act.wait_ge(S["sum_ps"], STEPS_PER_BLOCK * i + GROUP * (g + 1))
                act.wait_ge(S["tables_ready"], 3)
                nc.scalar.activation(step_idx[:, at], dst_ahead[:, bass.ds(STEPS_PER_BLOCK * i + GROUP * g, GROUP)],
                                     ACT.Copy).then_inc(S["idx_staged"], 1)

            def relu(m, slot, ps_done, ps, sb_t, bias, ready):
                act.wait_ge(ps_done, m + 1)
                for h in range(HALVES):
                    nc.scalar.activation(sb_t[:, slot % 2, h, :], ps[:, h, :], ACT.Relu, bias=bias[:, slot, h:h + 1]).then_inc(ready, 1)

            def act_round(i, n, steps, experts, lead):
                for j in range(STEPS_PER_BLOCK):
                    if steps and j == 2:
                        stage(i, 2)
                    if steps and j in (13, 24):
                        stage(i + 1, j // GROUP - 1)
                    if experts and j == GATES_AT:
                        act.wait_ge(S["gatesT_ps"], n + 1)
                        nc.scalar.activation(gates_T, ps_gates_T, ACT.Copy).then_inc(S["gatesT_ready"], 1)
                    if experts and j in FIRST_AT:
                        e = FIRST_AT.index(j)
                        relu(EXPERTS * n + e, e, S["h1_ps"], ps_h1, h1_T, b1, S["h1_ready"])
                    if experts and j in SECOND_AT:
                        e = SECOND_AT.index(j)
                        relu(EXPERTS * n + e, e, S["h2_ps"], ps_h2, h2_T, b2, S["h2_ready"])
                    if lead and j == ROOT_AT:
                        act.wait_ge(S["x2_var"], n + 2)
                        nc.scalar.activation(rstd[:, 1:2], mean_var[:, 1:2], ACT.Sqrt, bias=ln_eps[:, 0:1]).then_inc(S["x2_std"], 1)
                    if lead and j == TURN_AT:
                        act.wait_ge(S["x2T_ps"], n + 2)
                        nc.scalar.activation(next_T, ps_x2T, ACT.Copy).then_inc(S["x2T_ready"], 1)
                    if lead and j == ROUTER_AT:
                        act.wait_ge(S["router_ps"], n + 2)
                        nc.scalar.activation(router_hid, ps_router, ACT.Relu, bias=router_b1[:, 0:1]).then_inc(S["router_ready"], 1)
                    if lead and j == PEAK_AT:
                        act.wait_ge(S["logit_max_ready"], n + 2)
                        nc.scalar.activation(exp_l[:, :], ps_l, ACT.Exp, bias=logit_max[:, 0:1],
                                             accum_out=exp_sum[:, 0:1]).then_inc(S["exp_ready"], 1)
                    if lead and j == MOVE_AT:
                        act.wait_ge(S["x2T_ready"], n + 2)
                        nc.scalar.activation(this_T, next_T, ACT.Copy).then_inc(S["this_ready"], 1)
                    if lead and j == TOP_AT:
                        act.wait_ge(S["top_diff_ready"], n + 2)
                        nc.scalar.activation(top_w[:, 1:2], top_w[:, 0:1], ACT.Exp).then_inc(S["top_exp_ready"], 1)

            act.wait_ge(S["tables_ready"], 3)
            stage(0, 0)
            stage(0, 1)
            act_round(0, -2, True, False, False)
            act_round(1, -1, True, False, True)
            with nc.scalar.Fori(2, BLOCKS) as i:
                act_round(i, i - 2, True, True, True)
            act_round(None, BLOCKS - 2, False, True, True)
            act_round(None, BLOCKS - 1, False, True, False)
            with nc.scalar.If(act.value_load(late_flag[:, :], min_val=0, max_val=1)):
                act_round(None, BLOCKS - 1, False, False, True)
                with nc.scalar.Fori(0, FULL) as b:
                    act_round(None, b + BLOCKS, False, True, True)
                act_round(None, 2 * BLOCKS - 1, False, True, False)

        @block.tensor
        def _(pe):
            pe.nop().then_inc(S["logit_ps"], 1)
            pe.nop().then_inc(S["z_summed"], 1)
            pe.nop().then_inc(S["mix_ps"], 1)
            pe.nop().then_inc(S["sum_ps"], STEPS_PER_BLOCK)
            pe.wait_ge(S["consts"], N_CONSTS)
            pe.wait_ge(S["small_loaded"], 16 * N_SMALL)
            pe.wait_ge(S["z_zeroed"], 1)

            def turn_rows(u, tiles):
                pe.wait_ge(S["xs_ready"], 2 * u + tiles)
                pe.wait_ge(S["xT_ready"], u)
                for s in range(tiles):
                    for h in range(HALVES):
                        last = nc.tensor.transpose(ps_xT[:, h, s * P:(s + 1) * P], xs[:, s, h * P:(h + 1) * P], ident[:, :])
                last.then_inc(S["xT_ps"], 1)

            def hidden(u, tiles):
                pe.wait_ge(S["xT_ready"], u + 1)
                pe.wait_ge(S["hid_ready"], u)
                for h in range(HALVES):
                    last = nc.tensor.matmul(ps_hid[:, 0:tiles * P], gnn_w1[:, h, :], xsT[:, h, 0:tiles * P], start=(h == 0), stop=(h == 1))
                last.then_inc(S["hid_ps"], 1)
                pe.wait_ge(S["dev_ready"], u)
                for s in range(tiles):
                    for h in range(HALVES):
                        last = nc.tensor.matmul(ps_dev[:, s, h * P:(h + 1) * P], xsT[:, h, s * P:(s + 1) * P], centre[:, :],
                                                start=True, stop=True)
                last.then_inc(S["dev_ps"], 1)

            def logit(u, tiles):
                pe.wait_ge(S["hid_ready"], u + 1)
                for s in range(tiles):
                    last = nc.tensor.matmul(ps_logit[:, bass.ds(2 * u + s, 1)], hid[:, s * P:(s + 1) * P], gnn_w2[:, :], start=True,
                                            stop=True)
                last.then_inc(S["logit_ps"], 1)

            def sum_z(u, tiles):
                pe.wait_ge(S["zed_ready"], 1 + u + 1)
                for s in range(tiles):
                    for h in range(HALVES):
                        part = zed[:, s, h * P:(h + 1) * P]
                        nc.tensor.matmul(ps_z[:, h, 0:P], part, part, start=False, stop=False, skip_group_check=True)
                        last = nc.tensor.matmul(ps_z[:, h, P:P + 1], part, ones[:, 0:1], start=False, stop=False, skip_group_check=True)
                last.then_inc(S["z_summed"], 1)

            turn_rows(0, 2)
            turn_rows(1, 2)
            hidden(0, 2)
            logit(0, 2)
            with nc.tensor.Fori(1, PAIRS - 1) as u:
                turn_rows(u + 1, 2)
                hidden(u, 2)
                sum_z(u - 1, 2)
                logit(u, 2)
            turn_rows(PAIRS, 1)
            hidden(PAIRS - 1, 2)
            sum_z(PAIRS - 2, 2)
            logit(PAIRS - 1, 2)
            hidden(PAIRS, 1)
            sum_z(PAIRS - 1, 2)
            logit(PAIRS, 1)
            sum_z(PAIRS, 1)
            pe.wait_ge(S["diag_ready"], HALVES)
            for h in range(HALVES):
                nc.tensor.matmul(ps_z_row[:, h, :], ones[:, :], diag_sum[:, h, :], start=True, stop=True).then_inc(S["z_row_ps"], 1)

            def turn(level, bit):
                held = keys[exchanges_before(level, bit) % 2]
                for half in range(2):
                    pe.wait_ge(sorted_half[half], instructions_before(level, bit))
                    for at in range(half * HALF, (half + 1) * HALF, P):
                        last = nc.tensor.transpose(turned[:, at:at + P], held[:, at:at + P], ident[:, :])
                    last.then_inc(half_turned[half], 1)

            for level in range(TURNED + 1, LEVELS + 1):
                turn(level, level - 1)
                turn(level, TURNED - 1)
                first = (level - MIX_LEVEL) * TILES_PER_LEVEL
                if 0 <= first < BLOCKS:
                    pe.wait_ge(S["kv_final"], 1)
                    pe.wait_ge(S["dev_ready"], PAIRS + 1)
                    with nc.tensor.Fori(first, first + TILES_PER_LEVEL) as t:
                        pe.wait_ge(S["mix_staged"], t + 1)
                        pe.wait_ge(S["mix_done"], t + 1)
                        nc.tensor.matmul(ps_mix, ident[:, :], base[:, t, :], start=True, stop=False)
                        for h in range(HALVES):
                            last = nc.tensor.matmul(ps_mix[:, h * P:(h + 1) * P], mixT[:, h, :], kv[:, h, :],
                                                    start=False, stop=(h == 1))
                        last.then_inc(S["mix_ps"], 1)

            pe.wait_ge(S["below_ready"], 4)
            for n, (which, at) in enumerate(((0, 0), (0, 1), (1, 1))):
                last = nc.tensor.matmul(ps_counts[:, n:n + 1], below[:, which, at:at + BLOCKS], ones[:, 0:1], start=True, stop=True)
            last.then_inc(S["counts_ps"], 1)
            pe.wait_ge(S["counts_ready"], 2)
            nc.tensor.matmul(ps_end, upto[:, :], counts[:, 4:5], start=True, stop=True).then_inc(S["ends_ps"], 1)
            pe.wait_ge(S["past_ready"], 2)
            pe.wait_ge(S["mix_done"], 1 + BLOCKS)
            for ps, w in ((turned, chunk_w), (front, acc_w)):
                for at in range(0, STEPS, BANK):
                    to = min(at + BANK, STEPS)
                    last = nc.tensor.matmul(ps[:, at:to], w[:, :], past_block[:, at:to], start=True, stop=True)
                last.then_inc(S["steps_ps"], 1)
            pe.wait_ge(S["edges_ready"], 2)
            pe.wait_ge(S["chunk_ready"], 1)
            pe.wait_ge(S["acc_row_ready"], 1)
            picks = 0
            for tile in range(STEP_TILES):
                at, to = tile * P, min(tile * P + P, STEPS)
                sources = [c for c in (tile - 1, tile) if c >= 0]
                for c in sources:
                    chosen = pick[:, picks % PICKS, 0:to - at]
                    picks += 1
                    pe.wait_ge(S["pick_ready"], picks)
                    nc.tensor.matmul(turned[:, at:to], dst_of_edge[:, c * P:c * P + P], chosen, start=(c == sources[0]), stop=(c == tile))
                    nc.tensor.matmul(front[:, at:to], src_of_edge[:, c * P:c * P + P], chosen, start=(c == sources[0]),
                                     stop=False).then_inc(S["pick_used"], 1)
                nc.tensor.matmul(front[:, at:to], neg_block[:, :], past_block[:, at:to], start=False, stop=True)
            pe.wait_ge(S["counts_ready"], 6)
            nc.tensor.matmul(ps_late, late_block[:, :], ones[0:BLOCKS, 0:1], start=True, stop=True).then_inc(S["picked_ps"], 1)

            def step(i, j):
                slot, group = j % GROUP, j // GROUP
                for start, end in RUNS:
                    if slot == start:
                        pe.wait_ge(S["onehot_ready"], STEPS_PER_BLOCK * i + group * GROUP + end)
                pe.wait_ge(S["sum_added"], STEPS_PER_BLOCK * i + j + 1)
                pe.wait_ge(rows_in[slot], 16 * (GROUPS_PER_BLOCK * i + group + 1))
                nc.tensor.matmul(ps_sum[j % SUM_BANKS], onehot[:, j, :], gathered[:, slot, :], start=True,
                                 stop=True).then_inc(S["sum_ps"], 1)

            def first_layer(n, e):
                m = EXPERTS * n + e
                pe.wait_ge(S["h1_ready"], HALVES * m + HALVES)
                if e == 0:
                    pe.wait_ge(S["this_ready"], n + 1)
                for o in range(HALVES):
                    for h in range(HALVES):
                        last = nc.tensor.matmul(ps_h1[:, o, :], w1[:, e, h, o * P:(o + 1) * P], this_T[:, h, :],
                                                start=(h == 0), stop=(h == 1))
                last.then_inc(S["h1_ps"], 1)

            def second_layer(m, e):
                pe.wait_ge(S["h2_ready"], HALVES * m + HALVES)
                pe.wait_ge(S["h1_ready"], HALVES * m + 2 * HALVES)
                for o in range(HALVES):
                    for h in range(HALVES):
                        last = nc.tensor.matmul(ps_h2[:, o, :], w2[:, e, h, o * P:(o + 1) * P], h1_T[:, e % 2, h, :],
                                                start=(h == 0), stop=(h == 1))
                last.then_inc(S["h2_ps"], 1)

            def third_layer(m, e):
                pe.wait_ge(S["ey_added"], m + 1)
                pe.wait_ge(S["h2_ready"], HALVES * m + 2 * HALVES)
                for h in range(HALVES):
                    last = nc.tensor.matmul(ps_y, h2_T[:, e % 2, h, :], w3[:, e, h, :], start=(h == 0), stop=(h == 1))
                last.then_inc(S["ey_ps"], 1)

            def pe_round(i, n, steps, experts, lead):
                for j in range(STEPS_PER_BLOCK):
                    if steps:
                        step(i, j)
                    if experts and j == GATES_AT:
                        pe.wait_ge(S["gates_ready"], n + 1)
                        nc.tensor.transpose(ps_gates_T, gates[:, :], ident[:, :]).then_inc(S["gatesT_ps"], 1)
                    if experts and j == BIAS_AT:
                        pe.wait_ge(S["gatesT_ready"], n + 1)
                        nc.tensor.matmul(ps_b3, gates_T, b3[:, :], start=True, stop=True).then_inc(S["b3_ps"], 1)
                    if experts and j in FIRST_AT:
                        first_layer(n, FIRST_AT.index(j))
                    if experts and j in SECOND_AT:
                        second_layer(EXPERTS * n + SECOND_AT.index(j), SECOND_AT.index(j))
                    if experts and j in THIRD_AT:
                        third_layer(EXPERTS * n + THIRD_AT.index(j), THIRD_AT.index(j))
                    if lead and j == TURN_AT:
                        pe.wait_ge(S["x2_norm"], n + 2)
                        pe.wait_ge(S["y_begun"], n + 1)
                        for h in range(HALVES):
                            last = nc.tensor.transpose(ps_x2T[:, h, :], xn2[:, h * P:(h + 1) * P], ident[:, :])
                        last.then_inc(S["x2T_ps"], 1)
                    if lead and j == ROUTER_AT:
                        pe.wait_ge(S["x2T_ready"], n + 2)
                        for h in range(HALVES):
                            last = nc.tensor.matmul(ps_router, router_w1[:, h, :], next_T[:, h, :], start=(h == 0), stop=(h == 1))
                        last.then_inc(S["router_ps"], 1)
                    if lead and j == LOGITS_AT:
                        pe.wait_ge(S["router_ready"], n + 2)
                        nc.tensor.matmul(ps_l, router_hid, router_w2[:, :], start=True, stop=False)
                        nc.tensor.matmul(ps_l, ones[0:1, :], router_b2[:, :], start=False, stop=True).then_inc(S["logits_ps"], 1)

            pe.wait_ge(S["tables_ready"], 3)
            pe_round(0, -2, True, False, False)
            pe_round(1, -1, True, False, True)
            pe.wait_ge(S["weights_loaded"], 16 * 3 * EXPERTS)
            with nc.tensor.Fori(2, BLOCKS) as i:
                pe_round(i, i - 2, True, True, True)
            pe_round(None, BLOCKS - 2, False, True, True)
            pe_round(None, BLOCKS - 1, False, True, False)
            with nc.tensor.If(pe.value_load(late_flag[:, :], min_val=0, max_val=1)):
                pe_round(None, BLOCKS - 1, False, False, True)
                with nc.tensor.Fori(0, FULL) as b:
                    pe_round(None, b + BLOCKS, False, True, True)
                pe_round(None, 2 * BLOCKS - 1, False, True, False)

        @block.vector
        def _(dve):
            dve.nop().then_inc(S["sum_added"], SUM_BANKS)
            dve.nop().then_inc(S["ey_added"], 1)
            dve.nop().then_inc(S["row_stored"], 1)
            nc.vector.memset(bank(3), 0.0).then_inc(S["z_zeroed"], 1)
            nc.vector.memset(keys[1], PAD_KEY).then_inc(S["key_step"], 1)
            dve.wait_ge(S["consts"], 2)
            nc.vector.tensor_scalar(row_odd[:, :], row_no[:, :], 1, None, ALU.bitwise_and).then_inc(S["key_step"], 1)
            nc.vector.tensor_scalar(bound[:, :], bound[:, :], BLOCK_SHIFT, KEY_BASE, ALU.logical_shift_left,
                                    ALU.bitwise_or).then_inc(S["key_step"], 1)
            dve.wait_ge(S["key_step"], 3)
            nc.vector.tensor_scalar(sign[:, 0:1], row_odd[:, :], -2.0, 1.0, ALU.mult, ALU.add).then_inc(S["key_step"], 1)
            nc.vector.tensor_scalar(sign[:, 1:2], row_odd[:, :], 2.0, -1.0, ALU.mult, ALU.add).then_inc(S["key_step"], 1)
            dve.wait_ge(S["edges_loaded"], 32)
            nc.vector.tensor_scalar(src_in[0:LOAD_ROWS, :], src_in[0:LOAD_ROWS, :], DST_BITS, KEY_BASE, ALU.logical_shift_left,
                                    ALU.bitwise_or).then_inc(S["key_step"], 1)
            dve.wait_ge(S["key_step"], 6)
            nc.vector.tensor_tensor(keys[1][0:LOAD_ROWS, 0:LOAD_COLS].bitcast(I32), src_in[0:LOAD_ROWS, :], dst_in[0:LOAD_ROWS, :],
                                    ALU.bitwise_or).then_inc(S["key_step"], 1)
            dve.wait_ge(S["key_step"], 7)
            flat, signed = (t.rearrange("p (g t) -> p g t", t=2) for t in (keys[1], keys[0]))
            for t in range(2):
                nc.vector.tensor_scalar(signed[:, :, t], flat[:, :, t], sign[:, t:t + 1], None, ALU.mult).then_inc(S["key_step"], 1)

            dve.wait_ge(S["x_loaded"], 32)
            dve.wait_ge(S["x_zeroed"], 1)
            with nc.vector.Fori(0, BLOCKS // 7) as t:
                for k in range(7):
                    nc.vector.bn_stats(x_stats[:, 7 * t + k, :], base[:, 7 * t + k, :]).then_inc(S["x_stat"], 1)
            dve.wait_ge(S["x_stat"], BLOCKS)
            for t in range(BLOCKS):
                nc.vector.bn_aggr(x_mean_var[:, t, :], x_stats[:, t, :]).then_inc(S["x_stats_ready"], 1)

            def exchange(level, bit, half):
                done = exchanges_before(level, bit)
                held, into = keys[done % 2], keys[(done + 1) % 2]
                d = distance(bit)
                both = d == HALF
                for other in range(2):
                    if both or other == half or (level == LEVELS and d == HALF // 2):
                        dve.wait_ge(sorted_half[other], instructions_before(level, bit) if other >= half or both else
                                    instructions_before(level, bit))
                if is_after_turn(level, bit):
                    for other in (range(2) if both else (half,)):
                        dve.wait_ge(half_turned[other], turns_before(level, bit))
                        dve.wait_ge(upper_copied[other], turns_before(level, bit))
                lower_from = turned if is_after_turn(level, bit) else held
                views = [t[:, 0:COLS] if both else half_view(t, half) for t in (lower_from, held, into)]
                if bit == level - 1 and splits(level):
                    lower, upper, o = (v.rearrange("p (g r t d) -> p g r t d", r=2, t=2, d=d) for v in views)
                    for r in range(2):
                        sides = (lower[:, :, r, 0, :], upper[:, :, r, 1, :])
                        for t, op in ((0, ALU.min), (1, ALU.max)):
                            nc.vector.scalar_tensor_tensor(o[:, :, r, t, :], sides[1 - r], -1.0, sides[r], ALU.mult,
                                                           op).then_inc(sorted_half[half], 1)
                    return
                lower, upper, o = (v.rearrange("p (g t d) -> p g t d", t=2, d=d) for v in views)
                sides = (lower[:, :, 0, :], upper[:, :, 1, :])
                r = half if level == LEVELS - 1 else 0
                for t, op in ((0, ALU.min), (1, ALU.max)):
                    if bit == level - 1:
                        last = nc.vector.scalar_tensor_tensor(o[:, :, t, :], sides[1 - r], -1.0, sides[r], ALU.mult, op)
                    else:
                        last = nc.vector.tensor_tensor(o[:, :, t, :], sides[0], sides[1], op)
                    last.then_inc(sorted_half[t if both else half], 2 if both else 1)

            dve.wait_ge(S["key_step"], 9)
            for level in range(1, LEVELS + 1):
                for bit in range(level - 1, -1, -1):
                    for half in range(1 if distance(bit) == HALF and bit >= TURNED else 2):
                        exchange(level, bit, half)
            ordered = keys[exchanges_before(LEVELS + 1, LEVELS) % 2]

            for half in range(2):
                dve.wait_ge(sorted_half[half], SORT_END)
            bits = ordered[:, 0:EDGE_COLS].bitcast(I32)
            nc.vector.tensor_scalar(dst_of_edge.bitcast(I32), bits, DST_MASK, None, ALU.bitwise_and).then_inc(S["fields_ready"], 1)
            nc.vector.tensor_scalar(src_of_edge.bitcast(I32), bits, DST_BITS, DST_MASK, ALU.logical_shift_right,
                                    ALU.bitwise_and).then_inc(S["fields_ready"], 1)
            ends = ordered.rearrange("p (c n) -> p c n", n=P)
            limits = bound[:, :].bitcast(F32).unsqueeze(2).broadcast_to([P, BLOCKS + 1, COLS // P])
            for n, lane_of in enumerate((P - 1, 0)):
                keys_at = ends[:, :, lane_of].unsqueeze(1).broadcast_to([P, BLOCKS + 1, COLS // P])
                if n:
                    dve.wait_ge(S["below_ready"], 2)
                nc.vector.tensor_tensor(cut, keys_at, limits, ALU.is_lt).then_inc(S["below_ready"], 1)
                dve.wait_ge(S["below_ready"], 2 * n + 1)
                nc.vector.tensor_reduce(below[:, n, :], cut, AX.X, ALU.add).then_inc(S["below_ready"], 1)
            dve.wait_ge(S["counts_ps"], 1)
            nc.vector.tensor_copy(counts[:, 0:3], ps_counts[:, 0:3]).then_inc(S["counts_ready"], 1)
            dve.wait_ge(S["counts_ready"], 1)
            nc.vector.tensor_tensor(counts[:, 4:5], counts[:, 2:3], counts[:, 0:1], ALU.subtract).then_inc(S["counts_ready"], 1)
            nc.vector.tensor_tensor(counts[:, 5:6], counts[:, 1:2], counts[:, 2:3], ALU.subtract).then_inc(S["counts_ready"], 1)
            dve.wait_ge(S["counts_ready"], 3)
            nc.vector.scalar_tensor_tensor(counts[:, 6:7], last_block[:, :], 2.0 * EDGE_COLS, counts[:, 5:6], ALU.mult,
                                           ALU.add).then_inc(S["counts_ready"], 1)
            dve.wait_ge(S["counts_ready"], 4)
            nc.vector.tensor_scalar(chunk_w[:, :], ones[0:BLOCKS, :], counts[:, 6:7], None, ALU.mult).then_inc(S["past_ready"], 1)
            dve.wait_ge(S["ends_ps"], 1)
            nc.vector.tensor_copy(counts[:, 7:8], ps_end).then_inc(S["counts_ready"], 1)
            dve.wait_ge(S["counts_ready"], 5)
            nc.vector.tensor_tensor(late_block[:, :], counts[:, 7:8], step_limit[:, :], ALU.is_gt).then_inc(S["counts_ready"], 1)
            nc.vector.tensor_scalar(past_block, step_no[0:BLOCKS, :], counts[:, 7:8], None, ALU.is_ge).then_inc(S["past_ready"], 1)
            dve.wait_ge(S["steps_ps"], 1)
            nc.vector.tensor_tensor(chunk_of_step, turned[:, 0:STEPS], step_no, ALU.add).then_inc(S["chunk_ready"], 1)
            dve.wait_ge(S["chunk_ready"], 1)
            picks = 0
            for tile in range(STEP_TILES):
                at, to = tile * P, min(tile * P + P, STEPS)
                for c in [c for c in (tile - 1, tile) if c >= 0]:
                    if picks >= PICKS:
                        dve.wait_ge(S["pick_used"], picks - PICKS + 1)
                    nc.vector.tensor_scalar(pick[:, picks % PICKS, 0:to - at], chunk_of_step[:, at:to], edge_no[:, c:c + 1], None,
                                            ALU.is_equal).then_inc(S["pick_ready"], 1)
                    picks += 1
            dve.wait_ge(S["picked_ps"], 1)
            nc.vector.tensor_copy(step_dst, turned[:, 0:STEPS]).then_inc(S["tables_ready"], 1)
            nc.vector.tensor_scalar(late_flag[:, :], ps_late, 1.0, None, ALU.min).then_inc(S["tables_ready"], 1)

            def mark(first, at, count):
                dve.wait_ge(S["sum_ps"], first + count)
                dve.wait_ge(S["tables_ready"], 3)
                nc.vector.tensor_tensor(onehot[:, at:at + count, :], lane[:, :].unsqueeze(1).broadcast_to([P, count, P]),
                                        rel_ahead[:, bass.ds(first, count)].unsqueeze(2).broadcast_to([P, count, P]),
                                        ALU.is_equal).then_inc(S["onehot_ready"], count)

            place_regs = [dve.alloc_register(f"place{slot}") for slot in range(GROUP)]

            def load_places(i, g):
                dve.load(place_regs, step_acc[0:1, bass.ds(STEPS_PER_BLOCK * i + GROUP * g, GROUP)])

            def add_sums(i, j):
                at = STEPS_PER_BLOCK * i + j
                place = dve.snap(place_regs[j % GROUP], min_val=0, max_val=BLOCKS * ROW)
                sums = acc_mem[:, bass.ds(place, ROW)]
                dve.wait_ge(S["sum_added"], at + SUM_BANKS)
                dve.wait_ge(S["sum_ps"], at + 1 + STEPS_PER_BLOCK)
                nc.vector.tensor_tensor(sums, sums, ps_sum[j % SUM_BANKS], ALU.add).then_inc(S["sum_added"], 1)

            def normalise(n, b, steps, piece):
                links = FFN_LINKS * n + piece
                if piece == 0:
                    dve.wait_ge(S["sum_added"], SUM_BANKS + steps)
                    nc.vector.tensor_scalar(den[:, 0:1], acc_mem[:, bass.ds(ROW * b + DIM, 1)], 1e-12, None, ALU.max).then_inc(S["ffn_step"], 1)
                    dve.wait_ge(S["ffn_step"], links + 1)
                    dve.nop().then_inc(S["ffn_pass"], 1)
                if piece == 1:
                    nc.vector.reciprocal(den[:, 1:2], den[:, 0:1]).then_inc(S["ffn_step"], 1)
                if piece == 2:
                    dve.wait_ge(S["ffn_step"], links)
                    dve.wait_ge(S["sum_added"], SUM_BANKS + steps)
                    nc.vector.scalar_tensor_tensor(x2, acc_mem[:, bass.ds(ROW * b, DIM)], den[:, 1:2], base[:, b, :], ALU.mult,
                                                   ALU.add).then_inc(S["ffn_step"], 1)
                    dve.wait_ge(S["ffn_step"], links + 1)
                    dve.nop().then_inc(S["ffn_pass"], 1)
                if piece == 3:
                    nc.vector.bn_stats(stats[:, :], x2).then_inc(S["ffn_step"], 1)
                if piece == 4:
                    dve.wait_ge(S["ffn_step"], links)
                    dve.nop().then_inc(S["ffn_pass"], 1)
                    nc.vector.bn_aggr(mean_var[:, :], stats[:, :]).then_inc(S["x2_var"], 1)
                if piece == 6:
                    dve.wait_ge(S["x2_std"], n + 1)
                    nc.vector.reciprocal(rstd[:, 0:1], rstd[:, 1:2]).then_inc(S["ffn_step"], 1)
                if piece == 7:
                    dve.wait_ge(S["ffn_step"], FFN_LINKS * n + N_NORM)
                    nc.vector.tensor_scalar(xn2, x2, mean_var[:, 0:1], rstd[:, 0:1], ALU.subtract, ALU.mult).then_inc(S["x2_norm"], 1)

            def route(n, j):
                links = FFN_LINKS * n + N_NORM
                if j == PEAK_AT:
                    dve.wait_ge(S["logits_ps"], n + 1)
                    nc.vector.tensor_reduce(logit_max[:, :], ps_l, AX.X, ALU.max, negate=True).then_inc(S["logit_max_ready"], 1)
                if j == PROBS_AT:
                    dve.wait_ge(S["exp_ready"], n + 1)
                    nc.vector.reciprocal(exp_sum[:, 1:2], exp_sum[:, 0:1]).then_inc(S["ffn_step"], 1)
                    dve.wait_ge(S["ffn_step"], links + 1)
                    nc.vector.tensor_scalar(probs[:, 0:EXPERTS], exp_l[:, :], exp_sum[:, 1:2], None, ALU.mult).then_inc(S["ffn_step"], 1)
                if j == TOP_AT:
                    dve.wait_ge(S["ffn_step"], links + 2)
                    dve.nop().then_inc(S["ffn_pass"], 1)
                    nc.vector.max(top[:, :], probs[:, :]).then_inc(S["ffn_step"], 1)
                    dve.wait_ge(S["ffn_step"], links + 3)
                    nc.vector.tensor_tensor(top_w[:, 0:1], top[:, 1:2], top[:, 0:1], ALU.subtract).then_inc(S["top_diff_ready"], 1)
                    nc.vector.max_index(top_i[:, :], top[:, :], probs[:, :]).then_inc(S["ffn_step"], 1)
                if j == INDEX_AT:
                    dve.wait_ge(S["ffn_step"], links + 4)
                    nc.vector.tensor_copy(top_f[:, :], top_i[:, 0:2]).then_inc(S["ffn_step"], 1)
                if j == SHARE_AT:
                    dve.wait_ge(S["top_exp_ready"], n + 1)
                    nc.vector.tensor_scalar(top_w[:, 2:3], top_w[:, 1:2], 1.0, None, ALU.add).then_inc(S["ffn_step"], 1)
                    dve.wait_ge(S["ffn_step"], links + 6)
                    nc.vector.reciprocal(top_w[:, 3:4], top_w[:, 2:3]).then_inc(S["ffn_step"], 1)
                if j == SHARE_AT + 1:
                    dve.wait_ge(S["ffn_step"], links + 7)
                    nc.vector.tensor_tensor(top_w[:, 0:1], top_w[:, 1:2], top_w[:, 3:4], ALU.mult).then_inc(S["ffn_step"], 1)
                if j == SPREAD_AT:
                    dve.wait_ge(S["ffn_step"], links + 8)
                    nc.vector.tensor_scalar(gate_1[:, :], lane[:, 0:EXPERTS], top_f[:, 0:1], top_w[:, 3:4], ALU.is_equal,
                                            ALU.mult).then_inc(S["ffn_step"], 1)
                    nc.vector.tensor_scalar(gate_2[:, :], lane[:, 0:EXPERTS], top_f[:, 1:2], top_w[:, 0:1], ALU.is_equal,
                                            ALU.mult).then_inc(S["ffn_step"], 1)
                    dve.wait_ge(S["ffn_step"], links + N_ROUTE)
                    nc.vector.tensor_tensor(gates[:, :], gate_1[:, :], gate_2[:, :], ALU.add).then_inc(S["gates_ready"], 1)

            def dve_round(i, n, block_at, steps, experts, lead):
                for j in range(STEPS_PER_BLOCK):
                    if steps:
                        for start, end in RUNS:
                            if j % GROUP == start + 1:
                                ahead = j - 1 + GROUP
                                mark(STEPS_PER_BLOCK * i + ahead, ahead % STEPS_PER_BLOCK, end - start)
                        if j % GROUP == 0:
                            load_places(i, j // GROUP)
                        add_sums(i, j)
                    if experts and j == BEGIN_AT:
                        dve.wait_ge(S["row_stored"], 1 + 16 * n)
                        dve.wait_ge(S["b3_ps"], n + 1)
                        nc.vector.tensor_tensor(y_acc, x2, ps_b3, ALU.add).then_inc(S["y_begun"], 1)
                        dve.wait_ge(S["y_begun"], n + 1)
                    if experts and j in ADD_AT:
                        e = ADD_AT.index(j)
                        m = EXPERTS * n + e
                        dve.wait_ge(S["ey_added"], m + 1)
                        dve.wait_ge(S["ey_ps"], m + 1)
                        nc.vector.scalar_tensor_tensor(y_acc, ps_y, gates[:, e:e + 1], y_acc, ALU.mult, ALU.add).then_inc(S["ey_added"], 1)
                    if lead and NORM_AT <= j < NORM_AT + 8:
                        normalise(n + 1, block_at, STEPS_PER_BLOCK * i + j + 1 if steps else STEPS, j - NORM_AT)
                    if lead:
                        route(n + 1, j)

            dve.wait_ge(S["tables_ready"], 3)
            dve.wait_ge(S["acc_row_ready"], 1)
            dve.wait_ge(S["acc_zeroed"], 1)
            mark(0, 0, GROUP)
            dve_round(0, -2, None, True, False, False)
            dve_round(1, -1, 0, True, False, True)
            with nc.vector.Fori(2, BLOCKS) as i:
                dve_round(i, i - 2, i - 1, True, True, True)
            dve_round(None, BLOCKS - 2, FULL, False, True, True)
            dve_round(None, BLOCKS - 1, None, False, True, False)
            with nc.vector.If(dve.value_load(late_flag[:, :], min_val=0, max_val=1)):
                dve_round(None, BLOCKS - 1, 0, False, False, True)
                with nc.vector.Fori(0, FULL) as b:
                    dve_round(None, b + BLOCKS, b + 1, False, True, True)
                dve_round(None, 2 * BLOCKS - 1, None, False, True, False)


INPUTS = ["x", "src", "dst", "L0_gnn_W1", "L0_gnn_b1", "L0_gnn_W2", "L0_gnn_b2", "L0_mix_kln_weight", "L0_mix_kln_bias",
          "L0_mix_vln_weight", "L0_mix_vln_bias", "L0_ffn_router_w1", "L0_ffn_router_b1", "L0_ffn_router_w2", "L0_ffn_router_b2",
          "L0_ffn_expert_w1", "L0_ffn_expert_b1", "L0_ffn_expert_w2", "L0_ffn_expert_b2", "L0_ffn_expert_w3", "L0_ffn_expert_b3"]


def kernel(**inputs):
    import concourse.bacc as bacc
    from concourse.bass_utils import run_bass_kernel_spmd

    nc = bacc.Bacc("TRN2", target_bir_lowering=False, num_devices=1)
    arrays, aps = {}, {}
    for name in INPUTS:
        arrays[f"in_{name}"] = np.ascontiguousarray(inputs[name])
        shape, dt = arrays[f"in_{name}"].shape, mybir.dt.from_np(arrays[f"in_{name}"].dtype)
        aps[name] = nc.dram_tensor(f"in_{name}", shape, dt, kind="ExternalInput").ap()
    out = nc.dram_tensor("out_rows", (NODES, DIM), F32, kind="ExternalOutput").ap()
    y_table = nc.dram_tensor("gated_rows", (BLOCKS * P, ROW), F32, kind="Internal").ap()
    gps_layer(nc, aps, out, y_table)
    result = run_bass_kernel_spmd(nc, [arrays], core_ids=[0])
    return result.results[0]["out_rows"]
```

```python
from contextlib import ExitStack

import numpy as np
import concourse.bass as bass
from concourse import mybir

ALU = mybir.AluOpType
ACT = mybir.ActivationFunctionType
AX = mybir.AxisListType
F32 = mybir.dt.float32
I32 = mybir.dt.int32
U32 = mybir.dt.uint32

P = 128
NODES, DIM = 6250, 256
EDGES = 200000
HID = 128
HEADS = 8
HEAD_DIM = DIM // HEADS
EXPERTS = 6
HALVES = DIM // P
LN_EPS = 1e-5
HEAD_EPS = 1e-5

BLOCKS = -(-NODES // P)
LAST_ROWS = NODES - (BLOCKS - 1) * P
ROW = DIM + 1

LEVELS = 18
COLS = -(-EDGES // P**2) * P
HALF = 2**LEVELS // P // 2
TAIL = COLS - HALF
TURNED = 7
LAG = 2
STATS_AFTER = ((2, 0), (3, 0))
FRONT_FIRST = (1, 5)
FRONT_AT = {(8, 6): (5, 7), (9, 6): (7, 9), (10, 6): (9, 10), (11, 10): (10, 11), (11, 6): (11, 12), (12, 11): (12, 13),
            (12, 6): (13, 15), (13, 12): (15, 16), (13, 6): (16, 17), (14, 13): (17, 18), (14, 6): (18, 20), (15, 14): (20, 22)}
FRONT_END = ((15, 6), (16, 15), (16, 6))
GATED_AT = {(17, 16): (0, 24), (17, 6): (24, 42), (18, 17): (42, 49)}
MIX_AT = {(17, 6): (0, 2), (18, 17): (2, 5), (18, 6): (5, 8)}
MIX_KEPT_AT = {(18, 17): (0, 5), (18, 6): (5, 8)}
MIX_AFTER = {2: 8, 8: 9, 14: 10, 20: 11, 26: 12}
MIX_FIRST = 8
MIX_TILES = 4
MIX_BATCHES = -(-BLOCKS // MIX_TILES)
Y_SLOTS = 4
LOAD_ROWS = 125
LOAD_COLS = EDGES // LOAD_ROWS
DST_BITS = 13
DST_MASK = 2**DST_BITS - 1
BLOCK_SHIFT = DST_BITS + 7
KEY_BASE = 0x38000000
PAD_KEY = float(np.array([KEY_BASE | (BLOCKS * P) << DST_BITS], np.int32).view(np.float32)[0])

CHUNKS = -(-EDGES // P)
TILES = COLS // P
GROUP = 16
GROUPS_PER_BLOCK = 2
STEPS_PER_BLOCK = GROUP * GROUPS_PER_BLOCK
STEPS = STEPS_PER_BLOCK * BLOCKS
LAST_STEPS = STEPS_PER_BLOCK - (STEPS - CHUNKS)
assert 0 < LAST_STEPS <= STEPS_PER_BLOCK
SHARED = 2
SHARED_AT = BLOCKS + 1
CUT_ROUNDS = -(-(CHUNKS + BLOCKS - 1) // STEPS_PER_BLOCK)
CUT_STEPS = CUT_ROUNDS * STEPS_PER_BLOCK
assert COLS >= CUT_STEPS + STEPS_PER_BLOCK and COLS >= STEPS + STEPS_PER_BLOCK
PLACES = 8
SUM_BANKS = 4
assert STEPS_PER_BLOCK % SUM_BANKS == 0
BANK = 512
PICKS = 3
RUNS = ((0, 4), (4, 8), (8, 12), (12, GROUP))
NORM_PIECES = 10


def pieces(first, second, third, **others):
    places = dict(first=first, second=second, third=third, add=[at + 1 for at in third], **others)
    assert first[-1] < places["move"] and places["begin"] < min(places["add"][0], places["norm"] + 4)
    assert max(places["add"][-1], places["share"] + 1) <= places["spread"] < STEPS_PER_BLOCK
    return places


BESIDE = pieces([5 * e for e in range(EXPERTS)], [5 * e + 2 for e in range(EXPERTS)], [5 * e + 4 for e in range(EXPERTS)],
                gates=1, bias=2, begin=3, norm=6, root=12, turn=18, router=20, logits=22, peak=24, probs=26, top=27, index=28,
                share=29, move=30, spread=31)
ALONE = pieces([0, 1, 4, 8, 12, 16], [2, 5, 9, 13, 17, 20], [6, 10, 14, 18, 21, 23],
               gates=2, bias=3, begin=5, norm=2, root=9, turn=12, router=14, logits=15, peak=16, probs=18, top=19, index=20,
               share=21, move=17, spread=24)


def splits(level):
    return level not in (TURNED, LEVELS - 1, LEVELS)


def exchanges_before(level, bit):
    return level * (level - 1) // 2 + level - 1 - bit


def has_lone(bit, half):
    return distance(bit) >= P and bit >= TURNED and half == (bit < LEVELS - 1)


def stored_pairs(bit, half):
    if half == 0:
        return 0, HALF
    return HALF, COLS if bit < TURNED or distance(bit) < P else HALF + TAIL // (2 * P) * 2 * P


def instructions(level, bit, half):
    if bit == LEVELS - 1:
        return 2 if half == 0 else 1
    both_signs = bit == level - 1 and splits(level) and not (half == 1 and 4 * distance(bit) > TAIL and bit >= TURNED)
    return (4 if both_signs else 2) + has_lone(bit, half)


def instructions_before(level, bit, half):
    return sum(instructions(k, b, half) for k in range(1, level + 1) for b in range(k) if k < level or b > bit)


def turns_before(level, bit):
    if level <= TURNED:
        return 0
    return 2 * (level - TURNED - 1) + (2 if bit < TURNED else 1)


def is_after_turn(level, bit):
    return level > TURNED and bit in (level - 1, TURNED - 1)


def distance(bit):
    return 2**bit if bit < TURNED else 2 ** (bit - TURNED)


assert HALF // 2 < TAIL < HALF // 2 + 2 * P


def gps_layer(nc, a, out, y_table, kept_keys):
    with ExitStack() as ctx:
        def sb(name, shape, dt=F32):
            return ctx.enter_context(nc.sbuf_tensor(name, shape, dt))

        def sem(name):
            return ctx.enter_context(nc.semaphore(name))

        base = sb("base", [P, BLOCKS, DIM])
        acc_mem = sb("acc_mem", [P, (SHARED_AT + SHARED) * ROW])
        feat_mem = sb("feat_mem", [P, HALVES * BLOCKS * P])
        sort_mem = sb("sort_mem", [P, STEPS_PER_BLOCK * P])
        gath_mem = sb("gath_mem", [P, GROUP * ROW])
        tab_mem = sb("tab_mem", [P, 3 * COLS])

        keys = [sort_mem[:, 0:COLS], sort_mem[:, COLS:2 * COLS]]
        src_in = gath_mem[:, 0:LOAD_COLS].bitcast(I32)
        dst_in = gath_mem[:, LOAD_COLS:2 * LOAD_COLS].bitcast(I32)
        step_dst = tab_mem[:, 0:COLS].bitcast(U32)
        step_rel = tab_mem[:, COLS:2 * COLS]
        step_acc = tab_mem[0:1, 2 * COLS:3 * COLS].bitcast(I32)
        N_FIELDS = 6
        chunk_tmp = [tab_mem[:, 2 * COLS + k * TILES:2 * COLS + (k + 1) * TILES] for k in range(2 * N_FIELDS + 6)]
        chunk_int = tab_mem[:, 2 * COLS:2 * COLS + N_FIELDS * TILES].bitcast(I32).rearrange("p (k c) -> p k c", k=N_FIELDS)
        chunk_val = tab_mem[:, 2 * COLS + N_FIELDS * TILES:2 * COLS + 2 * N_FIELDS * TILES].rearrange("p (k c) -> p k c", k=N_FIELDS)
        straddles, span, to_shared, low, shift, place = chunk_tmp[2 * N_FIELDS:]
        share_low = sort_mem[:, 8 * P:8 * P + TILES * BLOCKS].rearrange("p (c b) -> p c b", c=TILES)
        begun = sort_mem[:, 2 * COLS:2 * COLS + TILES * (BLOCKS + 1)].rearrange("p (c b) -> p c b", c=TILES)
        sums_at = 2 * COLS + TILES * (BLOCKS + 1)
        row_sums = sort_mem[:, sums_at:sums_at + 2 * BLOCKS + 1]
        unfit = sort_mem[0:1, 2 * COLS:2 * COLS + 2 * BLOCKS + 2]
        assert 8 * P + TILES * BLOCKS <= COLS and sums_at + 2 * BLOCKS + 1 <= STEPS_PER_BLOCK * P
        dst_of_edge = gath_mem[:, 0:COLS]
        src_of_edge = gath_mem[:, COLS:2 * COLS]
        chunk_of_step = keys[0][:, 0:CUT_STEPS]
        pick = sort_mem[:, 2 * COLS:2 * COLS + PICKS * P].rearrange("p (s n) -> p s n", s=PICKS)
        past_block = keys[1][0:BLOCKS, 0:CUT_STEPS]
        step_no = tab_mem[:, 2 * COLS:2 * COLS + CUT_STEPS]
        chunk_w, neg_block, acc_w = (sort_mem[0:BLOCKS, 2 * COLS + (PICKS + k) * P:2 * COLS + (PICKS + k + 1) * P] for k in range(3))
        assert 2 * COLS + (PICKS + 3) * P <= STEPS_PER_BLOCK * P
        gathered = gath_mem[:, 0:GROUP * ROW].rearrange("p (s n) -> p s n", s=GROUP)
        onehot = sort_mem[:, :].rearrange("p (s n) -> p s n", s=STEPS_PER_BLOCK)
        used = [0]

        def early(n):
            at = used[0]
            used[0] += n
            assert used[0] <= (SHARED_AT + SHARED) * ROW
            return acc_mem[:, at:at + n]

        def slots(t, n=2):
            return t.rearrange("p (s n) -> p s n", s=n)

        xnT = feat_mem[:, :].rearrange("p (h n) -> p h n", h=HALVES)
        x_stats = early(6 * BLOCKS).rearrange("p (b n) -> p b n", n=6)
        x_mean_var = early(2 * BLOCKS).rearrange("p (b n) -> p b n", n=2)
        x_rstd, x_bias, gate, y_scale, y_bias = (early(BLOCKS) for _ in range(5))
        xs, dev = (slots(early(2 * DIM)) for _ in range(2))
        zed = early(2 * HALVES * (P + 1)).rearrange("p (k n) -> p k n", n=P + 1)
        xsT, sqT = (early(2 * DIM).rearrange("p (h n) -> p h n", h=HALVES) for _ in range(2))
        hid = early(2 * P)
        y_out = slots(early(Y_SLOTS * ROW), Y_SLOTS)
        var, std, std_eps, over_std = (early(2 * HEADS) for _ in range(4))
        k_col_w, k_col_b, z_sum, kw_sum = (early(HALVES) for _ in range(4))
        v_row_w, v_row_b, z_row, kv_a, kv_b = (early(DIM).rearrange("p (h n) -> p h n", h=HALVES) for _ in range(5))
        diag_sum = early(DIM).rearrange("p (h n) -> p h n", h=HALVES)
        late = [0]

        def after(n):
            at = late[0]
            late[0] += n
            assert late[0] <= HALVES * BLOCKS * P
            return feat_mem[:, at:at + n]

        w1, w2, w3 = (after(EXPERTS * HALVES * DIM).rearrange("p (e h n) -> p e h n", e=EXPERTS, h=HALVES) for _ in range(3))
        x2, xn2, y_acc = after(DIM), after(DIM), after(DIM)
        next_T, this_T = (after(DIM).rearrange("p (h n) -> p h n", h=HALVES) for _ in range(2))
        router_hid = after(P)
        gates_T = after(P)[0:EXPERTS, :]
        h1_T, h2_T = (after(2 * DIM).rearrange("p (s h n) -> p s h n", s=2, h=HALVES) for _ in range(2))
        ident, lane, ones = (sb(n, [P, P]) for n in ("ident", "lane", "ones"))
        kv = sb("kv", [P, HALVES, P])
        router_w1 = sb("router_w1", [P, HALVES, HID])
        router_b1 = sb("router_b1", [P, 1])
        router_w2, router_b2 = sb("router_w2", [P, EXPERTS]), sb("router_b2", [1, EXPERTS])
        b1, b2 = sb("b1", [P, EXPERTS, HALVES]), sb("b2", [P, EXPERTS, HALVES])
        b3 = sb("b3", [EXPERTS, DIM])
        bound = sb("bound", [P, BLOCKS + 1], I32)
        cut_cols = (BLOCKS + 1) * TILES
        cut = acc_mem[:, 0:cut_cols].rearrange("p (b c) -> p b c", b=BLOCKS + 1)
        below = acc_mem[:, cut_cols:cut_cols + 2 * (BLOCKS + 1)].rearrange("p (n b) -> p n b", n=2)
        upto = sb("upto", [BLOCKS, BLOCKS])
        edge_no = sb("edge_no", [P, TILES])
        last_block = sb("last_block", [BLOCKS, 1])
        is_earlier, is_later = sb("is_earlier", [P, BLOCKS]), sb("is_later", [P, BLOCKS + 1])
        cut_flag = sb("cut_flag", [1, 1], I32)
        ln_eps = sb("ln_eps", [P, 1])
        step_idx = sb("step_idx", [P, STEPS_PER_BLOCK], U32)
        front_at = [2 * COLS]

        def in_front(n):
            at = front_at[0]
            front_at[0] += n
            assert front_at[0] <= GROUP * ROW
            return gath_mem[:, at:at + n]

        centre, same_head = in_front(P), in_front(P)
        gnn_w1 = in_front(HALVES * HID).rearrange("p (h n) -> p h n", h=HALVES)
        gnn_w2, gnn_b1, gnn_b2 = (in_front(1) for _ in range(3))
        row_no, row_odd = (in_front(1).bitcast(I32) for _ in range(2))
        sign = in_front(2)
        minus_half = in_front(BLOCKS)
        minus_one, half_power, head_eps = (in_front(2 * HEADS) for _ in range(3))
        head_mean = in_front(P // HEAD_DIM)
        den, stats, mean_var, rstd, logit_max, exp_l = (after(n) for n in (2, 6, 2, 2, 1, EXPERTS))
        exp_sum, top, top_i, top_f, top_w = after(2), after(8), after(8).bitcast(U32), after(2), after(4)
        gate_1, gate_2, gates = (after(EXPERTS) for _ in range(3))
        probs = sb("probs", [P, 8])
        counts = after(8)[0:BLOCKS, :]

        turned = ctx.enter_context(nc.psum_tensor("turned", [P, 4 * BANK], F32))
        front = ctx.enter_context(nc.psum_tensor("front", [P, 4 * BANK], F32))

        def bank(i):
            return front[:, i * BANK:(i + 1) * BANK]

        ps_xT = bank(0).rearrange("p (h n) -> p h n", h=HALVES)
        ps_dev = slots(bank(1))
        ps_devT = bank(1).rearrange("p (h n) -> p h n", h=HALVES)
        ps_hid = bank(2)[:, 0:2 * P]
        ps_var = bank(2)[:, 2 * P + BLOCKS:2 * P + BLOCKS + 2 * HEADS]
        ps_z = bank(3)[:, 0:HALVES * (P + 1)].rearrange("p (h n) -> p h n", h=HALVES)
        ps_logit = bank(2)[:, 2 * P:2 * P + BLOCKS]
        ps_z_row = bank(0)[:, 0:DIM].rearrange("p (h n) -> p h n", h=HALVES)
        ps_mix = [front[:, s * MIX_TILES * DIM:(s + 1) * MIX_TILES * DIM].rearrange("p (t n) -> p t n", t=MIX_TILES) for s in range(2)]
        ps_counts = bank(3)[0:BLOCKS, 0:4]
        ps_end = bank(3)[0:BLOCKS, 4:5]
        ps_sum = [turned[:, BANK * i:BANK * i + ROW] for i in range(SUM_BANKS)]
        ps_row_sums = turned[:, COLS:COLS + 2 * BLOCKS + 1]
        ps_share_low, ps_begun = ps_row_sums[:, 0:BLOCKS], ps_row_sums[:, BLOCKS:2 * BLOCKS + 1]
        ps_h1, ps_h2 = (bank(n)[:, 0:DIM].rearrange("p (h n) -> p h n", h=HALVES) for n in range(2))
        ps_y = bank(3)[:, 0:DIM]
        ps_x2T = bank(2)[:, 0:DIM].rearrange("p (h n) -> p h n", h=HALVES)
        ps_b3 = bank(2)[:, 0:DIM]
        ps_router = bank(2)[:, DIM:DIM + P]
        ps_l = bank(2)[:, DIM:DIM + EXPERTS]
        ps_gates_T = bank(2)[0:EXPERTS, DIM + P:DIM + 2 * P]

        names = """x_zeroed edges_loaded small_loaded ln_loaded consts weights_loaded
            key_step pool_step act_step x_stat x_stats_ready x_norm
            xs_ready xT_ps xT_ready xT_filed devT_ps square_ready hid_ps hid_ready dev_ps dev_ready var_ps var_ready zed_ready
            z_summed z_zeroed z_copied diag_ready z_row_ps z_row_ready kv_final gate_ready y_params y_ready
            mix_ps mix_done
            sorted_turned kept_stored fields_ready rel_ready chunk_step place_ready places_ps places_ready
            marks_ready marks_ps flag_step flag_ready kept_loaded cut_consts
            cut_fields_ready edges_ready below_ready counts_ps counts_ready ends_ps past_ready steps_ps chunk_ready
            acc_row_ready pick_ready pick_used picked_ps cut_ready acc_zeroed
            idx_staged slot_free onehot_ready sum_ps sum_added
            ffn_step ffn_pass x2_var x2_std x2_norm x2T_ps x2T_ready router_ps router_ready logits_ps logit_max_ready
            exp_ready top_diff_ready top_exp_ready gates_ready gatesT_ps gatesT_ready b3_ps this_ready y_begun
            h1_ps h1_ready h2_ps h2_ready ey_ps ey_added row_stored""".split()
        S = {name: sem(name) for name in names}
        sorted_half = [sem("sorted_half0"), sem("sorted_half1")]
        x_loaded = [sem("x_loaded0"), sem("x_loaded1")]
        half_turned = [sem("half_turned0"), sem("half_turned1")]
        upper_copied = [sem("upper_copied0"), sem("upper_copied1")]
        y_stored = [sem(f"y_stored{s}") for s in range(Y_SLOTS)]
        rows_in = [sem(f"rows_in{i}") for i in range(GROUP)]

        N_CONSTS = 16
        SPREAD_LINKS = 3
        N_SMALL = 13
        N_MIX_LOADS = 6
        FULL = BLOCKS - 1
        PAIRS = FULL // 2
        TABLE_PARTS = ((0, P), (P, HALF), (HALF, COLS))
        X_PARTS = ((0, 21), (21, BLOCKS))
        N_NORM, N_ROUTE = 8, 10
        FFN_LINKS = N_NORM + N_ROUTE

        def sides(t, bit, half):
            if bit == LEVELS - 1:
                return t[:, 0:TAIL].unsqueeze(1), t[:, HALF:COLS].unsqueeze(1)
            if bit == LEVELS - 2 and half == 1:
                return t[:, HALF:HALF + TAIL - HALF // 2].unsqueeze(1), t[:, HALF + HALF // 2:COLS].unsqueeze(1)
            at, to = stored_pairs(bit, half)
            pairs = t[:, at:to].rearrange("p (g t d) -> p g t d", t=2, d=distance(bit))
            return pairs[:, :, 0, :], pairs[:, :, 1, :]

        def lone(t, bit):
            if bit == LEVELS - 1:
                return t[:, TAIL:HALF]
            if bit == LEVELS - 2:
                return t[:, HALF + TAIL - HALF // 2:HALF + HALF // 2]
            return t[:, stored_pairs(bit, 1)[1]:COLS]

        ordered = keys[exchanges_before(LEVELS + 1, LEVELS) % 2]
        assert ordered.shape == keys[1].shape

        block = ctx.enter_context(nc.Block())

        @block.sync
        def _(sp):
            sp.dma_start(src_in[0:LOAD_ROWS, :], a["src"].rearrange("(p c) -> p c", p=LOAD_ROWS)).then_inc(S["edges_loaded"], 16)
            sp.dma_start(dst_in[0:LOAD_ROWS, :], a["dst"].rearrange("(p c) -> p c", p=LOAD_ROWS)).then_inc(S["edges_loaded"], 16)
            for part, (at, to) in enumerate(X_PARTS):
                to = min(to, FULL)
                sp.dma_start(base[:, at:to, :], a["x"][at * P:to * P, :].rearrange("(b p) d -> p b d", p=P)).then_inc(x_loaded[part], 16)
            sp.wait_ge(S["x_zeroed"], 1)
            sp.dma_start(base[0:LAST_ROWS, FULL, :], a["x"][FULL * P:NODES, :]).then_inc(x_loaded[1], 16)
            sp.dma_start(gnn_w1[:, :, :], a["L0_gnn_W1"].rearrange("(h p) n -> p h n", p=P)).then_inc(S["small_loaded"], 16)
            sp.dma_start(gnn_b1[:, :], a["L0_gnn_b1"].rearrange("(p o) -> p o", o=1)).then_inc(S["small_loaded"], 16)
            sp.dma_start(gnn_w2[:, :], a["L0_gnn_W2"]).then_inc(S["small_loaded"], 16)
            sp.dma_start(gnn_b2[:, :], a["L0_gnn_b2"].partition_broadcast(P)).then_inc(S["small_loaded"], 16)
            sp.dma_start(router_w1[:, :, :], a["L0_ffn_router_w1"].rearrange("(h p) n -> p h n", p=P)).then_inc(S["small_loaded"], 16)
            sp.dma_start(router_b1[:, :], a["L0_ffn_router_b1"].rearrange("(p o) -> p o", o=1)).then_inc(S["small_loaded"], 16)
            sp.dma_start(router_w2[:, :], a["L0_ffn_router_w2"]).then_inc(S["small_loaded"], 16)
            sp.dma_start(router_b2[:, :], a["L0_ffn_router_b2"].rearrange("(o e) -> o e", o=1)).then_inc(S["small_loaded"], 16)
            sp.dma_start(b3[:, :], a["L0_ffn_expert_b3"]).then_inc(S["small_loaded"], 16)
            with nc.allow_non_contiguous_dma(reason="biases and head weights with the feature on the partition, once"):
                for bias, name in ((b1, "L0_ffn_expert_b1"), (b2, "L0_ffn_expert_b2")):
                    for h in range(HALVES):
                        sp.dma_start(bias[:, :, h], a[name][:, h * P:(h + 1) * P].rearrange("e p -> p e")).then_inc(S["small_loaded"], 16)
                for t, name in ((k_col_w, "kln_weight"), (k_col_b, "kln_bias")):
                    for h in range(HALVES):
                        rows = a["L0_mix_" + name].rearrange("g o c -> (g o c)")[h * P:(h + 1) * P]
                        sp.dma_start(t[:, h:h + 1], rows.rearrange("(p o) -> p o", o=1)).then_inc(S["ln_loaded"], 16)
            for t, name in ((v_row_w, "vln_weight"), (v_row_b, "vln_bias")):
                sp.dma_start(t.rearrange("p h n -> p (h n)"),
                             a["L0_mix_" + name].rearrange("g o c -> (g o c)").partition_broadcast(P)).then_inc(S["ln_loaded"], 16)

            with sp.Fori(0, FULL // Y_SLOTS) as i:
                for s in range(Y_SLOTS):
                    sp.wait_ge(S["y_ready"], Y_SLOTS * i + s + 1)
                    sp.dma_start(y_table[bass.ds((Y_SLOTS * i + s) * P, P), :], y_out[:, s, :]).then_inc(y_stored[s], 16)
            sp.wait_ge(S["y_ready"], BLOCKS)
            sp.dma_start(y_table[FULL * P:BLOCKS * P, :], y_out[:, 0, :]).then_inc(y_stored[0], 16)

            for half in range(2):
                sp.wait_ge(sorted_half[half], instructions_before(LEVELS, -1, half))
            sp.dma_start(kept_keys, ordered).then_inc(S["kept_stored"], 16)

            sp.wait_ge(S["mix_done"], MIX_BATCHES)
            for w, name in ((w1, "L0_ffn_expert_w1"), (w2, "L0_ffn_expert_w2"), (w3, "L0_ffn_expert_w3")):
                for e in range(EXPERTS):
                    sp.dma_start(w[:, e, :, :], a[name][e].rearrange("(h p) n -> p h n", p=P)).then_inc(S["weights_loaded"], 16)

            def store_all(first):
                with sp.Fori(0, FULL) as b:
                    sp.wait_ge(S["ey_added"], 1 + EXPERTS * (first + b + 1))
                    sp.dma_start(out[bass.ds(b * P, P), :], y_acc).then_inc(S["row_stored"], 16)
                sp.wait_ge(S["ey_added"], 1 + EXPERTS * (first + BLOCKS))
                sp.dma_start(out[FULL * P:NODES, :], y_acc[0:LAST_ROWS, :]).then_inc(S["row_stored"], 16)
                sp.wait_ge(S["row_stored"], 1 + 16 * (first + BLOCKS))

            store_all(0)
            sp.wait_ge(S["flag_ready"], 1)
            sp.wait_ge(S["kept_stored"], 16)
            with sp.If(sp.value_load(cut_flag[:, :], min_val=0, max_val=1)):
                sp.wait_ge(S["onehot_ready"], STEPS + GROUP)
                sp.wait_ge(S["sum_ps"], STEPS + STEPS_PER_BLOCK)
                sp.dma_start(ordered, kept_keys).then_inc(S["kept_loaded"], 16)
                store_all(BLOCKS)

        @block.gpsimd
        def _(pool):
            nc.gpsimd.memset(base[:, FULL, :], 0.0).then_inc(S["x_zeroed"], 1)
            nc.gpsimd.iota(row_no[:, :], pattern=[[0, 1]], base=0, channel_multiplier=1).then_inc(S["consts"], 1)
            nc.gpsimd.iota(bound[:, :], pattern=[[1, BLOCKS + 1]], base=0, channel_multiplier=0).then_inc(S["consts"], 1)
            nc.gpsimd.memset(ident[:, :], 0.0).then_inc(S["pool_step"], 1)
            nc.gpsimd.memset(same_head[:, :], 0.0).then_inc(S["pool_step"], 1)
            nc.gpsimd.memset(upto[:, :], 1.0).then_inc(S["pool_step"], 1)
            nc.gpsimd.memset(last_block[:, :], 0.0).then_inc(S["pool_step"], 1)
            nc.gpsimd.memset(is_later[:, :], 0.0).then_inc(S["consts"], 1)
            nc.gpsimd.memset(ln_eps[:, :], LN_EPS).then_inc(S["consts"], 1)
            nc.gpsimd.memset(ones[:, :], 1.0).then_inc(S["consts"], 1)
            nc.gpsimd.memset(probs[:, :], -1.0).then_inc(S["consts"], 1)
            nc.gpsimd.memset(minus_half[:, :], -0.5).then_inc(S["consts"], 1)
            nc.gpsimd.memset(minus_one[:, :], -1.0).then_inc(S["consts"], 1)
            nc.gpsimd.memset(half_power[:, :], 0.5).then_inc(S["consts"], 1)
            nc.gpsimd.memset(zed, 1.0).then_inc(S["consts"], 1)
            nc.gpsimd.memset(head_mean[:, :], 0.0).then_inc(S["pool_step"], 1)
            nc.gpsimd.memset(head_eps[:, :], HEAD_EPS).then_inc(S["consts"], 1)
            nc.gpsimd.iota(lane[:, :], pattern=[[1, P]], base=0, channel_multiplier=0,
                           allow_small_or_imprecise_dtypes=True).then_inc(S["consts"], 1)
            nc.gpsimd.iota(edge_no[:, :], pattern=[[P, TILES]], base=0, channel_multiplier=1,
                           allow_small_or_imprecise_dtypes=True).then_inc(S["consts"], 1)
            pool.wait_ge(S["pool_step"], 5)
            nc.gpsimd.affine_select(out=ident[:, :], in_=ident[:, :], compare_op=ALU.not_equal, fill=1.0, base=0,
                                    pattern=[[-1, P]], channel_multiplier=1).then_inc(S["consts"], 1)
            nc.gpsimd.affine_select(out=upto[:, :], in_=upto[:, :], compare_op=ALU.is_ge, fill=0.0, base=0,
                                    pattern=[[1, BLOCKS]], channel_multiplier=-1).then_inc(S["consts"], 1)
            nc.gpsimd.affine_select(out=last_block[:, :], in_=last_block[:, :], compare_op=ALU.not_equal, fill=1.0,
                                    base=-(BLOCKS - 1), pattern=[[0, 1]], channel_multiplier=1).then_inc(S["pool_step"], 1)
            pool.wait_ge(S["consts"], N_CONSTS - 1)
            pool.wait_ge(S["pool_step"], 6)
            for h in range(P // HEAD_DIM):
                part = slice(h * HEAD_DIM, (h + 1) * HEAD_DIM)
                nc.gpsimd.memset(same_head[part, part], 1.0).then_inc(S["pool_step"], 1)
                nc.gpsimd.memset(head_mean[part, h:h + 1], 1.0 / (HEAD_DIM - 1)).then_inc(S["pool_step"], 1)
            n = 6 + 2 * (P // HEAD_DIM)
            pool.wait_ge(S["pool_step"], n)
            nc.gpsimd.tensor_scalar(centre[:, :], same_head[:, :], -1.0 / HEAD_DIM, None, ALU.mult).then_inc(S["pool_step"], 1)
            pool.wait_ge(S["pool_step"], n + 1)
            nc.gpsimd.tensor_tensor(centre[:, :], centre[:, :], ident[:, :], ALU.add).then_inc(S["consts"], 1)
            pool.nop().then_inc(S["zed_ready"], 1)

            for part, (at, to) in enumerate(X_PARTS):
                mean, variance, scale, shift = x_mean_var[:, at:to, 0], x_mean_var[:, at:to, 1], x_rstd[:, at:to], x_bias[:, at:to]
                links = n + 3 * part
                pool.wait_ge(S["x_stats_ready"], to)
                nc.gpsimd.tensor_scalar(shift, variance, LN_EPS, None, ALU.add).then_inc(S["pool_step"], 1)
                pool.wait_ge(S["pool_step"], links + 2)
                nc.gpsimd.tensor_tensor(scale, shift, minus_half[:, at:to], ALU.pow).then_inc(S["pool_step"], 1)
                pool.wait_ge(S["pool_step"], links + 3)
                nc.gpsimd.tensor_tensor(shift, mean, scale, ALU.mult).then_inc(S["pool_step"], 1)
                pool.wait_ge(S["pool_step"], links + 4)
                nc.gpsimd.tensor_scalar(shift, shift, -1.0, None, ALU.mult).then_inc(S["x_norm"], 1)
            n += 7

            def spread(u, tiles, first):
                links = first + SPREAD_LINKS * u
                heads = tiles * HEADS
                halves = HALVES * tiles
                of, to = (v.rearrange("p k (h c) -> p k h c", c=HEAD_DIM)
                          for v in (dev[:, 0:tiles, :].rearrange("p s (h n) -> p (s h) n", n=P), zed[:, 0:halves, 0:P]))
                by = over_std[:, 0:heads].rearrange("p (k h) -> p k h", k=halves).unsqueeze(3).broadcast_to([P, halves, P // HEAD_DIM, HEAD_DIM])
                pool.wait_ge(S["var_ready"], u + 1)
                nc.gpsimd.tensor_tensor(std[:, 0:heads], var[:, 0:heads], half_power[:, 0:heads], ALU.pow).then_inc(S["pool_step"], 1)
                pool.wait_ge(S["pool_step"], links + 1)
                nc.gpsimd.tensor_tensor(std_eps[:, 0:heads], std[:, 0:heads], head_eps[:, 0:heads], ALU.add).then_inc(S["pool_step"], 1)
                pool.wait_ge(S["pool_step"], links + 2)
                nc.gpsimd.tensor_tensor(over_std[:, 0:heads], std_eps[:, 0:heads], minus_one[:, 0:heads], ALU.pow).then_inc(S["pool_step"], 1)
                pool.wait_ge(S["pool_step"], links + 3)
                pool.wait_ge(S["z_summed"], u + 1)
                nc.gpsimd.tensor_tensor(to, of, by, ALU.mult).then_inc(S["zed_ready"], 1)

            with nc.gpsimd.Fori(0, PAIRS) as u:
                spread(u, 2, n)
            spread(PAIRS, 1, n)
            n += SPREAD_LINKS * (PAIRS + 1)

            pool.wait_ge(S["gate_ready"], 1)
            nc.gpsimd.tensor_tensor(y_scale, x_rstd, gate, ALU.mult).then_inc(S["y_params"], 1)
            nc.gpsimd.tensor_tensor(y_bias, x_bias, gate, ALU.mult).then_inc(S["y_params"], 1)

            pool.wait_ge(S["ln_loaded"], 16 * N_MIX_LOADS)
            pool.wait_ge(S["z_copied"], 2)
            for h in range(HALVES):
                last = nc.gpsimd.tensor_scalar(diag_sum[:, h, :], ident[:, :], z_sum[:, h:h + 1], None, ALU.mult)
                last.then_inc(S["diag_ready"], 1)
            nc.gpsimd.tensor_tensor(kw_sum, k_col_w, z_sum, ALU.mult).then_inc(S["pool_step"], 1)
            nc.gpsimd.tensor_tensor(kv_a, kv_a, v_row_w, ALU.mult).then_inc(S["pool_step"], 1)
            nc.gpsimd.tensor_scalar(kv_b, v_row_b, float(NODES), None, ALU.mult).then_inc(S["pool_step"], 1)
            pool.wait_ge(S["z_row_ready"], 1)
            nc.gpsimd.tensor_tensor(z_row, z_row, v_row_w, ALU.mult).then_inc(S["pool_step"], 1)
            pool.wait_ge(S["pool_step"], n + 4)
            nc.gpsimd.tensor_tensor(kv_b, kv_b, z_row, ALU.add).then_inc(S["pool_step"], 1)
            pool.wait_ge(S["pool_step"], n + 5)
            for h in range(HALVES):
                nc.gpsimd.tensor_scalar(kv_a[:, h, :], kv_a[:, h, :], k_col_w[:, h:h + 1], None, ALU.mult).then_inc(S["pool_step"], 1)
                nc.gpsimd.tensor_scalar(kv_b[:, h, :], kv_b[:, h, :], k_col_b[:, h:h + 1], None, ALU.mult).then_inc(S["pool_step"], 1)
                nc.gpsimd.tensor_scalar(z_row[:, h, :], v_row_b[:, h, :], kw_sum[:, h:h + 1], None, ALU.mult).then_inc(S["pool_step"], 1)
            pool.wait_ge(S["pool_step"], n + 5 + 3 * HALVES)
            nc.gpsimd.tensor_tensor(kv_a, kv_a, kv_b, ALU.add).then_inc(S["pool_step"], 1)
            pool.wait_ge(S["pool_step"], n + 6 + 3 * HALVES)
            nc.gpsimd.tensor_tensor(kv_a, kv_a, z_row, ALU.add).then_inc(S["pool_step"], 1)
            pool.wait_ge(S["pool_step"], n + 7 + 3 * HALVES)
            nc.gpsimd.tensor_tensor(kv_a, kv_a, same_head[:, :].unsqueeze(1).broadcast_to([P, HALVES, P]),
                                    ALU.mult).then_inc(S["pool_step"], 1)
            pool.wait_ge(S["pool_step"], n + 8 + 3 * HALVES)
            nc.gpsimd.tensor_scalar(kv_a, kv_a, 1.0 / NODES, None, ALU.mult).then_inc(S["pool_step"], 1)
            pool.wait_ge(S["pool_step"], n + 9 + 3 * HALVES)
            nc.gpsimd.tensor_tensor(kv[:, :, :], kv_a, ident[:, :].unsqueeze(1).broadcast_to([P, HALVES, P]),
                                    ALU.add).then_inc(S["kv_final"], 1)

            pool.wait_ge(S["kv_final"], 1)
            for s in range(Y_SLOTS):
                pool.wait_ge(y_stored[s], 16 * (FULL // Y_SLOTS + (s == 0)))
            nc.gpsimd.memset(acc_mem[:, :], 0.0).then_inc(S["acc_zeroed"], 1)

            def gather_round(i, staged_before, steps=STEPS_PER_BLOCK):
                for g in range(GROUPS_PER_BLOCK):
                    pool.wait_ge(S["idx_staged"], GROUPS_PER_BLOCK * i + g + 1 + staged_before)
                    for start, end in RUNS:
                        pool.wait_ge(S["sum_ps"], STEPS_PER_BLOCK * i + g * GROUP + end + STEPS_PER_BLOCK - GROUP)
                        pool.nop().then_inc(S["slot_free"], 1)
                        for slot in range(start, end):
                            j = g * GROUP + slot
                            if j < steps:
                                nc.gpsimd.indirect_dma_start(
                                    out=gathered[:, slot, :], out_offset=None, in_=y_table,
                                    in_offset=bass.IndirectOffsetOnAxis(ap=step_idx[:, j:j + 1], axis=0)).then_inc(rows_in[slot], 16)

            with nc.gpsimd.Fori(0, FULL) as i:
                gather_round(i, 0)
            gather_round(FULL, 0, LAST_STEPS)
            pool.wait_ge(S["flag_ready"], 1)
            with nc.gpsimd.If(pool.value_load(cut_flag[:, :], min_val=0, max_val=1)):
                pool.wait_ge(S["sum_added"], SUM_BANKS + STEPS)
                pool.wait_ge(S["kept_loaded"], 16)
                nc.gpsimd.iota(step_no, pattern=[[1, CUT_STEPS]], base=0, channel_multiplier=0,
                               allow_small_or_imprecise_dtypes=True).then_inc(S["cut_consts"], 1)
                nc.gpsimd.memset(neg_block, -float(P)).then_inc(S["cut_consts"], 1)
                nc.gpsimd.memset(acc_w, float(ROW)).then_inc(S["cut_consts"], 1)
                pool.wait_ge(S["counts_ps"], 1)
                nc.gpsimd.memset(acc_mem[:, :], 0.0).then_inc(S["acc_zeroed"], 1)
                with nc.gpsimd.Fori(0, CUT_ROUNDS) as i:
                    gather_round(i + BLOCKS, 1)

        @block.scalar
        def _(act):
            act.nop().then_inc(S["h1_ready"], HALVES)
            act.nop().then_inc(S["h2_ready"], HALVES)
            act.wait_ge(S["small_loaded"], 16 * N_SMALL)
            act.wait_ge(x_loaded[0], 16)
            act.wait_ge(S["x_norm"], 1)

            def norm(u, tiles):
                act.wait_ge(S["xT_ps"], u)
                for s in range(tiles):
                    act.wait_ge(S["x_norm"], 1)
                    nc.scalar.activation(xs[:, s, :], base[:, 2 * u + s, :], ACT.Identity, bias=x_bias[:, bass.ds(2 * u + s, 1)],
                                         scale=x_rstd[:, bass.ds(2 * u + s, 1)]).then_inc(S["xs_ready"], 1)

            def keep_turned(u, tiles):
                act.wait_ge(S["xT_ps"], u + 1)
                act.wait_ge(S["dev_ps"], u)
                act.wait_ge(S["xT_filed"], u)
                nc.scalar.activation(xsT[:, :, 0:tiles * P], ps_xT[:, :, 0:tiles * P], ACT.Copy).then_inc(S["xT_ready"], 1)

            def file_turned(u, tiles):
                act.wait_ge(S["xT_ready"], u + 1)
                act.wait_ge(S["x_norm"], 1)
                nc.scalar.activation(xnT[:, :, bass.ds(2 * P * u, tiles * P)], xsT[:, :, 0:tiles * P], ACT.Copy).then_inc(S["xT_filed"], 1)

            def front_round(u):
                tiles, next_tiles, far_tiles = (2 if not isinstance(u, int) or u + k < PAIRS else 1 for k in range(3))
                act.wait_ge(S["devT_ps"], u + 1)
                act.wait_ge(S["var_ps"], u)
                nc.scalar.activation(sqT[:, :, 0:tiles * P], ps_devT[:, :, 0:tiles * P], ACT.Square).then_inc(S["square_ready"], 1)
                act.wait_ge(S["hid_ps"], u + 1)
                nc.scalar.activation(hid[:, 0:tiles * P], ps_hid[:, 0:tiles * P], ACT.Relu, bias=gnn_b1[:, 0:1]).then_inc(S["hid_ready"], 1)
                following = not isinstance(u, int) or u + 1 <= PAIRS
                if following:
                    keep_turned(u + 1, next_tiles)
                act.wait_ge(S["dev_ps"], u + 1)
                act.wait_ge(S["zed_ready"], u + 1)
                nc.scalar.activation(dev[:, 0:tiles, :], ps_dev[:, 0:tiles, :], ACT.Copy).then_inc(S["dev_ready"], 1)
                act.wait_ge(S["var_ps"], u + 1)
                nc.scalar.activation(var[:, 0:tiles * HEADS], ps_var[:, 0:tiles * HEADS], ACT.Copy).then_inc(S["var_ready"], 1)
                if not isinstance(u, int) or u + 2 <= PAIRS:
                    norm(u + 2, far_tiles)
                if following:
                    file_turned(u + 1, next_tiles)

            norm(0, 2)
            keep_turned(0, 2)
            norm(1, 2)
            file_turned(0, 2)
            front_round(0)
            with nc.scalar.Fori(*FRONT_FIRST) as u:
                front_round(u)
            act.wait_ge(x_loaded[1], 32)
            act.wait_ge(S["x_norm"], 2)

            def finish_front():
                act.wait_ge(S["z_summed"], 1 + PAIRS + 1)
                nc.scalar.activation(kv_a, ps_z[:, :, 0:P], ACT.Copy).then_inc(S["z_copied"], 1)
                nc.scalar.activation(z_sum, ps_z[:, :, P], ACT.Copy).then_inc(S["z_copied"], 1)
                nc.scalar.activation(gate, ps_logit, ACT.Sigmoid, bias=gnn_b2[:, 0:1]).then_inc(S["gate_ready"], 1)
                act.wait_ge(S["z_row_ps"], HALVES)
                nc.scalar.activation(z_row, ps_z_row, ACT.Copy).then_inc(S["z_row_ready"], 1)

            def gated(t):
                s = t % Y_SLOTS
                act.wait_ge(S["y_params"], 2)
                if t >= Y_SLOTS:
                    act.wait_ge(y_stored[s], 16 * (t // Y_SLOTS))
                nc.scalar.activation(y_out[:, s, 0:DIM], base[:, t, :], ACT.Identity, bias=y_bias[:, t:t + 1], scale=y_scale[:, t:t + 1])
                nc.scalar.activation(y_out[:, s, DIM:ROW], gate[:, t:t + 1], ACT.Copy).then_inc(S["y_ready"], 1)

            def keep_mixed(batch):
                at, to = batch * MIX_TILES, min(batch * MIX_TILES + MIX_TILES, BLOCKS)
                act.wait_ge(S["mix_ps"], batch + 1)
                act.wait_ge(S["y_ready"], to)
                nc.scalar.activation(base[:, at:to, :], ps_mix[batch % 2][:, 0:to - at, :], ACT.Copy).then_inc(S["mix_done"], 1)

            def copy_upper(level, bit):
                into = keys[exchanges_before(level, bit) % 2]
                for half in range(2):
                    act.wait_ge(half_turned[half], turns_before(level, bit))
                    if bit == LEVELS - 1 and half == 0:
                        act.nop().then_inc(upper_copied[0], 1)
                    else:
                        nc.scalar.activation(sides(into, bit, half)[1], sides(turned, bit, half)[1], ACT.Copy).then_inc(upper_copied[half], 1)

            for level in range(TURNED + 1, LEVELS + 1):
                for bit in (level - 1, TURNED - 1):
                    copy_upper(level, bit)
                    if (level, bit) in FRONT_AT:
                        with nc.scalar.Fori(*FRONT_AT[level, bit]) as u:
                            front_round(u)
                    if (level, bit) in FRONT_END:
                        front_round(PAIRS - 2 + FRONT_END.index((level, bit)))
                    if (level, bit) == FRONT_END[-1]:
                        finish_front()
                    for t in range(*GATED_AT.get((level, bit), (0, 0))):
                        gated(t)
                    for batch in range(*MIX_KEPT_AT.get((level, bit), (0, 0))):
                        keep_mixed(batch)

            def keep_rel(part):
                at, to = TABLE_PARTS[part]
                act.wait_ge(S["fields_ready"], 2 * part + 2)
                nc.scalar.activation(step_rel[:, at:to], step_rel[:, at:to].bitcast(I32), ACT.Copy).then_inc(S["rel_ready"], 1)

            def stage(i, t, g):
                at = slice(g * GROUP, (g + 1) * GROUP)
                act.wait_ge(S["sum_ps"], STEPS_PER_BLOCK * i + GROUP * (g + 1))
                nc.scalar.activation(step_idx[:, at], step_dst[:, bass.ds(STEPS_PER_BLOCK * t + GROUP * g, GROUP)],
                                     ACT.Copy).then_inc(S["idx_staged"], 1)

            def relu(m, slot, ps_done, ps, sb_t, bias, ready):
                act.wait_ge(ps_done, m + 1)
                for h in range(HALVES):
                    nc.scalar.activation(sb_t[:, slot % 2, h, :], ps[:, h, :], ACT.Relu, bias=bias[:, slot, h:h + 1]).then_inc(ready, 1)

            def act_round(i, t, n, steps, experts, lead, mixing=False):
                places = BESIDE if steps else ALONE
                for j in range(STEPS_PER_BLOCK):
                    if mixing and j - 2 in MIX_AFTER:
                        keep_mixed(MIX_AFTER[j - 2])
                    if steps and j == 2:
                        stage(i, t, 1)
                    if steps and j == GROUP + 2:
                        stage(i + 1, t + 1, 0)
                    if experts and j == places["gates"]:
                        act.wait_ge(S["gatesT_ps"], n + 1)
                        nc.scalar.activation(gates_T, ps_gates_T, ACT.Copy).then_inc(S["gatesT_ready"], 1)
                    if experts and j in places["first"]:
                        e = places["first"].index(j)
                        relu(EXPERTS * n + e, e, S["h1_ps"], ps_h1, h1_T, b1, S["h1_ready"])
                    if experts and j in places["second"]:
                        e = places["second"].index(j)
                        relu(EXPERTS * n + e, e, S["h2_ps"], ps_h2, h2_T, b2, S["h2_ready"])
                    if lead and j == places["root"]:
                        act.wait_ge(S["x2_var"], n + 2)
                        nc.scalar.activation(rstd[:, 1:2], mean_var[:, 1:2], ACT.Sqrt, bias=ln_eps[:, 0:1]).then_inc(S["x2_std"], 1)
                    if lead and j == places["turn"]:
                        act.wait_ge(S["x2T_ps"], n + 2)
                        nc.scalar.activation(next_T, ps_x2T, ACT.Copy).then_inc(S["x2T_ready"], 1)
                    if lead and j == places["router"]:
                        act.wait_ge(S["router_ps"], n + 2)
                        nc.scalar.activation(router_hid, ps_router, ACT.Relu, bias=router_b1[:, 0:1]).then_inc(S["router_ready"], 1)
                    if lead and j == places["peak"]:
                        act.wait_ge(S["logit_max_ready"], n + 2)
                        nc.scalar.activation(exp_l[:, :], ps_l, ACT.Exp, bias=logit_max[:, 0:1],
                                             accum_out=exp_sum[:, 0:1]).then_inc(S["exp_ready"], 1)
                    if lead and j == places["move"]:
                        act.wait_ge(S["x2T_ready"], n + 2)
                        nc.scalar.activation(this_T, next_T, ACT.Copy).then_inc(S["this_ready"], 1)
                    if lead and j == places["top"]:
                        act.wait_ge(S["top_diff_ready"], n + 2)
                        nc.scalar.activation(top_w[:, 1:2], top_w[:, 0:1], ACT.Exp).then_inc(S["top_exp_ready"], 1)

            keep_rel(0)
            stage(0, 0, 0)
            act.wait_ge(S["places_ps"], 1)
            act.wait_ge(S["chunk_step"], 16)
            nc.scalar.activation(step_acc, front[0:1, 0:COLS], ACT.Copy).then_inc(S["places_ready"], 1)
            keep_rel(1)
            keep_rel(2)
            act_round(0, 0, -2, True, False, False, mixing=True)
            act_round(1, 1, -1, True, False, True)
            with nc.scalar.Fori(2, BLOCKS) as i:
                act_round(i, i, i - 2, True, True, True)
            act_round(None, None, BLOCKS - 2, False, True, True)
            act_round(None, None, BLOCKS - 1, False, True, False)
            act.wait_ge(S["flag_ready"], 1)
            with nc.scalar.If(act.value_load(cut_flag[:, :], min_val=0, max_val=1)):
                for n, t in enumerate((dst_of_edge, src_of_edge)):
                    act.wait_ge(S["cut_fields_ready"], n + 1)
                    nc.scalar.activation(t, t.bitcast(I32), ACT.Copy).then_inc(S["edges_ready"], 1)
                act.wait_ge(S["steps_ps"], 2)
                act.wait_ge(S["chunk_ready"], 1)
                nc.scalar.activation(step_acc[:, 0:CUT_STEPS], front[0:1, 0:CUT_STEPS], ACT.Copy).then_inc(S["acc_row_ready"], 1)
                act.wait_ge(S["picked_ps"], 1)
                nc.scalar.activation(step_rel[:, 0:CUT_STEPS], front[:, 0:CUT_STEPS], ACT.Copy).then_inc(S["cut_ready"], 1)
                act.wait_ge(S["cut_ready"], 2)
                stage(BLOCKS, 0, 0)
                with nc.scalar.Fori(0, CUT_ROUNDS) as i:
                    act_round(i + BLOCKS, i, None, True, False, False)
                act_round(None, None, BLOCKS - 1, False, False, True)
                with nc.scalar.Fori(0, FULL) as b:
                    act_round(None, None, b + BLOCKS, False, True, True)
                act_round(None, None, 2 * BLOCKS - 1, False, True, False)

        @block.tensor
        def _(pe):
            pe.nop().then_inc(S["z_summed"], 1)
            pe.nop().then_inc(S["sum_ps"], STEPS_PER_BLOCK)
            pe.wait_ge(S["consts"], N_CONSTS)
            pe.wait_ge(S["small_loaded"], 16 * N_SMALL)
            pe.wait_ge(S["z_zeroed"], 1)

            def turn_rows(u, tiles):
                pe.wait_ge(S["xs_ready"], 2 * u + tiles)
                pe.wait_ge(S["xT_ready"], u)
                for s in range(tiles):
                    for h in range(HALVES):
                        last = nc.tensor.transpose(ps_xT[:, h, s * P:(s + 1) * P], xs[:, s, h * P:(h + 1) * P], ident[:, :])
                last.then_inc(S["xT_ps"], 1)

            def sum_z(u, tiles):
                pe.wait_ge(S["zed_ready"], 1 + u + 1)
                for s in range(tiles):
                    for h in range(HALVES):
                        part = zed[:, HALVES * s + h, :]
                        last = nc.tensor.matmul(ps_z[:, h, :], part[:, 0:P], part, start=False, stop=False, skip_group_check=True)
                last.then_inc(S["z_summed"], 1)

            def front_round(u):
                tiles, next_tiles = (2 if not isinstance(u, int) or u + k < PAIRS else 1 for k in range(2))
                width = tiles * P
                if not isinstance(u, int) or u + 1 <= PAIRS:
                    turn_rows(u + 1, next_tiles)
                pe.wait_ge(S["xT_ready"], u + 1)
                pe.wait_ge(S["dev_ready"], u)
                for h in range(HALVES):
                    last = nc.tensor.matmul(ps_devT[:, h, 0:width], centre[:, :], xsT[:, h, 0:width], start=True, stop=True)
                last.then_inc(S["devT_ps"], 1)
                pe.wait_ge(S["var_ready"], u)
                for h in range(HALVES):
                    last = nc.tensor.matmul(ps_hid[:, 0:width], gnn_w1[:, h, :], xsT[:, h, 0:width], start=(h == 0), stop=(h == 1))
                last.then_inc(S["hid_ps"], 1)
                pe.wait_ge(S["square_ready"], u + 1)
                for s in range(tiles):
                    for h in range(HALVES):
                        last = nc.tensor.matmul(ps_dev[:, s, h * P:(h + 1) * P], xsT[:, h, s * P:(s + 1) * P], centre[:, :],
                                                start=True, stop=True)
                last.then_inc(S["dev_ps"], 1)
                pe.wait_ge(S["hid_ready"], u + 1)
                heads = P // HEAD_DIM
                for s in range(tiles):
                    nc.tensor.matmul(ps_logit[:, bass.ds(2 * u + s, 1)], hid[:, s * P:(s + 1) * P], gnn_w2[:, :], start=True, stop=True)
                    for h in range(HALVES):
                        at = s * HEADS + h * heads
                        last = nc.tensor.matmul(ps_var[:, at:at + heads], sqT[:, h, s * P:(s + 1) * P], head_mean[:, :], start=True,
                                                stop=True)
                last.then_inc(S["var_ps"], 1)
                if not isinstance(u, int) or u:
                    sum_z(u - 1, 2)

            turn_rows(0, 2)
            front_round(0)
            with nc.tensor.Fori(*FRONT_FIRST) as u:
                front_round(u)

            def finish_front():
                sum_z(PAIRS, 1)
                pe.wait_ge(S["diag_ready"], HALVES)
                for h in range(HALVES):
                    nc.tensor.matmul(ps_z_row[:, h, :], ones[:, :], diag_sum[:, h, :], start=True, stop=True).then_inc(S["z_row_ps"], 1)

            def mix(batch):
                if batch == 0:
                    pe.wait_ge(S["kv_final"], 1)
                if batch >= 2:
                    pe.wait_ge(S["mix_done"], batch - 1)
                for t in range(batch * MIX_TILES, min(batch * MIX_TILES + MIX_TILES, BLOCKS)):
                    sums = ps_mix[batch % 2][:, t % MIX_TILES, :]
                    nc.tensor.matmul(sums, ident[:, :], base[:, t, :], start=True, stop=False)
                    for h in range(HALVES):
                        last = nc.tensor.matmul(sums[:, h * P:(h + 1) * P], xnT[:, h, t * P:(t + 1) * P], kv[:, h, :],
                                                start=False, stop=(h == 1))
                last.then_inc(S["mix_ps"], 1)

            def turn(level, bit):
                held = keys[exchanges_before(level, bit) % 2]
                for half in range(2):
                    pe.wait_ge(sorted_half[half], instructions_before(level, bit, half))
                    for at in range(half * HALF, COLS if half else HALF, P):
                        last = nc.tensor.transpose(turned[:, at:at + P], held[:, at:at + P], ident[:, :])
                    last.then_inc(half_turned[half], 1)

            for level in range(TURNED + 1, LEVELS + 1):
                for bit in (level - 1, TURNED - 1):
                    turn(level, bit)
                    if (level, bit) in FRONT_AT:
                        with nc.tensor.Fori(*FRONT_AT[level, bit]) as u:
                            front_round(u)
                    if (level, bit) in FRONT_END:
                        front_round(PAIRS - 2 + FRONT_END.index((level, bit)))
                    if (level, bit) == FRONT_END[-1]:
                        finish_front()
                    for batch in range(*MIX_AT.get((level, bit), (0, 0))):
                        mix(batch)

            for half in range(2):
                pe.wait_ge(sorted_half[half], instructions_before(LEVELS, -1, half))
                for at in range(half * HALF, COLS if half else HALF, P):
                    last = nc.tensor.transpose(turned[:, at:at + P], ordered[:, at:at + P], ident[:, :])
                last.then_inc(S["sorted_turned"], 1)
            pe.wait_ge(S["mix_done"], MIX_FIRST)
            pe.wait_ge(S["place_ready"], 1)
            for c in range(TILES):
                last = nc.tensor.matmul(front[0:1, c * P:c * P + P], place[:, c:c + 1], ident[:, :], start=True, stop=True)
            last.then_inc(S["places_ps"], 1)
            pe.wait_ge(S["fields_ready"], 2 * len(TABLE_PARTS))
            pe.wait_ge(S["marks_ready"], 2)
            nc.tensor.matmul(ps_row_sums, ones[:, :], row_sums, start=True, stop=True).then_inc(S["marks_ps"], 1)

            def step(i, j, marked_before, steps):
                if j >= steps:
                    pe.wait_ge(S["sum_ps"], STEPS_PER_BLOCK * (i + 1) + j)
                    pe.nop().then_inc(S["sum_ps"], 1)
                    return
                slot, group = j % GROUP, j // GROUP
                for start, end in RUNS:
                    if slot == start:
                        pe.wait_ge(S["onehot_ready"], STEPS_PER_BLOCK * i + group * GROUP + end + marked_before)
                pe.wait_ge(S["sum_added"], STEPS_PER_BLOCK * i + j + 1)
                missing = sum(k % GROUP == slot for k in range(LAST_STEPS, STEPS_PER_BLOCK)) if marked_before else 0
                pe.wait_ge(rows_in[slot], 16 * (GROUPS_PER_BLOCK * i + group + 1 - missing))
                nc.tensor.matmul(ps_sum[j % SUM_BANKS], onehot[:, j, :], gathered[:, slot, :], start=True,
                                 stop=True).then_inc(S["sum_ps"], 1)

            def first_layer(n, e):
                m = EXPERTS * n + e
                pe.wait_ge(S["h1_ready"], HALVES * m + HALVES)
                if e == 0:
                    pe.wait_ge(S["this_ready"], n + 1)
                for o in range(HALVES):
                    for h in range(HALVES):
                        last = nc.tensor.matmul(ps_h1[:, o, :], w1[:, e, h, o * P:(o + 1) * P], this_T[:, h, :],
                                                start=(h == 0), stop=(h == 1))
                last.then_inc(S["h1_ps"], 1)

            def second_layer(m, e):
                pe.wait_ge(S["h2_ready"], HALVES * m + HALVES)
                pe.wait_ge(S["h1_ready"], HALVES * m + 2 * HALVES)
                for o in range(HALVES):
                    for h in range(HALVES):
                        last = nc.tensor.matmul(ps_h2[:, o, :], w2[:, e, h, o * P:(o + 1) * P], h1_T[:, e % 2, h, :],
                                                start=(h == 0), stop=(h == 1))
                last.then_inc(S["h2_ps"], 1)

            def third_layer(m, e):
                pe.wait_ge(S["ey_added"], m + 1)
                pe.wait_ge(S["h2_ready"], HALVES * m + 2 * HALVES)
                for h in range(HALVES):
                    last = nc.tensor.matmul(ps_y, h2_T[:, e % 2, h, :], w3[:, e, h, :], start=(h == 0), stop=(h == 1))
                last.then_inc(S["ey_ps"], 1)

            def pe_round(i, n, steps, experts, lead, mixing=False, marked_before=0, here=STEPS_PER_BLOCK):
                places = BESIDE if steps else ALONE
                for j in range(STEPS_PER_BLOCK):
                    if steps:
                        step(i, j, marked_before, here)
                    if mixing and j in MIX_AFTER:
                        mix(MIX_AFTER[j])
                    if experts and j == places["gates"]:
                        pe.wait_ge(S["gates_ready"], n + 1)
                        nc.tensor.transpose(ps_gates_T, gates[:, :], ident[:, :]).then_inc(S["gatesT_ps"], 1)
                    if experts and j == places["bias"]:
                        pe.wait_ge(S["gatesT_ready"], n + 1)
                        nc.tensor.matmul(ps_b3, gates_T, b3[:, :], start=True, stop=True).then_inc(S["b3_ps"], 1)
                    if experts and j in places["first"]:
                        first_layer(n, places["first"].index(j))
                    if experts and j in places["second"]:
                        second_layer(EXPERTS * n + places["second"].index(j), places["second"].index(j))
                    if experts and j in places["third"]:
                        third_layer(EXPERTS * n + places["third"].index(j), places["third"].index(j))
                    if lead and j == places["turn"]:
                        pe.wait_ge(S["x2_norm"], n + 2)
                        pe.wait_ge(S["y_begun"], n + 1)
                        for h in range(HALVES):
                            last = nc.tensor.transpose(ps_x2T[:, h, :], xn2[:, h * P:(h + 1) * P], ident[:, :])
                        last.then_inc(S["x2T_ps"], 1)
                    if lead and j == places["router"]:
                        pe.wait_ge(S["x2T_ready"], n + 2)
                        for h in range(HALVES):
                            last = nc.tensor.matmul(ps_router, router_w1[:, h, :], next_T[:, h, :], start=(h == 0), stop=(h == 1))
                        last.then_inc(S["router_ps"], 1)
                    if lead and j == places["logits"]:
                        pe.wait_ge(S["router_ready"], n + 2)
                        nc.tensor.matmul(ps_l, router_hid, router_w2[:, :], start=True, stop=False)
                        nc.tensor.matmul(ps_l, ones[0:1, :], router_b2[:, :], start=False, stop=True).then_inc(S["logits_ps"], 1)

            pe.wait_ge(S["places_ready"], 1)
            pe.wait_ge(S["flag_step"], 7)
            pe_round(0, -2, True, False, False, mixing=True)
            pe.wait_ge(S["mix_done"], MIX_BATCHES)
            pe_round(1, -1, True, False, True)
            pe.wait_ge(S["weights_loaded"], 16 * 3 * EXPERTS)
            with nc.tensor.Fori(2, FULL) as i:
                pe_round(i, i - 2, True, True, True)
            pe_round(FULL, FULL - 2, True, True, True, here=LAST_STEPS)
            pe_round(None, BLOCKS - 2, False, True, True)
            pe_round(None, BLOCKS - 1, False, True, False)
            pe.wait_ge(S["flag_ready"], 1)
            with nc.tensor.If(pe.value_load(cut_flag[:, :], min_val=0, max_val=1)):
                pe.wait_ge(S["sum_added"], SUM_BANKS + STEPS)
                pe.wait_ge(S["ey_added"], 1 + EXPERTS * BLOCKS)
                pe.wait_ge(S["below_ready"], 4)
                for n, (which, at) in enumerate(((0, 0), (0, 1), (1, 1))):
                    last = nc.tensor.matmul(ps_counts[:, n:n + 1], below[:, which, at:at + BLOCKS], ones[:, 0:1], start=True, stop=True)
                last.then_inc(S["counts_ps"], 1)
                pe.wait_ge(S["counts_ready"], 2)
                nc.tensor.matmul(ps_end, upto[:, :], counts[:, 4:5], start=True, stop=True).then_inc(S["ends_ps"], 1)
                pe.wait_ge(S["past_ready"], 2)
                pe.wait_ge(S["cut_consts"], 3)
                for ps, w in ((turned, chunk_w), (front, acc_w)):
                    for at in range(0, CUT_STEPS, BANK):
                        to = min(at + BANK, CUT_STEPS)
                        last = nc.tensor.matmul(ps[:, at:to], w, past_block[:, at:to], start=True, stop=True)
                    last.then_inc(S["steps_ps"], 1)
                pe.wait_ge(S["edges_ready"], 2)
                pe.wait_ge(S["chunk_ready"], 1)
                pe.wait_ge(S["acc_row_ready"], 1)
                picks = 0
                for tile in range(TILES):
                    at, to = tile * P, min(tile * P + P, CUT_STEPS)
                    sources = [c for c in (tile - 1, tile) if c >= 0]
                    for c in sources:
                        chosen = pick[:, picks % PICKS, 0:to - at]
                        picks += 1
                        pe.wait_ge(S["pick_ready"], picks)
                        nc.tensor.matmul(turned[:, at:to], dst_of_edge[:, c * P:c * P + P], chosen, start=(c == sources[0]), stop=(c == tile))
                        nc.tensor.matmul(front[:, at:to], src_of_edge[:, c * P:c * P + P], chosen, start=(c == sources[0]),
                                         stop=False).then_inc(S["pick_used"], 1)
                    last = nc.tensor.matmul(front[:, at:to], neg_block, past_block[:, at:to], start=False, stop=True)
                last.then_inc(S["picked_ps"], 1)
                with nc.tensor.Fori(0, CUT_ROUNDS) as i:
                    pe_round(i + BLOCKS, None, True, False, False, marked_before=GROUP)
                pe_round(None, BLOCKS - 1, False, False, True)
                with nc.tensor.Fori(0, FULL) as b:
                    pe_round(None, b + BLOCKS, False, True, True)
                pe_round(None, 2 * BLOCKS - 1, False, True, False)

        @block.vector
        def _(dve):
            dve.nop().then_inc(S["sum_added"], SUM_BANKS)
            dve.nop().then_inc(S["ey_added"], 1)
            dve.nop().then_inc(S["row_stored"], 1)
            nc.vector.memset(bank(3), 0.0).then_inc(S["z_zeroed"], 1)
            nc.vector.memset(keys[1], PAD_KEY).then_inc(S["key_step"], 1)
            dve.wait_ge(S["consts"], 2)
            nc.vector.tensor_scalar(row_odd[:, :], row_no[:, :], 1, None, ALU.bitwise_and).then_inc(S["key_step"], 1)
            nc.vector.tensor_scalar(bound[:, :], bound[:, :], BLOCK_SHIFT, KEY_BASE, ALU.logical_shift_left,
                                    ALU.bitwise_or).then_inc(S["key_step"], 1)
            dve.wait_ge(S["key_step"], 3)
            nc.vector.tensor_scalar(sign[:, 0:1], row_odd[:, :], -2.0, 1.0, ALU.mult, ALU.add).then_inc(S["key_step"], 1)
            nc.vector.tensor_scalar(sign[:, 1:2], row_odd[:, :], 2.0, -1.0, ALU.mult, ALU.add).then_inc(S["key_step"], 1)
            dve.wait_ge(S["edges_loaded"], 32)
            nc.vector.tensor_scalar(src_in[0:LOAD_ROWS, :], src_in[0:LOAD_ROWS, :], DST_BITS, KEY_BASE, ALU.logical_shift_left,
                                    ALU.bitwise_or).then_inc(S["key_step"], 1)
            dve.wait_ge(S["key_step"], 6)
            nc.vector.tensor_tensor(keys[1][0:LOAD_ROWS, 0:LOAD_COLS].bitcast(I32), src_in[0:LOAD_ROWS, :], dst_in[0:LOAD_ROWS, :],
                                    ALU.bitwise_or).then_inc(S["key_step"], 1)
            dve.wait_ge(S["key_step"], 7)
            flat, signed = (t.rearrange("p (g t) -> p g t", t=2) for t in (keys[1], keys[0]))
            for t in range(2):
                nc.vector.tensor_scalar(signed[:, :, t], flat[:, :, t], sign[:, t:t + 1], None, ALU.mult).then_inc(S["key_step"], 1)

            def statistics(part):
                at, to = X_PARTS[part]
                dve.wait_ge(x_loaded[part], 16 * (part + 1))
                dve.wait_ge(S["x_zeroed"], 1)
                per = 7
                with nc.vector.Fori(at // per, to // per) as t:
                    for k in range(per):
                        nc.vector.bn_stats(x_stats[:, per * t + k, :], base[:, per * t + k, :]).then_inc(S["x_stat"], 1)
                dve.wait_ge(S["x_stat"], to)
                for t in range(at, to):
                    nc.vector.bn_aggr(x_mean_var[:, t, :], x_stats[:, t, :]).then_inc(S["x_stats_ready"], 1)

            def exchange(level, bit, half):
                done = exchanges_before(level, bit)
                held, into = keys[done % 2], keys[(done + 1) % 2]
                both = bit == LEVELS - 1
                for other in range(2):
                    if other == half or both or (level == LEVELS and bit == LEVELS - 2):
                        dve.wait_ge(sorted_half[other], instructions_before(level, bit, other))
                if is_after_turn(level, bit):
                    for other in (range(2) if both else (half,)):
                        dve.wait_ge(half_turned[other], turns_before(level, bit))
                        dve.wait_ge(upper_copied[other], turns_before(level, bit))
                lower_from = turned if is_after_turn(level, bit) else held
                lower, upper = sides(lower_from, bit, half)[0], sides(held, bit, half)[1]
                outs = sides(into, bit, half)
                ops = (ALU.min, ALU.max)
                first = bit == level - 1
                negated = {LEVELS - 2: (1, 0), LEVELS - 1: (half,), LEVELS: (1,), TURNED: (0,)}.get(level, (0, 1))
                if not first:
                    for t in range(2):
                        nc.vector.tensor_tensor(outs[t], lower, upper, ops[t]).then_inc(sorted_half[half], 1)
                else:
                    runs = lower.shape[1]
                    for r in range(min(runs, len(negated))):
                        pick_runs = slice(r, runs, len(negated))
                        pair = (lower[:, pick_runs, :], upper[:, pick_runs, :])
                        n = negated[r]
                        for t in range(2):
                            nc.vector.scalar_tensor_tensor(outs[t][:, pick_runs, :], pair[1 - n], -1.0, pair[n], ALU.mult,
                                                           ops[t]).then_inc(sorted_half[t if both else half], 1)
                if has_lone(bit, half):
                    if first and level >= LEVELS - 1:
                        nc.vector.tensor_scalar(lone(into, bit), lone(lower_from, bit), -1.0, None, ALU.mult).then_inc(sorted_half[half], 1)
                    else:
                        nc.vector.tensor_copy(lone(into, bit), lone(lower_from, bit)).then_inc(sorted_half[half], 1)

            dve.wait_ge(S["key_step"], 9)
            passes = [(level, bit) for level in range(1, LEVELS + 1) for bit in range(level - 1, -1, -1)]
            turns = [n for n, p in enumerate(passes) if is_after_turn(*p)]
            for start, end in zip([0, *turns], [*turns, len(passes)]):
                for n in range(start, end + LAG):
                    if n < end:
                        exchange(*passes[n], 0)
                    if n - LAG >= start and passes[n - LAG][1] != LEVELS - 1:
                        exchange(*passes[n - LAG], 1)
                        if passes[n - LAG] in STATS_AFTER:
                            statistics(STATS_AFTER.index(passes[n - LAG]))
            def fields(part):
                at, to = TABLE_PARTS[part]
                dve.wait_ge(S["sorted_turned"], 1 if to <= HALF else 2)
                bits = turned[:, at:to].bitcast(I32)
                nc.vector.tensor_scalar(step_dst[:, at:to].bitcast(I32), bits, DST_MASK, None, ALU.bitwise_and).then_inc(S["fields_ready"], 1)
                nc.vector.tensor_scalar(step_rel[:, at:to].bitcast(I32), bits, DST_BITS, P - 1, ALU.logical_shift_right,
                                        ALU.bitwise_and).then_inc(S["fields_ready"], 1)

            fields(0)
            for half in range(2):
                dve.wait_ge(sorted_half[half], instructions_before(LEVELS, -1, half))
            ends = ordered.bitcast(I32).rearrange("p (c n) -> p n c", n=P)
            for k, lane_of in enumerate((0, P - 1)):
                nc.vector.tensor_scalar(chunk_int[:, k, :], ends[:, lane_of, :], DST_BITS, DST_MASK, ALU.logical_shift_right,
                                        ALU.bitwise_and).then_inc(S["chunk_step"], 1)
            dve.wait_ge(S["chunk_step"], 2)
            nc.vector.tensor_scalar(chunk_int[:, 2:4, :], chunk_int[:, 0:2, :], BLOCK_SHIFT - DST_BITS, None,
                                    ALU.logical_shift_right).then_inc(S["chunk_step"], 1)
            nc.vector.tensor_scalar(chunk_int[:, 5, :], chunk_int[:, 0, :], P - 1, None, ALU.bitwise_and).then_inc(S["chunk_step"], 1)
            dve.wait_ge(S["chunk_step"], 4)
            nc.vector.tensor_scalar(chunk_int[:, 4, :], chunk_int[:, 2, :], SHARED - 1, None, ALU.bitwise_and).then_inc(S["chunk_step"], 1)
            dve.wait_ge(S["chunk_step"], 5)
            nc.vector.tensor_copy(chunk_val, chunk_int).then_inc(S["chunk_step"], 1)
            dve.wait_ge(S["chunk_step"], 6)
            first_node, last_node, first_block, last_block_of, shared_no, first_lane = (chunk_val[:, k, :] for k in range(N_FIELDS))
            nc.vector.tensor_tensor(straddles, last_block_of, first_block, ALU.is_gt).then_inc(S["chunk_step"], 1)
            nc.vector.scalar_tensor_tensor(to_shared, shared_no, float(SHARED_AT), first_block, ALU.add, ALU.subtract).then_inc(S["chunk_step"], 1)
            nc.vector.tensor_tensor(span, last_node, first_node, ALU.subtract).then_inc(S["chunk_step"], 1)
            dve.wait_ge(S["chunk_step"], 9)
            nc.vector.tensor_tensor(shift, to_shared, straddles, ALU.mult).then_inc(S["chunk_step"], 1)
            nc.vector.tensor_tensor(low, first_lane, straddles, ALU.mult).then_inc(S["chunk_step"], 1)
            dve.wait_ge(S["chunk_step"], 11)
            nc.vector.tensor_tensor(to_shared, shift, first_block, ALU.add).then_inc(S["chunk_step"], 1)
            dve.wait_ge(S["chunk_step"], 12)
            nc.vector.tensor_scalar(place, to_shared, float(ROW), None, ALU.mult).then_inc(S["place_ready"], 1)
            by_block = lane[:, 0:BLOCKS].unsqueeze(1).broadcast_to([P, TILES, BLOCKS])
            of_chunk = first_block.unsqueeze(2).broadcast_to([P, TILES, BLOCKS])
            nc.vector.tensor_tensor(share_low, by_block, of_chunk, ALU.is_equal).then_inc(S["chunk_step"], 1)
            nc.vector.tensor_tensor(begun[:, :, 0:BLOCKS], by_block, of_chunk, ALU.is_ge).then_inc(S["chunk_step"], 1)
            nc.vector.tensor_scalar(begun[:, :, BLOCKS], span, float(P), None, ALU.is_ge).then_inc(S["chunk_step"], 1)
            dve.wait_ge(S["chunk_step"], 13)
            nc.vector.tensor_tensor(share_low, share_low, low.unsqueeze(2).broadcast_to([P, TILES, BLOCKS]),
                                    ALU.mult).then_inc(S["chunk_step"], 1)
            dve.wait_ge(S["chunk_step"], 15)
            nc.vector.tensor_reduce(row_sums[:, BLOCKS:2 * BLOCKS + 1], begun.rearrange("p c b -> p b c"), AX.X, ALU.add).then_inc(S["marks_ready"], 1)
            dve.wait_ge(S["chunk_step"], 16)
            nc.vector.tensor_reduce(row_sums[:, 0:BLOCKS], share_low.rearrange("p c b -> p b c"), AX.X, ALU.add).then_inc(S["marks_ready"], 1)
            fields(1)
            fields(2)

            def check_chunks():
                dve.wait_ge(S["marks_ps"], 1)
                nc.vector.tensor_scalar(is_earlier[:, :], ps_share_low, edge_no[:, 0:1], None, ALU.is_le).then_inc(S["flag_step"], 1)
                for n, after_step in enumerate((STEPS_PER_BLOCK + BESIDE["norm"] + 2, BESIDE["norm"] + 3)):
                    nc.vector.tensor_scalar(unfit[:, n * BLOCKS:(n + 1) * BLOCKS], lane[0:1, 0:BLOCKS], float(STEPS_PER_BLOCK),
                                            float(after_step), ALU.mult, ALU.add).then_inc(S["flag_step"], 1)
                dve.wait_ge(S["flag_step"], 3)
                nc.vector.tensor_scalar(is_later[:, 1:BLOCKS + 1], is_earlier[:, :], -1.0, 1.0, ALU.mult, ALU.add).then_inc(S["flag_step"], 1)
                for n, beyond in enumerate((ALU.is_gt, ALU.is_lt)):
                    limit = unfit[:, n * BLOCKS:(n + 1) * BLOCKS]
                    nc.vector.tensor_tensor(limit, ps_begun[0:1, 0:BLOCKS], limit, beyond).then_inc(S["flag_step"], 1)
                nc.vector.tensor_copy(unfit[:, 2 * BLOCKS:2 * BLOCKS + 1], ps_begun[0:1, BLOCKS:BLOCKS + 1]).then_inc(S["flag_step"], 1)
                dve.wait_ge(S["flag_step"], 7)
                nc.vector.tensor_reduce(unfit[:, 2 * BLOCKS + 1:2 * BLOCKS + 2], unfit[:, 0:2 * BLOCKS + 1], AX.X, ALU.max).then_inc(S["flag_step"], 1)
                dve.wait_ge(S["flag_step"], 8)
                nc.vector.tensor_scalar(cut_flag[:, :], unfit[:, 2 * BLOCKS + 1:2 * BLOCKS + 2], 1.0, None, ALU.min).then_inc(S["flag_ready"], 1)
                dve.wait_ge(S["flag_ready"], 1)

            def mark(first, step, at, count):
                dve.wait_ge(S["sum_ps"], first + count)
                nc.vector.tensor_tensor(onehot[:, at:at + count, :], lane[:, :].unsqueeze(1).broadcast_to([P, count, P]),
                                        step_rel[:, bass.ds(step, count)].unsqueeze(2).broadcast_to([P, count, P]),
                                        ALU.is_equal).then_inc(S["onehot_ready"], count)

            place_regs = [dve.alloc_register(f"place{slot}") for slot in range(PLACES)]

            def load_places(t, j):
                dve.load(place_regs, step_acc[0:1, bass.ds(STEPS_PER_BLOCK * t + j, PLACES)])

            def add_sums(i, j, steps):
                if j >= steps:
                    dve.wait_ge(S["sum_added"], STEPS_PER_BLOCK * i + j + SUM_BANKS)
                    dve.nop().then_inc(S["sum_added"], 1)
                    return
                at = STEPS_PER_BLOCK * i + j
                to = dve.snap(place_regs[j % PLACES], min_val=0, max_val=(SHARED_AT + SHARED - 1) * ROW)
                sums = acc_mem[:, bass.ds(to, ROW)]
                dve.wait_ge(S["sum_added"], at + SUM_BANKS)
                dve.wait_ge(S["sum_ps"], at + 1 + STEPS_PER_BLOCK)
                nc.vector.tensor_tensor(sums, sums, ps_sum[j % SUM_BANKS], ALU.add).then_inc(S["sum_added"], 1)

            def shared_sums(b):
                return acc_mem[:, bass.ds(SHARED_AT * ROW + ROW * (b & (SHARED - 1)), ROW)]

            def normalise(n, b, steps, piece):
                links = FFN_LINKS * n + piece + 1
                own = acc_mem[:, bass.ds(ROW * b, ROW)]
                if piece == 0:
                    dve.wait_ge(S["sum_added"], SUM_BANKS + steps)
                    nc.vector.scalar_tensor_tensor(own, shared_sums(b + 1), is_later[:, bass.ds(b, 1)], own, ALU.mult, ALU.add).then_inc(S["ffn_step"], 1)
                    dve.wait_ge(S["ffn_step"], links)
                    dve.nop().then_inc(S["ffn_pass"], 1)
                if piece == 1:
                    dve.wait_ge(S["sum_added"], SUM_BANKS + steps)
                    dve.nop().then_inc(S["ffn_pass"], 1)
                    nc.vector.tensor_copy(shared_sums(b + 1), is_later[:, 0:1].broadcast_to([P, ROW])).then_inc(S["ffn_step"], 1)
                    nc.vector.scalar_tensor_tensor(own, shared_sums(b), is_earlier[:, bass.ds(b, 1)], own, ALU.mult, ALU.add).then_inc(S["ffn_step"], 1)
                    dve.wait_ge(S["ffn_step"], links + 1)
                    dve.nop().then_inc(S["ffn_pass"], 1)
                if piece == 2:
                    dve.wait_ge(S["sum_added"], SUM_BANKS + steps)
                    nc.vector.tensor_scalar(den[:, 0:1], acc_mem[:, bass.ds(ROW * b + DIM, 1)], 1e-12, None, ALU.max).then_inc(S["ffn_step"], 1)
                    dve.wait_ge(S["ffn_step"], links + 1)
                    dve.nop().then_inc(S["ffn_pass"], 1)
                if piece == 3:
                    nc.vector.reciprocal(den[:, 1:2], den[:, 0:1]).then_inc(S["ffn_step"], 1)
                if piece == 4:
                    dve.wait_ge(S["ffn_step"], links)
                    dve.wait_ge(S["sum_added"], SUM_BANKS + steps)
                    nc.vector.scalar_tensor_tensor(x2, acc_mem[:, bass.ds(ROW * b, DIM)], den[:, 1:2], base[:, b, :], ALU.mult,
                                                   ALU.add).then_inc(S["ffn_step"], 1)
                    dve.wait_ge(S["ffn_step"], links + 1)
                    dve.nop().then_inc(S["ffn_pass"], 1)
                if piece == 5:
                    nc.vector.bn_stats(stats[:, :], x2).then_inc(S["ffn_step"], 1)
                if piece == 6:
                    dve.wait_ge(S["ffn_step"], links)
                    dve.nop().then_inc(S["ffn_pass"], 1)
                    nc.vector.bn_aggr(mean_var[:, :], stats[:, :]).then_inc(S["x2_var"], 1)
                if piece == 8:
                    dve.wait_ge(S["x2_std"], n + 1)
                    nc.vector.reciprocal(rstd[:, 0:1], rstd[:, 1:2]).then_inc(S["ffn_step"], 1)
                if piece == 9:
                    dve.wait_ge(S["ffn_step"], FFN_LINKS * n + N_NORM)
                    nc.vector.tensor_scalar(xn2, x2, mean_var[:, 0:1], rstd[:, 0:1], ALU.subtract, ALU.mult).then_inc(S["x2_norm"], 1)

            def route(n, j, places):
                links = FFN_LINKS * n + N_NORM
                if j == places["peak"]:
                    dve.wait_ge(S["logits_ps"], n + 1)
                    nc.vector.tensor_reduce(logit_max[:, :], ps_l, AX.X, ALU.max, negate=True).then_inc(S["logit_max_ready"], 1)
                if j == places["probs"]:
                    dve.wait_ge(S["exp_ready"], n + 1)
                    nc.vector.reciprocal(exp_sum[:, 1:2], exp_sum[:, 0:1]).then_inc(S["ffn_step"], 1)
                    dve.wait_ge(S["ffn_step"], links + 1)
                    nc.vector.tensor_scalar(probs[:, 0:EXPERTS], exp_l[:, :], exp_sum[:, 1:2], None, ALU.mult).then_inc(S["ffn_step"], 1)
                if j == places["top"]:
                    dve.wait_ge(S["ffn_step"], links + 2)
                    dve.nop().then_inc(S["ffn_pass"], 1)
                    nc.vector.max(top[:, :], probs[:, :]).then_inc(S["ffn_step"], 1)
                    dve.wait_ge(S["ffn_step"], links + 3)
                    nc.vector.tensor_tensor(top_w[:, 0:1], top[:, 1:2], top[:, 0:1], ALU.subtract).then_inc(S["top_diff_ready"], 1)
                    nc.vector.max_index(top_i[:, :], top[:, :], probs[:, :]).then_inc(S["ffn_step"], 1)
                if j == places["index"]:
                    dve.wait_ge(S["ffn_step"], links + 4)
                    nc.vector.tensor_copy(top_f[:, :], top_i[:, 0:2]).then_inc(S["ffn_step"], 1)
                if j == places["share"]:
                    dve.wait_ge(S["top_exp_ready"], n + 1)
                    nc.vector.tensor_scalar(top_w[:, 2:3], top_w[:, 1:2], 1.0, None, ALU.add).then_inc(S["ffn_step"], 1)
                    dve.wait_ge(S["ffn_step"], links + 6)
                    nc.vector.reciprocal(top_w[:, 3:4], top_w[:, 2:3]).then_inc(S["ffn_step"], 1)
                if j == places["share"] + 1:
                    dve.wait_ge(S["ffn_step"], links + 7)
                    nc.vector.tensor_tensor(top_w[:, 0:1], top_w[:, 1:2], top_w[:, 3:4], ALU.mult).then_inc(S["ffn_step"], 1)
                if j == places["spread"]:
                    dve.wait_ge(S["ffn_step"], links + 8)
                    nc.vector.tensor_scalar(gate_1[:, :], lane[:, 0:EXPERTS], top_f[:, 0:1], top_w[:, 3:4], ALU.is_equal,
                                            ALU.mult).then_inc(S["ffn_step"], 1)
                    nc.vector.tensor_scalar(gate_2[:, :], lane[:, 0:EXPERTS], top_f[:, 1:2], top_w[:, 0:1], ALU.is_equal,
                                            ALU.mult).then_inc(S["ffn_step"], 1)
                    dve.wait_ge(S["ffn_step"], links + N_ROUTE)
                    nc.vector.tensor_tensor(gates[:, :], gate_1[:, :], gate_2[:, :], ALU.add).then_inc(S["gates_ready"], 1)

            def dve_round(i, t, n, block_at, steps, experts, lead, all_steps=STEPS, here=STEPS_PER_BLOCK):
                places = BESIDE if steps else ALONE
                for j in range(STEPS_PER_BLOCK):
                    if steps:
                        for start, end in RUNS:
                            if j % GROUP == start + 1:
                                ahead = j - 1 + GROUP
                                mark(STEPS_PER_BLOCK * i + ahead, STEPS_PER_BLOCK * t + ahead, ahead % STEPS_PER_BLOCK, end - start)
                        if j % PLACES == 0:
                            load_places(t, j)
                        add_sums(i, j, here)
                    if experts and j == places["begin"]:
                        dve.wait_ge(S["row_stored"], 1 + 16 * n)
                        dve.wait_ge(S["b3_ps"], n + 1)
                        nc.vector.tensor_tensor(y_acc, x2, ps_b3, ALU.add).then_inc(S["y_begun"], 1)
                        dve.wait_ge(S["y_begun"], n + 1)
                    if experts and j in places["add"]:
                        e = places["add"].index(j)
                        m = EXPERTS * n + e
                        dve.wait_ge(S["ey_added"], m + 1)
                        dve.wait_ge(S["ey_ps"], m + 1)
                        nc.vector.scalar_tensor_tensor(y_acc, ps_y, gates[:, e:e + 1], y_acc, ALU.mult, ALU.add).then_inc(S["ey_added"], 1)
                    if lead and places["norm"] <= j < places["norm"] + NORM_PIECES:
                        normalise(n + 1, block_at, STEPS_PER_BLOCK * i + j + 1 if steps else all_steps, j - places["norm"])
                    if lead:
                        route(n + 1, j, places)

            dve.wait_ge(S["rel_ready"], 1)
            dve.wait_ge(S["kept_stored"], 16)
            dve.wait_ge(S["marks_ready"], 2)
            mark(0, 0, 0, GROUP)
            check_chunks()
            dve.wait_ge(S["rel_ready"], len(TABLE_PARTS))
            dve.wait_ge(S["places_ready"], 1)
            dve.wait_ge(S["acc_zeroed"], 1)
            dve_round(0, 0, -2, None, True, False, False)
            dve.wait_ge(S["mix_done"], MIX_BATCHES)
            dve_round(1, 1, -1, 0, True, False, True)
            with nc.vector.Fori(2, FULL) as i:
                dve_round(i, i, i - 2, i - 1, True, True, True)
            dve_round(FULL, FULL, FULL - 2, FULL - 1, True, True, True, here=LAST_STEPS)
            dve_round(None, None, BLOCKS - 2, FULL, False, True, True)
            dve_round(None, None, BLOCKS - 1, None, False, True, False)
            with nc.vector.If(dve.value_load(cut_flag[:, :], min_val=0, max_val=1)):
                dve.wait_ge(S["kept_loaded"], 16)
                dve.wait_ge(S["sum_ps"], STEPS + STEPS_PER_BLOCK)
                bits = ordered[:, 0:COLS].bitcast(I32)
                nc.vector.tensor_scalar(dst_of_edge.bitcast(I32), bits, DST_MASK, None, ALU.bitwise_and).then_inc(S["cut_fields_ready"], 1)
                nc.vector.tensor_scalar(src_of_edge.bitcast(I32), bits, DST_BITS, DST_MASK, ALU.logical_shift_right,
                                        ALU.bitwise_and).then_inc(S["cut_fields_ready"], 1)
                ends = ordered.rearrange("p (c n) -> p c n", n=P)
                limits = bound[:, :].bitcast(F32).unsqueeze(2).broadcast_to([P, BLOCKS + 1, TILES])
                for n, lane_of in enumerate((P - 1, 0)):
                    keys_at = ends[:, :, lane_of].unsqueeze(1).broadcast_to([P, BLOCKS + 1, TILES])
                    if n:
                        dve.wait_ge(S["below_ready"], 2)
                    nc.vector.tensor_tensor(cut, keys_at, limits, ALU.is_lt).then_inc(S["below_ready"], 1)
                    dve.wait_ge(S["below_ready"], 2 * n + 1)
                    nc.vector.tensor_reduce(below[:, n, :], cut, AX.X, ALU.add).then_inc(S["below_ready"], 1)
                dve.wait_ge(S["counts_ps"], 1)
                nc.vector.tensor_copy(counts[:, 0:3], ps_counts[:, 0:3]).then_inc(S["counts_ready"], 1)
                dve.wait_ge(S["counts_ready"], 1)
                nc.vector.tensor_tensor(counts[:, 4:5], counts[:, 2:3], counts[:, 0:1], ALU.subtract).then_inc(S["counts_ready"], 1)
                nc.vector.tensor_tensor(counts[:, 5:6], counts[:, 1:2], counts[:, 2:3], ALU.subtract).then_inc(S["counts_ready"], 1)
                dve.wait_ge(S["counts_ready"], 3)
                nc.vector.scalar_tensor_tensor(counts[:, 6:7], last_block[:, :], 2.0 * COLS, counts[:, 5:6], ALU.mult,
                                               ALU.add).then_inc(S["counts_ready"], 1)
                dve.wait_ge(S["counts_ready"], 4)
                nc.vector.tensor_scalar(chunk_w, ones[0:BLOCKS, :], counts[:, 6:7], None, ALU.mult).then_inc(S["past_ready"], 1)
                dve.wait_ge(S["ends_ps"], 1)
                nc.vector.tensor_copy(counts[:, 7:8], ps_end).then_inc(S["counts_ready"], 1)
                dve.wait_ge(S["counts_ready"], 5)
                dve.wait_ge(S["cut_consts"], 3)
                nc.vector.tensor_scalar(past_block, step_no[0:BLOCKS, :], counts[:, 7:8], None, ALU.is_ge).then_inc(S["past_ready"], 1)
                dve.wait_ge(S["steps_ps"], 1)
                nc.vector.tensor_tensor(chunk_of_step, turned[:, 0:CUT_STEPS], step_no, ALU.add).then_inc(S["chunk_ready"], 1)
                dve.wait_ge(S["chunk_ready"], 1)
                picks = 0
                for tile in range(TILES):
                    at, to = tile * P, min(tile * P + P, CUT_STEPS)
                    for c in [c for c in (tile - 1, tile) if c >= 0]:
                        if picks >= PICKS:
                            dve.wait_ge(S["pick_used"], picks - PICKS + 1)
                        nc.vector.tensor_scalar(pick[:, picks % PICKS, 0:to - at], chunk_of_step[:, at:to], edge_no[:, c:c + 1], None,
                                                ALU.is_equal).then_inc(S["pick_ready"], 1)
                        picks += 1
                dve.wait_ge(S["picked_ps"], 1)
                nc.vector.tensor_copy(step_dst[:, 0:CUT_STEPS], turned[:, 0:CUT_STEPS]).then_inc(S["cut_ready"], 1)
                dve.wait_ge(S["cut_ready"], 2)
                dve.wait_ge(S["acc_row_ready"], 1)
                dve.wait_ge(S["acc_zeroed"], 2)
                mark(STEPS, 0, 0, GROUP)
                with nc.vector.Fori(0, CUT_ROUNDS) as i:
                    dve_round(i + BLOCKS, i, None, None, True, False, False)
                dve_round(None, None, BLOCKS - 1, 0, False, False, True, STEPS + CUT_STEPS)
                with nc.vector.Fori(0, FULL) as b:
                    dve_round(None, None, b + BLOCKS, b + 1, False, True, True, STEPS + CUT_STEPS)
                dve_round(None, None, 2 * BLOCKS - 1, None, False, True, False)


INPUTS = ["x", "src", "dst", "L0_gnn_W1", "L0_gnn_b1", "L0_gnn_W2", "L0_gnn_b2", "L0_mix_kln_weight", "L0_mix_kln_bias",
          "L0_mix_vln_weight", "L0_mix_vln_bias", "L0_ffn_router_w1", "L0_ffn_router_b1", "L0_ffn_router_w2", "L0_ffn_router_b2",
          "L0_ffn_expert_w1", "L0_ffn_expert_b1", "L0_ffn_expert_w2", "L0_ffn_expert_b2", "L0_ffn_expert_w3", "L0_ffn_expert_b3"]


def kernel(**inputs):
    import concourse.bacc as bacc
    from concourse.bass_utils import run_bass_kernel_spmd

    nc = bacc.Bacc("TRN2", target_bir_lowering=False, num_devices=1)
    arrays, aps = {}, {}
    for name in INPUTS:
        arrays[f"in_{name}"] = np.ascontiguousarray(inputs[name])
        shape, dt = arrays[f"in_{name}"].shape, mybir.dt.from_np(arrays[f"in_{name}"].dtype)
        aps[name] = nc.dram_tensor(f"in_{name}", shape, dt, kind="ExternalInput").ap()
    out = nc.dram_tensor("out_rows", (NODES, DIM), F32, kind="ExternalOutput").ap()
    y_table = nc.dram_tensor("gated_rows", (BLOCKS * P, ROW), F32, kind="Internal").ap()
    kept_keys = nc.dram_tensor("kept_keys", (P, COLS), F32, kind="Internal").ap()
    gps_layer(nc, aps, out, y_table, kept_keys)
    result = run_bass_kernel_spmd(nc, [arrays], core_ids=[0])
    return result.results[0]["out_rows"]
```
